# Optimizing a Trainium2 kernel written in Bass

```python
import numpy as np
import jax
import jax.numpy as jnp

def _softmax(x, axis=-1):
    return jax.nn.softmax(x, axis=axis)

def _gelu(x):
    return jax.nn.gelu(x, approximate=True)

def _silu(x):
    return jax.nn.silu(x)

def _sigmoid(x):
    return jax.nn.sigmoid(x)

def _layernorm(x, axis=-1, eps=1e-05):
    m = jnp.mean(x, axis=axis, keepdims=True)
    v = jnp.var(x, axis=axis, keepdims=True)
    return (x - m) / jnp.sqrt(v + eps)

def _scatter_add(tgt, idx, src, axis=0):
    return tgt.at[idx].add(src)

def _segment_sum(src, seg, n):
    return jax.ops.segment_sum(src, seg, n)
kernel_name = 'mk_perceiver_d1_seqx_r4_b5f8c8'

def setup_inputs(seed: int=0):
    np.random.seed(seed)
    _w = jnp.asarray

    def _rec_inputs():
        import jax
        import jax.numpy as jnp
        _rk = jax.random.key(seed)
        x = 7.22e-05 + 1 * jax.random.normal(jax.random.fold_in(_rk, 1), (64, 32, 256), jnp.float32)
        _lenS = 32 - jax.random.randint(jax.random.fold_in(_rk, 7), (64,), 0, max(1, 32 // 4) + 1, jnp.int32)
        _lenS2 = 257 - jax.random.randint(jax.random.fold_in(_rk, 8), (64,), 0, max(1, 257 // 4) + 1, jnp.int32)
        _ctx_768P = jax.random.normal(jax.random.fold_in(_rk, 11), (64, 16, 192), jnp.float32)
        _ctx_768c = jax.random.dirichlet(jax.random.fold_in(_rk, 511), 0.3 * jnp.ones((16,), jnp.float32), (64, 257))
        _ctx_768t = jnp.einsum('bsk,bkd->bsd', _ctx_768c, _ctx_768P)
        _ctx_768t = _ctx_768t * jax.lax.rsqrt(jnp.mean(jnp.square(_ctx_768t)) + 1e-12) * 0.953939
        ctx_768 = -0.000191848 + 0.999787 * (_ctx_768t + 0.3 * jax.random.normal(jax.random.fold_in(_rk, 611), (64, 257, 192), jnp.float32))
        return (x, ctx_768)
    x, ctx_768 = _rec_inputs()

    def _L0_xattn_setup():
        import jax, jax.numpy as jnp
        import numpy as np
        NUM_HEADS = 16
        CLAMP = 10000.0
        key = jax.random.key(seed)
        ks = jax.random.split(key, 8)
        B, Nq, Nkv, Cq, Ckv = (4, 512, 512, 256, 192)
        s_q = 1.0 / np.sqrt(Cq)
        s_kv = 1.0 / np.sqrt(Ckv)
        return {'query': jax.random.normal(ks[0], (B, Nq, Cq), jnp.float32), 'key_value': jax.random.normal(ks[1], (B, Nkv, Ckv), jnp.float32), 'Wq': jax.random.normal(ks[2], (Cq, Cq), jnp.float32) * s_q, 'bq': jnp.zeros((Cq,), jnp.float32), 'Wk': jax.random.normal(ks[3], (Ckv, Cq), jnp.float32) * s_kv, 'bk': jnp.zeros((Cq,), jnp.float32), 'Wv': jax.random.normal(ks[4], (Ckv, Cq), jnp.float32) * s_kv, 'bv': jnp.zeros((Cq,), jnp.float32), 'Wo': jax.random.normal(ks[5], (Cq, Cq), jnp.float32) * s_q, 'bo': jnp.zeros((Cq,), jnp.float32)}
    _L0_xattn_all = _L0_xattn_setup()
    _L0_xattn_in = {k: v for k, v in _L0_xattn_all.items() if k in ('Wq', 'bq', 'Wk', 'bk', 'Wv', 'bv', 'Wo', 'bo')}
    del _L0_xattn_all

    def _L0_attn_setup():
        import jax, jax.numpy as jnp
        import numpy as np
        T, B, H = (256, 32, 256)
        key = jax.random.key(seed)
        k1, k2, k3, k4 = jax.random.split(key, 4)
        s = 1.0 / np.sqrt(H)
        return {'inputs': jax.random.normal(k1, (T, B, H), dtype=jnp.float32), 'W': jax.random.normal(k2, (H, H), dtype=jnp.float32) * s, 'proj': jax.random.normal(k3, (H,), dtype=jnp.float32) * s, 'concat_w': jax.random.normal(k4, (H, 2 * H), dtype=jnp.float32) * s, 'concat_b': jnp.zeros((H,), dtype=jnp.float32)}
    _L0_attn_all = _L0_attn_setup()
    _L0_attn_in = {k: v for k, v in _L0_attn_all.items() if k in ('W', 'proj', 'concat_w', 'concat_b')}
    del _L0_attn_all

    def _L0_ffn_setup():
        import jax, jax.numpy as jnp
        import numpy as np
        TOP_K = 2
        EPS = 1e-09
        key = jax.random.key(seed)
        ks = jax.random.split(key, 6)
        B, T, D, H, E = (4, 512, 256, 512, 8)
        x = jax.random.normal(ks[0], (B, T, D), dtype=jnp.float32)
        Wg = jax.random.normal(ks[1], (E, D), dtype=jnp.float32) * 0.02
        W1 = jax.random.normal(ks[2], (E, 2 * H, D), dtype=jnp.float32) * 0.02
        b1 = jax.random.normal(ks[3], (E, 2 * H), dtype=jnp.float32) * 0.02
        Wo = jax.random.normal(ks[4], (D, H), dtype=jnp.float32) * 0.02
        bo = jax.random.normal(ks[5], (D,), dtype=jnp.float32) * 0.02
        return {'x': x, 'Wg': Wg, 'W1': W1, 'b1': b1, 'Wo': Wo, 'bo': bo}
    _L0_ffn_all = _L0_ffn_setup()
    _L0_ffn_in = {k: v for k, v in _L0_ffn_all.items() if k in ('Wg', 'W1', 'b1', 'Wo', 'bo')}
    del _L0_ffn_all
    return {'x': x, 'ctx_768': ctx_768, 'L0_xattn_Wq': _L0_xattn_in['Wq'], 'L0_xattn_bq': _L0_xattn_in['bq'], 'L0_xattn_Wk': _L0_xattn_in['Wk'], 'L0_xattn_bk': _L0_xattn_in['bk'], 'L0_xattn_Wv': _L0_xattn_in['Wv'], 'L0_xattn_bv': _L0_xattn_in['bv'], 'L0_xattn_Wo': _L0_xattn_in['Wo'], 'L0_xattn_bo': _L0_xattn_in['bo'], 'L0_attn_W': _L0_attn_in['W'], 'L0_attn_proj': _L0_attn_in['proj'], 'L0_attn_concat_w': _L0_attn_in['concat_w'], 'L0_attn_concat_b': _L0_attn_in['concat_b'], 'L0_ffn_Wg': _L0_ffn_in['Wg'], 'L0_ffn_W1': _L0_ffn_in['W1'], 'L0_ffn_b1': _L0_ffn_in['b1'], 'L0_ffn_Wo': _L0_ffn_in['Wo'], 'L0_ffn_bo': _L0_ffn_in['bo']}

def reference(x, ctx_768, L0_xattn_Wq, L0_xattn_bq, L0_xattn_Wk, L0_xattn_bk, L0_xattn_Wv, L0_xattn_bv, L0_xattn_Wo, L0_xattn_bo, L0_attn_W, L0_attn_proj, L0_attn_concat_w, L0_attn_concat_b, L0_ffn_Wg, L0_ffn_W1, L0_ffn_b1, L0_ffn_Wo, L0_ffn_bo):
    import jax
    import jax.numpy as jnp

    def _L0_xattn_ref(query, key_value, Wq, bq, Wk, bk, Wv, bv, Wo, bo):
        import jax, jax.numpy as jnp
        import numpy as np
        NUM_HEADS = 16
        CLAMP = 10000.0
        B, Nq, Cq = query.shape
        Nkv = key_value.shape[1]
        H = NUM_HEADS
        D = Cq // H
        scale = D ** (-0.5)
        q = (query @ Wq + bq).reshape(B, Nq, H, D).transpose(0, 2, 1, 3)
        k = (key_value @ Wk + bk).reshape(B, Nkv, H, D).transpose(0, 2, 1, 3)
        v = (key_value @ Wv + bv).reshape(B, Nkv, H, D).transpose(0, 2, 1, 3)
        attn = jnp.einsum('bhqd,bhkd->bhqk', q, k) * scale
        attn = jnp.clip(attn, -CLAMP, CLAMP)
        attn = jax.nn.softmax(attn, axis=-1)
        attn = jnp.where(jnp.any(jnp.isnan(attn)), jnp.asarray(1.0 / Nkv, attn.dtype), attn)
        x = jnp.einsum('bhqk,bhkd->bqhd', attn, v).reshape(B, Nq, Cq)
        return x @ Wo + bo

    def _L0_attn_ref(inputs, W, proj, concat_w, concat_b):
        import jax, jax.numpy as jnp
        import numpy as np
        T, B, H = (256, 32, 256)
        T_, B_, H_ = inputs.shape
        hp = jnp.tanh(jnp.einsum('sbh,hk->sbk', inputs, W))
        scores = jnp.einsum('sbk,k->sb', hp, proj)
        t_idx = jnp.arange(T_)
        mask = t_idx[None, :] < t_idx[:, None]
        neg = jnp.finfo(scores.dtype).min
        logits = jnp.where(mask[:, :, None], scores[None, :, :], neg)
        attn = jax.nn.softmax(logits, axis=1)
        context = jnp.einsum('tsb,sbh->tbh', attn, inputs)
        cat = jnp.concatenate([inputs, context], axis=-1)
        out = jnp.tanh(jnp.einsum('tbc,hc->tbh', cat, concat_w) + concat_b)
        out = out.at[:2].set(inputs[:2])
        return out

    def _L0_ffn_ref(x, Wg, W1, b1, Wo, bo):
        import jax, jax.numpy as jnp
        import numpy as np
        TOP_K = 2
        EPS = 1e-09
        E = Wg.shape[0]
        gate_logits = jnp.einsum('btd,ed->bte', x, Wg)
        gate_scores = jax.nn.softmax(gate_logits, axis=-1)
        topk_val, topk_idx = jax.lax.top_k(gate_scores, TOP_K)
        topk_val = topk_val / (topk_val.sum(axis=-1, keepdims=True) + EPS)
        comb = (jax.nn.one_hot(topk_idx, E, dtype=x.dtype) * topk_val[..., None]).sum(axis=-2)
        out = jnp.zeros_like(x)
        for e in range(E):
            h = jnp.einsum('btd,hd->bth', x, W1[e]) + b1[e]
            a, b = jnp.split(h, 2, axis=-1)
            g = a * jax.nn.sigmoid(b)
            eo = jnp.einsum('bth,dh->btd', g, Wo) + bo
            out = out + eo * comb[..., e:e + 1]
        return out
    x = x + _L0_xattn_ref(_layernorm(x, axis=-1), ctx_768, L0_xattn_Wq, L0_xattn_bq, L0_xattn_Wk, L0_xattn_bk, L0_xattn_Wv, L0_xattn_bv, L0_xattn_Wo, L0_xattn_bo)
    x = x + _L0_attn_ref(_layernorm(x, axis=-1), L0_attn_W, L0_attn_proj, L0_attn_concat_w, L0_attn_concat_b)
    x = x + _L0_ffn_ref(_layernorm(x, axis=-1), L0_ffn_Wg, L0_ffn_W1, L0_ffn_b1, L0_ffn_Wo, L0_ffn_bo)
    return x

_drawn_inputs = setup_inputs


def setup_inputs(seed=0):
    import zlib

    import numpy as np

    out = dict(_drawn_inputs(seed))
    spreads = {'L0_xattn_bq': (0.0, 0.372),
     'L0_xattn_bk': (0.0, 2.0),
     'L0_xattn_bv': (0.0, 0.1),
     'L0_xattn_bo': (0.0, 0.1),
     'L0_attn_concat_b': (0.0, 0.1)}
    factors = {'L0_ffn_b1': 22.851, 'L0_ffn_bo': 3.647}
    for name, (base, spread) in spreads.items():
        noise = np.random.default_rng([zlib.crc32(name.encode()), seed]).standard_normal(out[name].shape)
        drawn = base * np.exp(spread * noise) if base else spread * noise
        out[name] = jnp.asarray(drawn.astype(out[name].dtype))
    for name, factor in factors.items():
        out[name] = (out[name] * factor).astype(out[name].dtype)
    return out
```

```python
from contextlib import ExitStack

import numpy as np
import concourse.bass as bass
from concourse import mybir

ALU = mybir.AluOpType
ACT = mybir.ActivationFunctionType
AX = mybir.AxisListType
F32 = mybir.dt.float32
F32R = mybir.dt.float32r

T, NQ, C, CK, NK = 64, 32, 256, 192, 257
NKP = 258
NT = T * NQ
NTILE = NT // 128
CLAMP = 10000.0
EPS = 1e-5
NEG = float(np.finfo(np.float32).min)
E, HF = 8, 512
NPAIR = T // 2
CH = 8

C_ID = 0
C_GM = 128
C_OM = 132
C_R = 136
C_MN = 168
C_M01 = 232
C_IOTA = 234
C_END = 242


def constants():
    p = np.arange(128)
    c = np.zeros((128, C_END), np.float32)
    c[:, C_ID:C_ID + 128] = np.eye(128)
    c[:, C_GM:C_GM + 4] = (p[:, None] // 16) % 4 == np.arange(4)
    c[:, C_OM:C_OM + 4] = p[:, None] // 32 == np.arange(4)
    c[:, C_R:C_R + 32] = p[:, None] % 32 == np.arange(32)
    c[:, C_MN:C_MN + 64] = np.where(np.arange(64) < (p % 64)[:, None], 0.0, NEG)
    c[:, C_M01] = (p % 64) >= 2
    c[:, C_M01 + 1] = (p % 64) < 2
    c[:, C_IOTA:C_IOTA + 8] = np.arange(8)
    return c


def build(nc, d, out, vx_d, cb_d, dbg=None):
    ctx = ExitStack()
    with ctx:
        def sem(name):
            return ctx.enter_context(nc.semaphore(name))

        def alloc(stack, name, shape, dt=F32):
            return stack.enter_context(nc.sbuf_tensor(name, shape, dt))

        B = [ctx.enter_context(nc.psum_tensor(f"bank{i}", [128, 512], F32)) for i in range(8)]

        def per(name, shape, dt=F32):
            return alloc(ctx, name, shape, dt)

        cst = per("cst", [128, C_END])
        xb = per("xb", [128, NTILE, C])
        OT = per("OT", [128, 2, NT])
        Wo = per("Wo", [128, 2, C])
        bcol = per("bcol", [128, 8])
        bcc = per("bcc", [128, 3, C])
        base = per("base", [128, C])
        Wa = per("Wa", [128, 2, C])
        WcT = per("WcT", [128, 2, 2 * C])
        WgT = per("WgT", [128, 2, E])
        WgR = per("WgR", [128, 2, 2, E], F32R)
        b1c = per("b1c", [128, E, 8])
        WoT = per("WoT", [128, 4, C])
        st = per("st", [128, NTILE, 6])
        mv = per("mv", [128, NTILE, 2])
        rs = per("rs", [128, NTILE])
        epw = per("epw", [128, 2, NTILE])

        ident = cst[:, C_ID:C_ID + 128]

        s_c = sem("s_c")
        s_w = sem("s_w")
        s_w2 = sem("s_w2")
        s_x = [sem(f"s_x{i}") for i in range(4)]
        s_xb = sem("s_xb")
        s_st = sem("s_st")
        s_mv = sem("s_mv")
        s_ep = sem("s_ep")
        s_rs = sem("s_rs")
        s_xn = sem("s_xn")
        s_t0 = sem("s_t0")
        s_t0e = sem("s_t0e")
        s_q = sem("s_q")
        s_qe = sem("s_qe")
        s_bd = sem("s_bd")
        s_wh = sem("s_wh")
        s_wl = sem("s_wl")
        s_cx = [sem("s_cx0"), sem("s_cx1")]
        s_hi = sem("s_hi")
        s_lo = sem("s_lo")
        s_vx = sem("s_vx")
        s_vxe = sem("s_vxe")
        s_vz = sem("s_vz")
        s_vd = sem("s_vd")
        s_vb = [sem("s_vb0"), sem("s_vb1")]
        s_v1 = sem("s_v1")
        s_base = sem("s_base")
        s_basee = sem("s_basee")
        s_xbb = sem("s_xbb")
        s_k = sem("s_k")
        s_v = sem("s_v")
        s_s = sem("s_s")
        s_t = sem("s_t")
        s_tt = sem("s_tt")
        s_o = sem("s_o")
        s_ot = sem("s_ot")
        s_cl = sem("s_cl")
        s_nm = sem("s_nm")
        s_pte = sem("s_pte")
        s_rc = sem("s_rc")
        s_rm = sem("s_rm")
        s_m = sem("s_m")
        s_ke = sem("s_ke")
        s_pe = sem("s_pe")
        s_ve = sem("s_ve")
        s_tte = sem("s_tte")
        s_ex = sem("s_ex")
        s_pt = sem("s_pt")
        s_ote = sem("s_ote")

        ph1 = ExitStack()
        Wq = alloc(ph1, "Wq", [128, 2, C])
        wA = alloc(ph1, "wA", [128, 2, 2 * C])
        wH = alloc(ph1, "wH", [128, 2, 2 * C], F32R)
        wL = alloc(ph1, "wL", [128, 2, 2 * C], F32R)
        c256 = alloc(ph1, "c256", [128, 2, T])
        cx = alloc(ph1, "cx", [128, 2, 2, 2, NKP])
        hA = alloc(ph1, "hA", [128, 2, 2, 2, NKP], F32R)
        lA = alloc(ph1, "lA", [128, 2, 2, NKP], F32R)
        qbd = alloc(ph1, "qbd", [128, 2, T, 4, NQ])
        vx = alloc(ph1, "vx", [T, 4, 65])
        Vs = alloc(ph1, "Vs", [128, 3, 2, 4, 65])
        Vbd = alloc(ph1, "Vbd", [4, 2, CH, 260])
        st1 = ExitStack()
        xnT = alloc(st1, "xnT", [128, 2, NT])
        qT = alloc(st1, "qT", [128, 2, NT])
        st1.close()
        Sc = alloc(ph1, "Sc", [128, 2, 4, NK])
        Pm = alloc(ph1, "Pm", [128, 2, 4, NK])
        PT = alloc(ph1, "PT", [128, 2, 2, 4, 128])
        KT = alloc(ph1, "KT", [128, 2, 2, NKP])
        mx = alloc(ph1, "mx", [128, 2, 4])
        nm = alloc(ph1, "nm", [128, 2, 4])
        Pt = alloc(ph1, "Pt", [128, 2, 4])
        PTt = alloc(ph1, "PTt", [4, 2, 128])
        rc = alloc(ph1, "rc", [128, 2, 4])
        rm = alloc(ph1, "rm", [128, 2, 4, 4])
        Mb = alloc(ph1, "Mb", [128, 2, C])

        xa = OT[:, :, :].rearrange("p a (n c) -> p (a n) c", c=C)
        cf = cst
        gm = cf[:, C_GM:C_GM + 4]
        om = cf[:, C_OM:C_OM + 4]

        def sbank(n):
            return B[n % 4]

        pP = [B[2], B[3]]
        pT = [B[4], B[5]]
        pO = [B[6], B[7]]
        NST = 16

        with nc.Block() as block:

            @block.sync
            def _(sp):
                for g in range(4):
                    sp.dma_start(xa[:, 4 * g:4 * g + 4, :],
                                 d["x"].rearrange("(n a) b c -> (a b) n c", a=4)[:, 4 * g:4 * g + 4, :]
                                 ).then_inc(s_x[g], 16)
                sp.dma_start(cst[:, :], d["cst"]).then_inc(s_c, 16)
                sp.dma_start(Wq[:, :, :], d["Wq"].rearrange("(k p) n -> p k n", p=128)).then_inc(s_c, 16)
                sp.dma_start(bcol[:, :], d["bcol"]).then_inc(s_c, 16)
                for i, w in enumerate(("Wk", "Wv")):
                    o = i * C
                    sp.dma_start(wA[:, 0, o:o + C], d[w][0:128, :]).then_inc(s_w, 16)
                    sp.dma_start(wA[0:64, 1, o:o + C], d[w][128:192, :]).then_inc(s_w, 16)
                    sp.dma_start(wA[64:128, 1, o:o + C], d[w][128:192, :]).then_inc(s_w, 16)
                sp.dma_start(c256[:, 0, :], d["c256"][0:128, :]).then_inc(s_w, 16)
                sp.dma_start(c256[0:64, 1, :], d["c256"][128:192, :]).then_inc(s_w, 16)
                sp.dma_start(Wo[:, :, :], d["xWo"].rearrange("(k p) n -> p k n", p=128)).then_inc(s_w, 16)
                sp.dma_start(bcc[:, :, :], bcast(d["brow"], 128)).then_inc(s_w, 16)

                def load_ctx(j):
                    if j >= 2:
                        sp.wait_ge(s_lo, 2 * (j - 1))
                    s = s_cx[j % 2]
                    src = d["ctxT"]
                    sp.dma_start(cx[:, j % 2, 0, :, :], src[2 * j:2 * j + 2, 0:128, :].rearrange("b p n -> p b n")).then_inc(s, 16)
                    for h in range(2):
                        sp.dma_start(cx[64 * h:64 * h + 64, j % 2, 1, :, :],
                                     src[2 * j:2 * j + 2, 128:192, :].rearrange("b p n -> p b n")).then_inc(s, 16)

                load_ctx(0)
                load_ctx(1)
                sp.wait_ge(s_vxe, 1)
                sp.wait_ge(s_v1, 2)
                sp.dma_start(vx_d.rearrange("g t c -> t g c"), vx[:, :, :]).then_inc(s_vd, 16)
                sp.wait_ge(s_vd, 16)
                sp.wait_ge(s_vz, 1)

                def load_vb(c):
                    if c >= 2:
                        sp.wait_ge(s_o, CH * (c - 1))
                    for g in range(4):
                        sp.dma_start(Vbd[g:g + 1, c % 2, :, 65 * g:65 * g + 65],
                                     vx_d[g:g + 1, CH * c:CH * c + CH, :]).then_inc(s_vb[c % 2], 16)

                load_vb(0)
                load_vb(1)
                sp.dma_start(xb[0:64, :, :], d["x"].rearrange("t (n b) c -> b t n c", b=2)[0]).then_inc(s_xb, 16)
                sp.dma_start(xb[64:128, :, :], d["x"].rearrange("t (n b) c -> b t n c", b=2)[1]).then_inc(s_xb, 16)
                for j in range(2, NPAIR):
                    load_ctx(j)
                    if j % 4 == 3 and 2 <= (j + 1) // 4 < T // CH:
                        load_vb((j + 1) // 4)
                    if j == 4:
                        sp.dma_start(Wa[:, :, :], d["aW"].rearrange("(k p) n -> p k n", p=128)).then_inc(s_w2, 16)
                        sp.dma_start(WcT[:, 0, :], d["cwT"][0:128].rearrange("p k n -> p (k n)")).then_inc(s_w2, 16)
                        sp.dma_start(WcT[:, 1, :], d["cwT"][128:256].rearrange("p k n -> p (k n)")).then_inc(s_w2, 16)
                        sp.dma_start(WgT[:, :, :], d["WgT"].rearrange("(k p) n -> p k n", p=128)).then_inc(s_w2, 16)
                        sp.dma_start(b1c[:, :, :], d["b1c"]).then_inc(s_w2, 16)
                        sp.dma_start(WoT[:, :, :], d["fWoT"].rearrange("(k p) n -> p k n", p=128)).then_inc(s_w2, 16)

            @block.gpsimd
            def _(g):
                g.memset(epw[:, 0, :], EPS).then_inc(s_ep, 1)
                g.memset(epw[:, 1, :], -0.5).then_inc(s_ep, 1)
                g.memset(Vbd[:, :, :, :], 0.0).then_inc(s_vz, 1)
                g.memset(Vs[:, :, :, :, 64:65], 1.0).then_inc(s_v1, 1)
                g.memset(vx[:, :, 64:65], 1.0).then_inc(s_v1, 1)
                g.wait_ge(s_mv, NTILE)
                g.wait_ge(s_ep, 2)
                g.tensor_tensor(rs[:, :], mv[:, :, 1], epw[:, 0, :], ALU.add).then_inc(s_ep, 1)
                g.wait_ge(s_ep, 3)
                g.tensor_tensor(rs[:, :], rs[:, :], epw[:, 1, :], ALU.pow).then_inc(s_rs, 1)

                def split(j):
                    g.wait_ge(s_cx[j % 2], 48 * (j // 2 + 1))
                    if j >= 2:
                        g.wait_ge(s_v, 2 * (j - 1))
                    b = j % 2
                    g.tensor_scalar(hA[:, b, :, :, :].rearrange("p k b n -> p (k b n)"),
                                    cx[:, b, :, :, :].rearrange("p k b n -> p (k b n)"), 1.0, None, ALU.mult
                                    ).then_inc(s_hi, 1)
                    g.wait_ge(s_hi, j + 1)
                    g.tensor_tensor(lA[:, b, :, :], cx[:, b, 0, :, :], hA[:, b, 0, :, :].bitcast(F32), ALU.subtract
                                    ).then_inc(s_lo, 1)
                    g.wait_ge(s_lo, 2 * j + 1)
                    g.tensor_tensor(hA[64:128, b, 1, :, :], cx[64:128, b, 1, :, :],
                                    hA[64:128, b, 1, :, :].bitcast(F32), ALU.subtract).then_inc(s_lo, 1)
                    g.wait_ge(s_lo, 2 * j + 2)

                split(0)
                split(1)
                for i in range(T):
                    g.wait_ge(s_ex, 4 * i + 4)
                    g.tensor_scalar(Pt[:, i % 2, :], Pm[:, i % 2, :, NK - 1], 1.0, None, ALU.min).then_inc(s_pt, 1)
                    if i == 0:
                        g.wait_ge(s_xb, 32)
                        g.wait_ge(s_basee, 1)
                    if i < NTILE:
                        g.tensor_tensor(xb[:, i, :], xb[:, i, :], base[:, :], ALU.add).then_inc(s_xbb, 1)
                    if i % 2 == 1 and (i + 3) // 2 < NPAIR:
                        split((i + 3) // 2)

            @block.vector
            def _(v):
                for n in range(NTILE):
                    v.wait_ge(s_x[n // 4], 16)
                    v.bn_stats(st[:, n, :], xa[:, n, :]).then_inc(s_st, 1)
                    if n >= 1:
                        v.wait_ge(s_st, n)
                        v.bn_aggr(mv[:, n - 1, :], st[:, n - 1, :]).then_inc(s_mv, 1)
                v.wait_ge(s_st, NTILE)
                v.bn_aggr(mv[:, NTILE - 1, :], st[:, NTILE - 1, :]).then_inc(s_mv, 1)
                v.wait_ge(s_w, 16 * 10)
                v.tensor_copy(wH[:, :, :], wA[:, :, :]).then_inc(s_wh, 1)
                v.wait_ge(s_wh, 1)
                v.tensor_tensor(wL[:, :, :], wA[:, :, :], wH[:, :, :].bitcast(F32), ALU.subtract).then_inc(s_wl, 1)
                v.wait_ge(s_mv, NTILE)
                v.wait_ge(s_rs, 1)
                for n in range(NTILE):
                    v.tensor_scalar(xa[:, n, :], xa[:, n, :], mv[:, n, 0:1], rs[:, n:n + 1],
                                    ALU.subtract, ALU.mult).then_inc(s_xn, 1)
                v.wait_ge(s_vx, 1)
                v.tensor_copy(vx[:, :, 0:64], B[4][0:T, 0:C].rearrange("p (g c) -> p g c", g=4)).then_inc(s_vxe, 1)
                v.wait_ge(s_base, 1)
                v.tensor_tensor(base[:, :], B[5][:, 0:C], bcc[:, 0, :], ALU.add).then_inc(s_basee, 1)
                for n in range(8):
                    nb, m = n // 2, n % 2
                    v.wait_ge(s_q, n + 1)
                    v.tensor_scalar(qT[:, m, 512 * nb:512 * nb + 512], sbank(8 + n)[:, :], bcol[:, m:m + 1], 0.25,
                                    ALU.add, ALU.mult).then_inc(s_qe, 1)
                for nb in range(4):
                    for m in range(2):
                        for h in range(4):
                            v.wait_ge(s_qe, 2 * nb + m + 1)
                            v.tensor_scalar(qbd[:, m, 16 * nb:16 * nb + 16, h, :],
                                            qT[:, m, 512 * nb:512 * nb + 512].rearrange("p (t b) -> p t b", b=NQ),
                                            gm[:, h:h + 1], None, ALU.mult).then_inc(s_bd, 1)
                v.wait_ge(s_bd, 32)

                def clip(i, g):
                    v.wait_ge(s_s, 4 * i + g + 1)
                    v.tensor_scalar(Sc[:, i % 2, g, :], B[g % 2][:, 0:NK], -CLAMP, -CLAMP, ALU.max, ALU.max,
                                    accum_out=mx[:, i % 2, g:g + 1]).then_inc(s_cl, 1)

                def negmax(i, p):
                    v.wait_ge(s_cl, 4 * i + 2 * p + 2)
                    v.tensor_scalar(nm[:, i % 2, 2 * p:2 * p + 2], mx[:, i % 2, 2 * p:2 * p + 2], CLAMP, -1.0,
                                    ALU.min, ALU.mult).then_inc(s_nm, 1)

                def ptevac(i, p):
                    v.wait_ge(s_t, 2 * i + p + 1)
                    v.tensor_scalar(PT[:, i % 2, p, :, :].rearrange("p a b -> p (a b)"), pT[p][:, :], 1.0, None,
                                    ALU.min).then_inc(s_pte, 1)

                def recip(i):
                    v.wait_ge(s_o, i + 1)
                    v.reciprocal(rc[:, i % 2, :], pO[i % 2][:, 0:260].rearrange("p (g c) -> p g c", g=4)[:, :, 64]
                                 ).then_inc(s_rc, 1)

                def rmask(i):
                    v.wait_ge(s_rc, i + 1)
                    v.tensor_tensor(rm[:, i % 2, :, :], rc[:, i % 2, :].unsqueeze(2).broadcast_to([128, 4, 4]),
                                    om.unsqueeze(1).broadcast_to([128, 4, 4]), ALU.mult).then_inc(s_rm, 1)

                def norm(i):
                    v.wait_ge(s_rm, i + 1)
                    v.tensor_tensor(Mb[:, i % 2, :].rearrange("p (g h c) -> p g h c", g=4, h=4),
                                    pO[i % 2][:, 0:260].rearrange("p (g c) -> p g c", g=4)[:, :, 0:64]
                                    .rearrange("p g (h c) -> p g h c", h=4),
                                    rm[:, i % 2, :, :].unsqueeze(3).broadcast_to([128, 4, 4, 16]), ALU.mult
                                    ).then_inc(s_m, 1)

                for i in range(T + 2):
                    if i < T:
                        clip(i, 0)
                    if i >= 2:
                        recip(i - 2)
                    if i < T:
                        clip(i, 1)
                    if i >= 2:
                        rmask(i - 2)
                    if i < T:
                        negmax(i, 0)
                    if 1 <= i <= T:
                        ptevac(i - 1, 0)
                    if i >= 2:
                        norm(i - 2)
                    if i < T:
                        clip(i, 2)
                        clip(i, 3)
                    if 1 <= i <= T:
                        ptevac(i - 1, 1)
                    if i < T:
                        negmax(i, 1)

            @block.scalar
            def _(a):
                for n in range(8):
                    nb, k = n // 2, n % 2
                    a.wait_ge(s_t0, n + 1)
                    a.activation(xnT[:, k, 512 * nb:512 * nb + 512], sbank(n)[:, :], ACT.Copy).then_inc(s_t0e, 1)

                def kevac(i, m):
                    a.wait_ge(s_k, 2 * i + m + 1)
                    n = 3 * i + m
                    if m == 1 and i >= 2:
                        a.wait_ge(s_tt, i - 1)
                    ins = a.activation(KT[:, i % 2, m, :], pP[n % 2][:, 0:NKP], ACT.Identity,
                                       bias=bcol[:, 2 + m:3 + m])
                    ins.then_inc(s_ke, 1)

                def vevac(i):
                    a.wait_ge(s_v, i + 1)
                    n = 3 * i + 2
                    if i == 0:
                        a.wait_ge(s_v1, 2)
                    a.activation(Vs[:, i % 3, :, :, 0:64],
                                 pP[n % 2][:, :].rearrange("p (c g e) -> p c g e", c=2, g=4), ACT.Copy
                                 ).then_inc(s_ve, 1)

                def tevac(i):
                    a.wait_ge(s_tt, i + 1)
                    n = 3 * (i + 2) + 1
                    a.activation(PTt[:, i % 2, :], pP[n % 2][0:4, 384:512], ACT.Copy).then_inc(s_tte, 1)

                def exps(i, g):
                    a.wait_ge(s_nm, 2 * i + g // 2 + 1)
                    a.activation(Pm[:, i % 2, g, :], Sc[:, i % 2, g, :], ACT.Exp, bias=nm[:, i % 2, g:g + 1]
                                 ).then_inc(s_ex, 1)

                def otevac(i):
                    a.wait_ge(s_ot, i + 1)
                    a.activation(OT[:, :, :].rearrange("p m (b t) -> p m b t", t=T)[:, :, :, i],
                                 pO[i % 2][:, 320:384].rearrange("p (m q) -> p m q", m=2), ACT.Copy
                                 ).then_inc(s_ote, 1)

                for i in range(-1, T + 2):
                    if i + 1 < T:
                        kevac(i + 1, 0)
                    if 0 <= i < T:
                        exps(i, 0)
                        exps(i, 1)
                    if i + 1 < T:
                        kevac(i + 1, 1)
                    if 1 <= i <= T:
                        tevac(i - 1)
                    if 0 <= i < T:
                        exps(i, 2)
                        exps(i, 3)
                    if i + 1 < T:
                        vevac(i + 1)
                    if i >= 2:
                        otevac(i - 2)

            @block.tensor
            def _(t):
                t.wait_ge(s_c, 48)
                t.wait_ge(s_w, 16 * 10)
                for k in range(2):
                    K = 128 - 64 * k
                    mm = t.matmul(B[4][0:T, 0:C], c256[0:K, k, :], wA[0:K, k, C:2 * C], start=(k == 0), stop=(k == 1))
                mm.then_inc(s_vx, 1)
                for k in range(2):
                    mm = t.matmul(B[5][:, 0:C], bcol[:, 4 + k:5 + k].broadcast_to([128, 128]), Wo[:, k, :],
                                  start=(k == 0), stop=(k == 1))
                mm.then_inc(s_base, 1)
                for n in range(8):
                    nb, k = n // 2, n % 2
                    if n >= 4:
                        t.wait_ge(s_t0e, n - 3)
                    for j in range(4):
                        t.wait_ge(s_xn, 4 * nb + j + 1)
                        mm = t.transpose(sbank(n)[:, 128 * j:128 * j + 128], xa[:, 4 * nb + j, 128 * k:128 * k + 128],
                                         ident)
                    mm.then_inc(s_t0, 1)
                for n in range(8):
                    nb, m = n // 2, n % 2
                    t.wait_ge(s_t0e, min(8, max(2 * nb + 2, n + 5)))
                    if n >= 4:
                        t.wait_ge(s_qe, n - 3)
                    for k in range(2):
                        mm = t.matmul(sbank(n)[:, :], Wq[:, k, 128 * m:128 * m + 128], xnT[:, k, 512 * nb:512 * nb + 512],
                                      start=(k == 0), stop=(k == 1))
                    mm.then_inc(s_q, 1)

                def terms(b, bi):
                    hi0, hi1 = hA[:, b, 0, bi, :], hA[:, b, 1, bi, :]
                    lo0 = lA[:, b, bi, :]
                    return [(hi0, wH[:, 0, :]), (hi0, wL[:, 0, :]), (lo0, wH[:, 0, :]),
                            (hi1, wH[:, 1, :]), (hi1, wL[:, 1, :])]

                def wait_pp(n):
                    if n < 2:
                        return
                    i, r = (n - 2) // 3, (n - 2) % 3
                    if r == 2:
                        t.wait_ge(s_ve, i + 1)
                    else:
                        t.wait_ge(s_ke, 2 * i + r + 1)
                        if r == 1 and i >= 2:
                            t.wait_ge(s_tte, i - 1)

                def kproj(i, m):
                    n = 3 * i + m
                    wait_pp(n)
                    t.wait_ge(s_lo, 2 * (i // 2 + 1))
                    for e, (c, w) in enumerate(terms((i // 2) % 2, i % 2)):
                        mm = t.matmul(pP[n % 2][:, 0:NKP], w[:, 128 * m:128 * m + 128], c, start=(e == 0), stop=(e == 4))
                    mm.then_inc(s_k, 1)

                def vproj(i):
                    n = 3 * i + 2
                    wait_pp(n)
                    for c in range(2):
                        for e, (x, w) in enumerate(terms((i // 2) % 2, i % 2)):
                            mm = t.matmul(pP[n % 2][:, C * c:C * c + C], x[:, 128 * c:128 * c + 128], w[:, C:2 * C],
                                          start=(e == 0), stop=(e == 4))
                    mm.then_inc(s_v, 1)

                def scores(i, p):
                    if p == 0:
                        t.wait_ge(s_ke, 2 * i + 2)
                    for gg in range(2):
                        if 4 * i + 2 * p >= 2:
                            t.wait_ge(s_cl, 4 * i + 2 * p - 1 + gg)
                        r = slice(64 * gg, 64 * gg + 64)
                        t.matmul(B[gg][:, 0:NK], qbd[r, p, i, :, :], KT[r, i % 2, p, 0:NK], start=True, stop=True
                                 ).then_inc(s_s, 1)

                def transp(i, p):
                    t.wait_ge(s_ex, 4 * i + 2 * p + 2)
                    if i >= 1:
                        t.wait_ge(s_pte, 2 * (i - 1) + p + 1)
                    for gg in range(2):
                        for c in range(2):
                            o = 256 * gg + 128 * c
                            mm = t.transpose(pT[p][:, o:o + 128], Pm[:, i % 2, 2 * p + gg, 128 * c:128 * c + 128], ident)
                    mm.then_inc(s_t, 1)

                def tail(i):
                    t.wait_ge(s_pt, i + 1)
                    n = 3 * (i + 2) + 1
                    if i + 2 >= T:
                        t.wait_ge(s_ve, T)
                        t.wait_ge(s_tte, i)
                    t.transpose(pP[n % 2][0:4, 384:512], Pt[:, i % 2, :], ident).then_inc(s_tt, 1)

                def pv(i):
                    if i >= 2:
                        t.wait_ge(s_ote, i - 1)
                    t.wait_ge(s_ve, i + 1)
                    first = True
                    for p in range(2):
                        t.wait_ge(s_pte, 2 * i + p + 1)
                        for gg in range(2):
                            g = 2 * p + gg
                            for c in range(2):
                                t.matmul(pO[i % 2][:, 65 * g:65 * g + 65], PT[:, i % 2, p, 2 * gg + c, :],
                                         Vs[:, i % 3, c, g, :], start=first, stop=False, skip_group_check=True)
                                first = False
                    t.wait_ge(s_tte, i + 1)
                    c = i // CH
                    t.wait_ge(s_vb[c % 2], 64 * (c // 2 + 1))
                    t.matmul(pO[i % 2][:, 0:260], PTt[:, i % 2, :], Vbd[:, c % 2, i % CH, :], start=False, stop=True,
                             skip_group_check=True).then_inc(s_o, 1)

                def gather(i):
                    t.wait_ge(s_m, i + 1)
                    for m in range(2):
                        mm = t.matmul(pO[i % 2][:, 320 + NQ * m:320 + NQ * m + NQ], Mb[:, i % 2, 128 * m:128 * m + 128],
                                      cst[:, C_R:C_R + 32], start=True, stop=True)
                    mm.then_inc(s_ot, 1)

                t.wait_ge(s_wl, 1)
                t.wait_ge(s_qe, 8)
                t.wait_ge(s_bd, 32)
                t.wait_ge(s_vxe, 1)
                t.wait_ge(s_basee, 1)
                for i in range(-1, T + 2):
                    if 0 <= i < T:
                        scores(i, 0)
                    if i + 1 < T:
                        kproj(i + 1, 0)
                    if 1 <= i <= T:
                        transp(i - 1, 0)
                    if 0 <= i < T:
                        scores(i, 1)
                    if i + 1 < T:
                        kproj(i + 1, 1)
                    if 1 <= i <= T:
                        tail(i - 1)
                        transp(i - 1, 1)
                    if i + 1 < T:
                        vproj(i + 1)
                    if 1 <= i <= T:
                        pv(i - 1)
                    if i >= 2:
                        gather(i - 2)
        ph1.close()

        ph2 = ExitStack()
        xn = alloc(ph2, "xn", [128, NTILE, C])
        xT = alloc(ph2, "xT", [128, 2, NT])
        hp = alloc(ph2, "hp", [128, 2, NT])
        L = alloc(ph2, "L", [128, NTILE, 64])
        sm = alloc(ph2, "sm", [128, 3, NTILE])
        Ab = alloc(ph2, "Ab", [128, NTILE, 128])
        AT = alloc(ph2, "AT", [128, 2, 128])
        Y = alloc(ph2, "Y", [128, 2, C])
        z = alloc(ph2, "z", [128, 2, C])
        zt = alloc(ph2, "zt", [128, 2, C])
        u_y = sem("u_y")
        u_x = sem("u_x")
        u_st = sem("u_st")
        u_mv = sem("u_mv")
        u_e = sem("u_e")
        u_rs = sem("u_rs")
        u_xn = sem("u_xn")
        u_t = sem("u_t")
        u_te = sem("u_te")
        u_h = sem("u_h")
        u_he = sem("u_he")
        u_sc = sem("u_sc")
        u_l = sem("u_l")
        u_sm = sem("u_sm")
        u_ex = sem("u_ex")
        u_az = sem("u_az")
        u_a = sem("u_a")
        u_at = sem("u_at")
        u_ate = sem("u_ate")
        u_xy = sem("u_xy")
        u_ye = sem("u_ye")
        u_o = sem("u_o")
        u_z = sem("u_z")
        u_zt = sem("u_zt")
        u_b2 = sem("u_b2")
        u_x3 = sem("u_x3")
        m01 = cst[:, C_M01:C_M01 + 1]
        m10 = cst[:, C_M01 + 1:C_M01 + 2]

        with nc.Block() as block:

            @block.tensor
            def _(t):
                t.wait_ge(s_ote, T)
                t.wait_ge(s_w2, 96)
                for n in range(8):
                    for jj in range(2):
                        j = 2 * n + jj
                        for k in range(2):
                            mm = t.matmul(B[n][:, C * jj:C * jj + C],
                                          OT[:, k, 128 * j:128 * j + 128],
                                          Wo[:, k, :], start=(k == 0), stop=(k == 1))
                    mm.then_inc(u_y, 1)
                for n in range(8):
                    nb, k = n // 2, n % 2
                    t.wait_ge(u_x, n + 1)
                    for j in range(4):
                        t.wait_ge(u_xn, 4 * nb + j + 1)
                        mm = t.transpose(B[n][:, 128 * j:128 * j + 128], xn[:, 4 * nb + j, 128 * k:128 * k + 128], ident)
                    mm.then_inc(u_t, 1)
                for n in range(8):
                    nb, m = n // 2, n % 2
                    t.wait_ge(u_te, max(2 * nb + 2, n + 1))
                    for k in range(2):
                        mm = t.matmul(B[n][:, :], Wa[:, k, 128 * m:128 * m + 128], xT[:, k, 512 * nb:512 * nb + 512],
                                      start=(k == 0), stop=(k == 1))
                    mm.then_inc(u_h, 1)
                for nb in range(4):
                    t.wait_ge(u_he, 2 * nb + 2)
                    for k in range(2):
                        mm = t.matmul(B[nb][:, :], bcol[:, 6 + k:7 + k].broadcast_to([128, 128]),
                                      hp[:, k, 512 * nb:512 * nb + 512], start=(k == 0), stop=(k == 1))
                    mm.then_inc(u_sc, 1)
                ob = [B[6], B[7], B[0], B[1]]

                def xy(j):
                    if j >= 4:
                        t.wait_ge(u_z, j - 3)
                    if 2 <= j < 4:
                        t.wait_ge(u_l, 8)
                    for k in range(2):
                        mm = t.matmul(ob[j % 4][:, :], xT[:, k, 128 * j:128 * j + 128], WcT[:, k, :],
                                      start=(k == 0), stop=False, skip_group_check=True)
                    mm.then_inc(u_xy, 1)

                xy(0)
                for j in range(NTILE):
                    if j + 1 < NTILE:
                        xy(j + 1)
                    t.wait_ge(u_a, 2)
                    if j >= 2:
                        t.wait_ge(u_ate, j - 1)
                    t.transpose(B[4 + j % 2][:, 0:128], Ab[:, j, :], ident).then_inc(u_at, 1)
                    t.wait_ge(u_ate, j + 1)
                    t.wait_ge(u_ye, j + 1)
                    t.matmul(ob[j % 4][:, 0:C], AT[:, j % 2, :], Y[:, j % 2, :], start=False, stop=True,
                             skip_group_check=True).then_inc(u_o, 1)

            def resid(v, j):
                v.wait_ge(u_zt, j + 1)
                v.wait_ge(u_b2, j + 1)
                v.scalar_tensor_tensor(out=xb[:, j, :], in0=zt[:, j % 2, :], scalar=m01, in1=xb[:, j, :],
                                       op0=ALU.mult, op1=ALU.add).then_inc(u_x3, 1)

            def layer_stats(v, n, src, ready, done):
                v.wait_ge(ready, n + 1)
                for jj in range(2):
                    v.bn_stats(st[:, 2 * n + jj, :], src[:, 2 * n + jj, :]).then_inc(done, 1)

            @block.vector
            def _(v):
                for n in range(8):
                    v.wait_ge(u_y, n + 1)
                    v.wait_ge(s_xbb, NTILE)
                    v.tensor_tensor(xb[:, 2 * n:2 * n + 2, :], B[n][:, :].rearrange("p (a c) -> p a c", a=2),
                                    xb[:, 2 * n:2 * n + 2, :], ALU.add).then_inc(u_x, 1)
                    if n:
                        layer_stats(v, n - 1, xb, u_x, u_st)
                layer_stats(v, 7, xb, u_x, u_st)
                for n in range(NTILE):
                    v.wait_ge(u_st, n + 1)
                    v.bn_aggr(mv[:, n, :], st[:, n, :]).then_inc(u_mv, 1)
                v.wait_ge(u_rs, 1)
                for n in range(NTILE):
                    v.tensor_scalar(xn[:, n, :], xb[:, n, :], mv[:, n, 0:1], rs[:, n:n + 1],
                                    ALU.subtract, ALU.mult).then_inc(u_xn, 1)
                for nb in range(4):
                    v.wait_ge(u_sc, nb + 1)
                    for h in range(2):
                        r = slice(64 * h, 64 * h + 64)
                        v.tensor_tensor(L[r, 4 * nb:4 * nb + 4, :],
                                        B[nb][r, :].rearrange("p (j h s) -> p j h s", h=2, s=64)[:, :, h, :],
                                        cst[r, C_MN:C_MN + 64].unsqueeze(1).broadcast_to([64, 4, 64]), ALU.add
                                        ).then_inc(u_l, 1)
                v.wait_ge(u_l, 8)
                v.tensor_reduce(sm[:, 0, :], L[:, :, :], AX.X, ALU.max).then_inc(u_sm, 1)
                v.wait_ge(u_sm, 1)
                v.tensor_tensor(L[:, :, :], L[:, :, :], sm[:, 0, :].unsqueeze(2).broadcast_to([128, NTILE, 64]),
                                ALU.subtract).then_inc(u_sm, 1)
                v.wait_ge(u_ex, 1)
                v.tensor_reduce(sm[:, 1, :], L[:, :, :], AX.X, ALU.add).then_inc(u_sm, 1)
                v.wait_ge(u_sm, 3)
                v.reciprocal(sm[:, 2, :], sm[:, 1, :]).then_inc(u_sm, 1)
                v.wait_ge(u_sm, 4)
                v.wait_ge(u_az, 1)
                for h in range(2):
                    r = slice(64 * h, 64 * h + 64)
                    v.tensor_tensor(Ab[r, :, 64 * h:64 * h + 64], L[r, :, :],
                                    sm[r, 2, :].unsqueeze(2).broadcast_to([64, NTILE, 64]), ALU.mult).then_inc(u_a, 1)
                for j in range(NTILE):
                    v.wait_ge(u_at, j + 1)
                    v.tensor_copy(AT[:, j % 2, :], B[4 + j % 2][:, 0:128]).then_inc(u_ate, 1)
                    v.scalar_tensor_tensor(out=xb[:, j, :], in0=xn[:, j, :], scalar=m10, in1=xb[:, j, :],
                                           op0=ALU.mult, op1=ALU.add).then_inc(u_b2, 1)
                    v.wait_ge(u_o, j + 1)
                    v.tensor_tensor(z[:, j % 2, :], [B[6], B[7], B[0], B[1]][j % 4][:, 0:C], bcc[:, 1, :], ALU.add
                                    ).then_inc(u_z, 1)
                    if j:
                        resid(v, j - 1)
                resid(v, NTILE - 1)

            @block.gpsimd
            def _(g):
                g.wait_ge(s_ote, T)
                g.memset(Ab[:, :, :], 0.0).then_inc(u_az, 1)
                g.wait_ge(u_mv, NTILE)
                g.tensor_tensor(rs[:, :], mv[:, :, 1], epw[:, 0, :], ALU.add).then_inc(u_e, 1)
                g.wait_ge(u_e, 1)
                g.tensor_tensor(rs[:, :], rs[:, :], epw[:, 1, :], ALU.pow).then_inc(u_rs, 1)

            @block.scalar
            def _(a):
                for n in range(8):
                    nb, k = n // 2, n % 2
                    a.wait_ge(u_t, n + 1)
                    a.activation(xT[:, k, 512 * nb:512 * nb + 512], B[n][:, :], ACT.Copy).then_inc(u_te, 1)
                for n in range(8):
                    nb, m = n // 2, n % 2
                    a.wait_ge(u_h, n + 1)
                    a.activation(hp[:, m, 512 * nb:512 * nb + 512], B[n][:, :], ACT.Tanh).then_inc(u_he, 1)
                a.wait_ge(u_sm, 2)
                a.activation(L[:, :, :], L[:, :, :], ACT.Exp).then_inc(u_ex, 1)

                ob = [B[6], B[7], B[0], B[1]]
                for j in range(NTILE):
                    a.wait_ge(u_xy, j + 1)
                    if j >= 2:
                        a.wait_ge(u_o, j - 1)
                    a.activation(Y[:, j % 2, :], ob[j % 4][:, C:2 * C], ACT.Copy).then_inc(u_ye, 1)
                    if j:
                        a.wait_ge(u_z, j)
                        if j >= 3:
                            a.wait_ge(u_x3, j - 2)
                        a.activation(zt[:, (j - 1) % 2, :], z[:, (j - 1) % 2, :], ACT.Tanh).then_inc(u_zt, 1)
                a.wait_ge(u_z, NTILE)
                a.activation(zt[:, 1, :], z[:, 1, :], ACT.Tanh).then_inc(u_zt, 1)
        ph2.close()

        ph3 = ExitStack()
        yn = alloc(ph3, "yn", [128, 2, C])
        xh = alloc(ph3, "xh", [128, 2, NT], F32R)
        xl = alloc(ph3, "xl", [128, 2, NT], F32R)
        w1 = alloc(ph3, "w1", [128, 2, 2 * HF])
        w1h = alloc(ph3, "w1h", [128, 2, 2, 2 * HF], F32R)
        w1l = alloc(ph3, "w1l", [128, 2, 2, 2 * HF], F32R)
        G = alloc(ph3, "G", [128, 4, NT])
        cbc = alloc(ph3, "cbc", [128, 2, NT])
        sg = alloc(ph3, "sg", [128, 2, 512])
        ug = alloc(ph3, "ug", [128, 2, 512])
        vg = alloc(ph3, "vg", [128, 2, 512])
        gl = alloc(ph3, "gl", [128, NTILE, E])
        g8 = alloc(ph3, "g8", [128, NTILE, E])
        gi = alloc(ph3, "gi", [128, NTILE, E], mybir.dt.uint32)
        gf = alloc(ph3, "gf", [128, NTILE, 2])
        g1 = alloc(ph3, "g1", [128, NTILE, E])
        g2 = alloc(ph3, "g2", [128, NTILE, E])
        gs = alloc(ph3, "gs", [128, 4, NTILE])
        cT = alloc(ph3, "cT", [E, NT])
        fo = alloc(ph3, "fo", [128, 2, 2 * C])
        f_st = sem("f_st")
        f_mv = sem("f_mv")
        f_e = sem("f_e")
        f_rs = sem("f_rs")
        f_xn = sem("f_xn")
        f_t = sem("f_t")
        f_hi = sem("f_hi")
        f_lo = sem("f_lo")
        f_wg = sem("f_wg")
        f_g = sem("f_g")
        f_gc = sem("f_gc")
        f_ge = sem("f_ge")
        f_cm = sem("f_cm")
        f_ct = sem("f_ct")
        f_cte = sem("f_cte")
        f_cd = sem("f_cd")
        f_cb = [sem("f_cb0"), sem("f_cb1")]
        f_w = sem("f_w")
        f_wh = sem("f_wh")
        f_wl = sem("f_wl")
        f_h = sem("f_h")
        f_sg = sem("f_sg")
        f_ug = sem("f_ug")
        f_vg = sem("f_vg")
        f_ac = sem("f_ac")
        f_b3 = sem("f_b3")
        f_o = sem("f_o")
        f_fo = sem("f_fo")
        f_out = [sem("f_out0"), sem("f_out1")]
        NU = E * 16

        def unit(n):
            return n // 16, (n // 4) % 4, n % 4

        with nc.Block() as block:

            @block.sync
            def _(sp):
                sp.wait_ge(u_x3, NTILE)
                for e in range(E):
                    if e >= 1:
                        sp.wait_ge(f_wl, e)
                    sp.dma_start(w1[:, :, :], d["W1T"][e].rearrange("(k p) n -> p k n", p=128)).then_inc(f_w, 16)
                    if e == 0:
                        sp.wait_ge(f_cte, 4)
                        sp.dma_start(cb_d, cT[:, :]).then_inc(f_cd, 16)
                        sp.wait_ge(f_cd, 16)
                        sp.dma_start(cbc[:, 0, :], bcast(cb_d[0:1, :], 128, True)).then_inc(f_cb[0], 16)
                        sp.dma_start(cbc[:, 1, :], bcast(cb_d[1:2, :], 128, True)).then_inc(f_cb[1], 16)
                    if e >= 2:
                        sp.wait_ge(f_ug, 16 * (e - 1))
                        sp.dma_start(cbc[:, e % 2, :], bcast(cb_d[e:e + 1, :], 128, True)).then_inc(f_cb[e % 2], 16)
                for n in range(8):
                    sp.wait_ge(f_fo, n + 1)
                    for jj in range(2):
                        j = 2 * n + jj
                        sp.dma_start(out.rearrange("t (n b) c -> n b t c", b=2)[j],
                                     fo[:, n % 2, C * jj:C * jj + C]).then_inc(f_out[n % 2], 16)
                sp.wait_ge(f_out[0], 128)
                sp.wait_ge(f_out[1], 128)

            @block.gpsimd
            def _(g):
                g.wait_ge(u_x3, NTILE)
                g.wait_ge(f_mv, NTILE)
                g.tensor_tensor(rs[:, :], mv[:, :, 1], epw[:, 0, :], ALU.add).then_inc(f_e, 1)
                g.wait_ge(f_e, 1)
                g.tensor_tensor(rs[:, :], rs[:, :], epw[:, 1, :], ALU.pow).then_inc(f_rs, 1)

                def wsplit(e):
                    g.wait_ge(f_w, 16 * (e + 1))
                    if e >= 2:
                        g.wait_ge(f_h, 16 * (e - 1))
                    g.tensor_scalar(w1h[:, e % 2, :, :].rearrange("p k n -> p (k n)"),
                                    w1[:, :, :].rearrange("p k n -> p (k n)"), 1.0, None, ALU.mult).then_inc(f_wh, 1)
                    g.wait_ge(f_wh, e + 1)
                    g.tensor_tensor(w1l[:, e % 2, :, :], w1[:, :, :], w1h[:, e % 2, :, :].bitcast(F32), ALU.subtract
                                    ).then_inc(f_wl, 1)

                wsplit(0)
                for n in range(NU):
                    e, m, nb = unit(n)
                    if n % 16 == 0:
                        g.wait_ge(f_cb[e % 2], 16 * (e // 2 + 1))
                    g.wait_ge(f_sg, n + 1)
                    if n >= 2:
                        g.wait_ge(f_vg, n - 1)
                    g.tensor_tensor(ug[:, n % 2, :], sg[:, n % 2, :], cbc[:, e % 2, 512 * nb:512 * nb + 512], ALU.mult
                                    ).then_inc(f_ug, 1)
                    if n % 16 == 4 and e + 1 < E:
                        wsplit(e + 1)

            @block.vector
            def _(v):
                for n in range(NTILE):
                    v.wait_ge(u_x3, n + 1)
                    v.bn_stats(st[:, n, :], xb[:, n, :]).then_inc(f_st, 1)
                for n in range(NTILE):
                    v.wait_ge(f_st, n + 1)
                    v.bn_aggr(mv[:, n, :], st[:, n, :]).then_inc(f_mv, 1)
                v.wait_ge(s_w2, 96)
                v.tensor_copy(WgR[:, 0, :, :], WgT[:, :, :]).then_inc(f_wg, 1)
                v.wait_ge(f_wg, 1)
                v.tensor_tensor(WgR[:, 1, :, :], WgT[:, :, :], WgR[:, 0, :, :].bitcast(F32), ALU.subtract
                                ).then_inc(f_wg, 1)
                v.wait_ge(f_rs, 1)
                def low(j):
                    v.wait_ge(f_hi, j + 1)
                    v.tensor_tensor(xl[:, :, 128 * j:128 * j + 128],
                                    B[j % 4][:, 0:C].rearrange("p (k n) -> p k n", k=2),
                                    xh[:, :, 128 * j:128 * j + 128].bitcast(F32), ALU.subtract).then_inc(f_lo, 1)

                for j in range(NTILE):
                    if j >= 2:
                        v.wait_ge(f_t, j - 1)
                    v.tensor_scalar(yn[:, j % 2, :], xb[:, j, :], mv[:, j, 0:1], rs[:, j:j + 1],
                                    ALU.subtract, ALU.mult).then_inc(f_xn, 1)
                    if j:
                        low(j - 1)
                low(NTILE - 1)
                v.wait_ge(f_g, NTILE)
                cnt = [0]

                def step(ins):
                    cnt[0] += 1
                    ins.then_inc(f_gc, 1)
                    v.wait_ge(f_gc, cnt[0])

                def bc(ap):
                    return ap.unsqueeze(2).broadcast_to([128, NTILE, E])

                step(v.tensor_copy(gl[:, :, :], B[4][:, 0:NTILE * E].rearrange("p (n e) -> p n e", e=E)))
                step(v.tensor_reduce(gs[:, 0, :], gl[:, :, :], AX.X, ALU.max))
                v.tensor_tensor(gl[:, :, :], gl[:, :, :], bc(gs[:, 0, :]), ALU.subtract).then_inc(f_ge, 1)
                v.wait_ge(f_ge, 2)
                step(v.tensor_reduce(gs[:, 1, :], gl[:, :, :], AX.X, ALU.add))
                step(v.reciprocal(gs[:, 2, :], gs[:, 1, :]))
                step(v.tensor_tensor(gl[:, :, :], gl[:, :, :], bc(gs[:, 2, :]), ALU.mult))
                for j in range(NTILE):
                    step(v.max(g8[:, j, :], gl[:, j, :]))
                for j in range(NTILE):
                    step(v.max_index(gi[:, j, :], g8[:, j, :], gl[:, j, :]))
                step(v.tensor_copy(gf[:, :, :], gi[:, :, 0:2]))
                iot = cst[:, C_IOTA:C_IOTA + 8].unsqueeze(1).broadcast_to([128, NTILE, E])
                step(v.tensor_tensor(g1[:, :, :], iot, bc(gf[:, :, 0]), ALU.is_equal))
                step(v.tensor_tensor(g2[:, :, :], iot, bc(gf[:, :, 1]), ALU.is_equal))
                step(v.tensor_tensor(g1[:, :, :], g1[:, :, :], g2[:, :, :], ALU.add))
                step(v.tensor_tensor(g1[:, :, :], g1[:, :, :], gl[:, :, :], ALU.mult))
                step(v.tensor_tensor(gs[:, 0, :], g8[:, :, 0], g8[:, :, 1], ALU.add))
                step(v.tensor_scalar(gs[:, 0, :], gs[:, 0, :], 1e-9, None, ALU.add))
                step(v.reciprocal(gs[:, 1, :], gs[:, 0, :]))
                step(v.tensor_tensor(g1[:, :, :], g1[:, :, :], bc(gs[:, 1, :]), ALU.mult))
                v.tensor_reduce(gs[:, 3, :], g1[:, :, :], AX.X, ALU.add).then_inc(f_cm, 1)
                for nb in range(4):
                    v.wait_ge(f_ct, nb + 1)
                    v.tensor_copy(cT[:, 512 * nb:512 * nb + 512], B[nb][0:E, :]).then_inc(f_cte, 1)
                v.wait_ge(f_cm, 1)
                for j in range(NTILE):
                    v.scalar_tensor_tensor(out=xb[:, j, :], in0=bcc[:, 2, :], scalar=gs[:, 3, j:j + 1],
                                           in1=xb[:, j, :], op0=ALU.mult, op1=ALU.add).then_inc(f_b3, 1)
                def acc(n):
                    e, m, nb = unit(n)
                    v.wait_ge(f_vg, n + 1)
                    s = slice(512 * nb, 512 * nb + 512)
                    v.tensor_tensor(G[:, m, s], G[:, m, s], vg[:, n % 2, :], ALU.add).then_inc(f_ac, 1)

                for n in range(NU):
                    e, m, nb = unit(n)
                    s = slice(512 * nb, 512 * nb + 512)
                    v.wait_ge(f_ug, n + 1)
                    if n >= 18:
                        v.wait_ge(f_ac, n - 17)
                    o = G[:, m, s] if e == 0 else vg[:, n % 2, :]
                    v.scalar_tensor_tensor(out=o, in0=B[2 * (n % 4)][:, :], scalar=b1c[:, e, m:m + 1],
                                           in1=ug[:, n % 2, :], op0=ALU.add, op1=ALU.mult).then_inc(f_vg, 1)
                    if n > 16:
                        acc(n - 1)
                acc(NU - 1)
                v.wait_ge(f_b3, NTILE)
                for n in range(8):
                    v.wait_ge(f_o, n + 1)
                    if n >= 2:
                        v.wait_ge(f_out[n % 2], 32 * (n // 2))
                    v.tensor_tensor(fo[:, n % 2, :].rearrange("p (a c) -> p a c", a=2),
                                    B[n][:, :].rearrange("p (a c) -> p a c", a=2), xb[:, 2 * n:2 * n + 2, :], ALU.add
                                    ).then_inc(f_fo, 1)

            @block.scalar
            def _(a):
                for j in range(NTILE):
                    a.wait_ge(f_t, j + 1)
                    a.activation(xh[:, :, 128 * j:128 * j + 128],
                                 B[j % 4][:, 0:C].rearrange("p (k n) -> p k n", k=2), ACT.Copy).then_inc(f_hi, 1)
                a.wait_ge(s_w2, 96)
                a.wait_ge(f_ge, 1)
                a.activation(gl[:, :, :], gl[:, :, :], ACT.Exp).then_inc(f_ge, 1)
                for n in range(NU):
                    e, m, nb = unit(n)
                    a.wait_ge(f_h, n + 1)
                    if n >= 2:
                        a.wait_ge(f_ug, n - 1)
                    a.activation(sg[:, n % 2, :], B[2 * (n % 4) + 1][:, :], ACT.Sigmoid, bias=b1c[:, e, 4 + m:5 + m]
                                 ).then_inc(f_sg, 1)

            @block.tensor
            def _(t):
                t.wait_ge(u_x3, NTILE)
                for j in range(NTILE):
                    t.wait_ge(f_xn, j + 1)
                    if j >= 4:
                        t.wait_ge(f_lo, j - 3)
                    for k in range(2):
                        mm = t.transpose(B[j % 4][:, 128 * k:128 * k + 128], yn[:, j % 2, 128 * k:128 * k + 128], ident)
                    mm.then_inc(f_t, 1)
                t.wait_ge(f_wg, 2)
                for j in range(NTILE):
                    t.wait_ge(f_lo, j + 1)
                    e = 0
                    for k in range(2):
                        s = slice(128 * j, 128 * j + 128)
                        for x, w in ((xh, 0), (xh, 1), (xl, 0)):
                            mm = t.matmul(B[4][:, E * j:E * j + E], x[:, k, s], WgR[:, w, k, :],
                                          start=(e == 0), stop=(e == 5))
                            e += 1
                    mm.then_inc(f_g, 1)
                t.wait_ge(f_cm, 1)
                for nb in range(4):
                    for j in range(4):
                        mm = t.transpose(B[nb][0:E, 128 * j:128 * j + 128], g1[:, 4 * nb + j, :], ident)
                    mm.then_inc(f_ct, 1)
                t.wait_ge(f_cte, 4)
                for n in range(NU):
                    e, m, nb = unit(n)
                    if n % 16 == 0:
                        t.wait_ge(f_wl, e + 1)
                    if n >= 4:
                        t.wait_ge(f_vg, n - 3)
                    s = slice(512 * nb, 512 * nb + 512)
                    for h in (1, 0):
                        q = 0
                        for k in range(2):
                            c = slice(HF * h + 128 * m, HF * h + 128 * m + 128)
                            for w, x in ((w1h, xh), (w1l, xh), (w1h, xl)):
                                mm = t.matmul(B[2 * (n % 4) + h][:, :], w[:, e % 2, k, c], x[:, k, s],
                                              start=(q == 0), stop=(q == 5))
                                q += 1
                    mm.then_inc(f_h, 1)
                for n in range(8):
                    t.wait_ge(f_ac, NU - 16 if n else NU - 16)
                    for jj in range(2):
                        j = 2 * n + jj
                        for m in range(4):
                            mm = t.matmul(B[n][:, C * jj:C * jj + C], G[:, m, 128 * j:128 * j + 128], WoT[:, m, :],
                                          start=(m == 0), stop=(m == 3))
                    mm.then_inc(f_o, 1)
        ph3.close()


def bcast(ap, n, row=False):
    if row:
        return bass.AP(tensor=ap.tensor, offset=ap.offset, ap=[[0, n]] + list(ap.ap[1:]))
    return bass.AP(tensor=ap.tensor, offset=ap.offset, ap=[[0, n]] + list(ap.ap))


def kernel(**inputs):
    import concourse.bacc as bacc
    from concourse.bass_utils import run_bass_kernel_spmd

    nc = bacc.Bacc("TRN2", target_bir_lowering=False, num_devices=1)
    a = {k: np.asarray(v) for k, v in inputs.items()}
    ctx = a["ctx_768"]
    col = lambda v: v.reshape(-1, 128).T
    arrays = {
        "x": a["x"],
        "cst": constants(),
        "Wq": a["L0_xattn_Wq"],
        "Wk": a["L0_xattn_Wk"],
        "Wv": a["L0_xattn_Wv"],
        "xWo": a["L0_xattn_Wo"],
        "ctxT": np.concatenate([ctx, ctx[:, -1:]], axis=1).transpose(0, 2, 1),
        "c256": ctx[:, NK - 1, :].T,
        "bcol": np.concatenate([col(a["L0_xattn_bq"]), col(a["L0_xattn_bk"]), col(a["L0_xattn_bv"]),
                                col(a["L0_attn_proj"])], axis=1),
        "brow": np.stack([a["L0_xattn_bo"], a["L0_attn_concat_b"], a["L0_ffn_bo"]]),
        "aW": a["L0_attn_W"],
        "cwT": a["L0_attn_concat_w"].T.reshape(2, 256, 256).transpose(1, 0, 2),
        "WgT": a["L0_ffn_Wg"].T,
        "W1T": a["L0_ffn_W1"].transpose(0, 2, 1),
        "b1c": a["L0_ffn_b1"].reshape(E, 8, 128).transpose(2, 0, 1),
        "fWoT": a["L0_ffn_Wo"].T,
    }
    arrays = {k: np.ascontiguousarray(v) for k, v in arrays.items()}
    d = {k: nc.dram_tensor("in_" + k, v.shape, F32, kind="ExternalInput").ap() for k, v in arrays.items()}
    out = nc.dram_tensor("out", [T, NQ, C], F32, kind="ExternalOutput").ap()
    vx_d = nc.dram_tensor("vx_d", [4, T, 65], F32, kind="Internal").ap()
    cb_d = nc.dram_tensor("cb_d", [E, NT], F32, kind="Internal").ap()
    build(nc, d, out, vx_d, cb_d)
    r = run_bass_kernel_spmd(nc, [{"in_" + k: v for k, v in arrays.items()}], core_ids=[0])
    return r.results[0]["out"]
```

```python
from contextlib import ExitStack

import numpy as np
import concourse.bass as bass
from concourse import mybir

ALU = mybir.AluOpType
ACT = mybir.ActivationFunctionType
AX = mybir.AxisListType
F32 = mybir.dt.float32
F32R = mybir.dt.float32r
F16 = mybir.dt.float16
I32 = mybir.dt.int32

T, NQ, C, CK, NK = 64, 32, 256, 192, 257
NKP = 258
NT = T * NQ
NTILE = NT // 128
CLAMP = 10000.0
EPS = 1e-5
NEG = float(np.finfo(np.float32).min)
E, HF = 8, 512
NPAIR = T // 2
CH = 4
NS = 39
BASE = 16512
KB = 1024

C_ID = 0
C_GM = 128
C_OM = 132
C_R = 136
C_MN = 168
C_M01 = 232
C_IOTA = 234
C_U = 242
C_I128 = 370
C_ONE = 498
C_PE = 626
C_TH = 627
C_TOK = 643
C_END = 659


def constants():
    p = np.arange(128)
    c = np.zeros((128, C_END), np.float32)
    c[:, C_ID:C_ID + 128] = np.eye(128)
    c[:, C_GM:C_GM + 4] = (p[:, None] // 16) % 4 == np.arange(4)
    c[:, C_OM:C_OM + 4] = p[:, None] // 32 == np.arange(4)
    c[:, C_R:C_R + 32] = p[:, None] % 32 == np.arange(32)
    c[:, C_MN:C_MN + 64] = np.where(np.arange(64) < (p % 64)[:, None], 0.0, NEG)
    c[:, C_M01] = (p % 64) >= 2
    c[:, C_M01 + 1] = (p % 64) < 2
    c[:, C_IOTA:C_IOTA + 8] = np.arange(8)
    c[:, C_U:C_U + 128] = p[:, None] < np.arange(128)
    c[:, C_I128:C_I128 + 128] = np.arange(128)
    c[:, C_ONE:C_ONE + 128] = 1.0
    c[:, C_PE] = np.where(p % 32 < 8, p % 32, -1)
    c[:, C_TH:C_TH + 16] = 128.0 * np.arange(16)
    c[:, C_TOK:C_TOK + 16] = 128 * np.arange(16) + p[:, None]
    return c


def build(nc, d, out, vx_d, y_d, g_d):
    ctx = ExitStack()
    with ctx:
        def sem(name):
            return ctx.enter_context(nc.semaphore(name))

        B = [ctx.enter_context(nc.psum_tensor(f"bank{i}", [128, 512], F32)) for i in range(8)]

        top = [0]

        def area(start, end):
            top[0] = [BASE + int(start * KB), BASE + int(end * KB)]

        def put(name, shape, dt=F32):
            size = 2 if dt == F16 else 4
            for n in shape[1:]:
                size *= n
            size = -(-size // 32) * 32
            at, end = top[0]
            assert at + size <= end, (name, at + size - end)
            top[0][0] += size
            return nc.alloc_sbuf_tensor_at(name, shape, dt, offset=at)

        area(0, 27)
        cst = put("cst", [128, C_END])
        xb = put("xb", [128, NTILE, C])
        bcol = put("bcol", [128, 8])
        bcc = put("bcc", [128, 3, C])
        st = put("st", [128, NTILE, 6])
        mv = put("mv", [128, NTILE, 2])
        rs = put("rs", [128, NTILE])
        epw = put("epw", [128, 2, NTILE])
        WgT = put("WgT", [128, 2, E])
        WgR = put("WgR", [128, 2, 2, E], F32R)
        gl = put("gl", [128, NTILE, E])
        g8 = put("g8", [128, NTILE, E])
        gi = put("gi", [128, NTILE, E], mybir.dt.uint32)
        oh = put("oh", [128, 2, NTILE, E])
        Mk = put("Mk", [128, NTILE, E])
        cum = put("cum", [128, NTILE + 1, E])
        gs = put("gs", [128, 4, NTILE])
        cmb = put("cmb", [128, 2, NTILE])
        area(27, 155)
        W1 = put("W1", [128, E * 2 * 2 * 1024], F32R)
        area(107, 123)
        OT = put("OT", [128, 2, NT])
        area(123, 139)
        Wo = put("Wo", [128, 2, C])
        WaR = put("WaR", [128, 2, 2, C], F32R)
        WcR = put("WcR", [128, 2, 2, 2 * C], F32R)

        ident = cst[:, C_ID:C_ID + 128]

        s_c = sem("s_c")
        s_w = sem("s_w")
        s_w2 = sem("s_w2")
        s_x = [sem(f"s_x{i}") for i in range(4)]
        s_xb = sem("s_xb")
        s_st = sem("s_st")
        s_mv = sem("s_mv")
        s_ep = sem("s_ep")
        s_rs = sem("s_rs")
        s_xn = sem("s_xn")
        s_t0 = sem("s_t0")
        s_t0e = sem("s_t0e")
        s_q = sem("s_q")
        s_qe = sem("s_qe")
        s_bd = sem("s_bd")
        s_wh = sem("s_wh")
        s_wl = sem("s_wl")
        s_cx = [sem("s_cx0"), sem("s_cx1")]
        s_hi = sem("s_hi")
        s_lo = sem("s_lo")
        s_vx = sem("s_vx")
        s_vxe = sem("s_vxe")
        s_vz = sem("s_vz")
        s_vd = sem("s_vd")
        s_vb = [sem("s_vb0"), sem("s_vb1")]
        s_v1 = sem("s_v1")
        s_base = sem("s_base")
        s_basee = sem("s_basee")
        s_xbb = sem("s_xbb")
        s_ws = sem("s_ws")
        s_wsd = sem("s_wsd")
        s_k = sem("s_k")
        s_v = sem("s_v")
        s_s = sem("s_s")
        s_t = sem("s_t")
        s_tt = sem("s_tt")
        s_o = sem("s_o")
        s_ot = sem("s_ot")
        s_cl = sem("s_cl")
        s_nm = sem("s_nm")
        s_pte = sem("s_pte")
        s_rc = sem("s_rc")
        s_rm = sem("s_rm")
        s_m = sem("s_m")
        s_ke = sem("s_ke")
        s_pe = sem("s_pe")
        s_ve = sem("s_ve")
        s_tte = sem("s_tte")
        s_ex = sem("s_ex")
        s_pt = sem("s_pt")
        s_ote = sem("s_ote")

        area(27, 107)
        qbd = put("qbd", [128, 2, T, 4, NQ])
        wA = put("wA", [128, 2, 2 * C])
        wH = put("wH", [128, 2, 2 * C], F32R)
        wL = put("wL", [128, 2, 2 * C], F32R)
        Wq = put("Wq", [128, 2, C])
        base = put("base", [128, C])
        c256 = put("c256", [128, 2, T])
        area(22.5, 27)
        lA = put("lA", [128, 2, 2, NKP], F32R)
        area(137, 139)
        Mb = put("Mb", [128, 2, C])
        area(139, 207.75)
        cx = put("cx", [128, 2, 2, 2, NKP])
        hA = put("hA", [128, 2, 2, 2, NKP], F32R)
        vx = put("vx", [T, 4, 65])
        Vs = put("Vs", [128, 3, 2, 4, 65])
        Vbd = put("Vbd", [4, 2, CH, 260])
        KT = put("KT", [128, 2, 2, NKP])
        Sc = put("Sc", [128, 2, 4, NK])
        xnT = put("xnT", [128, 2, 512])
        qT = put("qT", [128, 512])
        Pm = put("Pm", [128, 2, 4, NK])
        PT = put("PT", [128, 2, 2, 4, 128])
        mx = put("mx", [128, 2, 4])
        nm = put("nm", [128, 2, 4])
        Pt = put("Pt", [128, 2, 4])
        PTt = put("PTt", [4, 2, 128])
        rc = put("rc", [128, 2, 4])
        rm = put("rm", [128, 2, 4, 4])

        xa = xb
        cf = cst
        gm = cf[:, C_GM:C_GM + 4]
        om = cf[:, C_OM:C_OM + 4]

        pP = [B[2], B[3]]
        pT = [B[4], B[5]]
        pO = [B[6], B[7]]
        NST = 16

        with nc.Block() as block:

            @block.sync
            def _(sp):
                for g in range(4):
                    sp.dma_start(xa[:, 4 * g:4 * g + 4, :],
                                 d["x"].rearrange("(n a) b c -> (a b) n c", a=4)[:, 4 * g:4 * g + 4, :]
                                 ).then_inc(s_x[g], 16)
                sp.dma_start(cst[:, :], d["cst"]).then_inc(s_c, 16)
                sp.dma_start(Wq[:, :, :], d["Wq"].rearrange("(k p) n -> p k n", p=128)).then_inc(s_c, 16)
                sp.dma_start(bcol[:, :], d["bcol"]).then_inc(s_c, 16)
                for i, w in enumerate(("Wk", "Wv")):
                    o = i * C
                    sp.dma_start(wA[:, 0, o:o + C], d[w][0:128, :]).then_inc(s_w, 16)
                    sp.dma_start(wA[0:64, 1, o:o + C], d[w][128:192, :]).then_inc(s_w, 16)
                    sp.dma_start(wA[64:128, 1, o:o + C], d[w][128:192, :]).then_inc(s_w, 16)
                sp.dma_start(c256[:, 0, :], d["c256"][0:128, :]).then_inc(s_w, 16)
                sp.dma_start(c256[0:64, 1, :], d["c256"][128:192, :]).then_inc(s_w, 16)
                sp.dma_start(Wo[:, :, :], d["xWo"].rearrange("(k p) n -> p k n", p=128)).then_inc(s_w, 16)
                sp.dma_start(bcc[:, :, :], bcast(d["brow"], 128)).then_inc(s_w, 16)

                def load_ctx(j):
                    if j >= 2:
                        sp.wait_ge(s_lo, 2 * (j - 1))
                    s = s_cx[j % 2]
                    src = d["ctxT"]
                    sp.dma_start(cx[:, j % 2, 0, :, :], src[2 * j:2 * j + 2, 0:128, :].rearrange("b p n -> p b n")).then_inc(s, 16)
                    for h in range(2):
                        sp.dma_start(cx[64 * h:64 * h + 64, j % 2, 1, :, :],
                                     src[2 * j:2 * j + 2, 128:192, :].rearrange("b p n -> p b n")).then_inc(s, 16)

                load_ctx(0)
                load_ctx(1)
                sp.wait_ge(s_vxe, 1)
                sp.wait_ge(s_v1, 2)
                sp.dma_start(vx_d.rearrange("g t c -> t g c"), vx[:, :, :]).then_inc(s_vd, 16)
                sp.wait_ge(s_vd, 16)
                sp.wait_ge(s_vz, 1)

                def load_vb(c):
                    if c >= 2:
                        sp.wait_ge(s_o, CH * (c - 1))
                    for g in range(4):
                        sp.dma_start(Vbd[g:g + 1, c % 2, :, 65 * g:65 * g + 65],
                                     vx_d[g:g + 1, CH * c:CH * c + CH, :]).then_inc(s_vb[c % 2], 16)

                load_vb(0)
                load_vb(1)
                xbd = d["x"].rearrange("t (n b) c -> b t n c", b=2)
                for j in range(2, NPAIR):
                    load_ctx(j)
                    if (j + 1) % 2 == 0 and 2 <= (j + 1) // 2 < T // CH:
                        load_vb((j + 1) // 2)
                    if j == 3:
                        sp.wait_ge(s_wl, 1)
                        sp.dma_start(wA[:, 0, :].rearrange("p (k n) -> p k n", k=2),
                                     d["aW"].rearrange("(k p) n -> p k n", p=128)).then_inc(s_w2, 16)
                        sp.dma_start(wA[:, 1, :], d["cwT"][0:128].rearrange("p k n -> p (k n)")).then_inc(s_w2, 16)
                        sp.dma_start(WgT[:, :, :], d["WgT"].rearrange("(k p) n -> p k n", p=128)).then_inc(s_w2, 16)
                    if j == 10:
                        sp.wait_ge(s_wsd, 4)
                        sp.dma_start(wA[:, 0, :], d["cwT"][128:256].rearrange("p k n -> p (k n)")).then_inc(s_ws, 16)
                    if j == 22:
                        sp.wait_ge(s_t0, 8)
                        sp.dma_start(xb[0:64, :, :], xbd[0]).then_inc(s_xb, 16)
                        sp.dma_start(xb[64:128, :, :], xbd[1]).then_inc(s_xb, 16)

            @block.gpsimd
            def _(g):
                g.memset(epw[:, 0, :], EPS).then_inc(s_ep, 1)
                g.memset(epw[:, 1, :], -0.5).then_inc(s_ep, 1)
                g.memset(Vbd[:, :, :, :], 0.0).then_inc(s_vz, 1)
                g.memset(Vs[:, :, :, :, 64:65], 1.0).then_inc(s_v1, 1)
                g.memset(vx[:, :, 64:65], 1.0).then_inc(s_v1, 1)

                def rstd(c):
                    k = slice(4 * c, 4 * c + 4)
                    g.wait_ge(s_mv, 4 * c + 4)
                    if c == 0:
                        g.wait_ge(s_ep, 2)
                    g.tensor_tensor(rs[:, k], mv[:, k, 1], epw[:, 0, k], ALU.add).then_inc(s_ep, 1)
                    g.wait_ge(s_ep, 3 + c)
                    g.tensor_tensor(rs[:, k], rs[:, k], epw[:, 1, k], ALU.pow).then_inc(s_rs, 1)

                def wsplit(n):
                    if n < 2:
                        g.wait_ge(s_w2, 48)
                    else:
                        g.wait_ge(s_ws, 16)
                    src = wA[:, n % 2, :]
                    hi, lo = ((WaR[:, w, :, :].rearrange("p k n -> p (k n)") for w in range(2)) if n == 0 else
                              (WcR[:, w, n - 1, :] for w in range(2)))
                    g.tensor_scalar(hi, src, 1.0, None, ALU.mult).then_inc(s_wsd, 1)
                    g.wait_ge(s_wsd, 2 * n + 1)
                    g.tensor_tensor(lo, src, hi.bitcast(F32), ALU.subtract).then_inc(s_wsd, 1)

                rstd(0)
                def split(j):
                    g.wait_ge(s_cx[j % 2], 48 * (j // 2 + 1))
                    if j >= 2:
                        g.wait_ge(s_v, 2 * (j - 1))
                    b = j % 2
                    g.tensor_scalar(hA[:, b, :, :, :].rearrange("p k b n -> p (k b n)"),
                                    cx[:, b, :, :, :].rearrange("p k b n -> p (k b n)"), 1.0, None, ALU.mult
                                    ).then_inc(s_hi, 1)
                    g.wait_ge(s_hi, j + 1)
                    g.tensor_tensor(lA[:, b, :, :], cx[:, b, 0, :, :], hA[:, b, 0, :, :].bitcast(F32), ALU.subtract
                                    ).then_inc(s_lo, 1)
                    g.wait_ge(s_lo, 2 * j + 1)
                    g.tensor_tensor(hA[64:128, b, 1, :, :], cx[64:128, b, 1, :, :],
                                    hA[64:128, b, 1, :, :].bitcast(F32), ALU.subtract).then_inc(s_lo, 1)
                    g.wait_ge(s_lo, 2 * j + 2)

                split(0)
                split(1)
                for i in range(T):
                    g.wait_ge(s_ex, 4 * i + 4)
                    g.tensor_scalar(Pt[:, i % 2, :], Pm[:, i % 2, :, NK - 1], 1.0, None, ALU.min).then_inc(s_pt, 1)
                    if i % 16 == 2 and i < 48:
                        rstd(i // 16 + 1)
                    if i in (10, 12, 26):
                        wsplit((10, 12, 26).index(i))
                    if i == 47:
                        g.wait_ge(s_xb, 32)
                        g.wait_ge(s_basee, 1)
                    if 47 <= i < 47 + NTILE:
                        n = i - 47
                        g.tensor_tensor(xb[:, n, :], xb[:, n, :], base[:, :], ALU.add).then_inc(s_xbb, 1)
                    if i % 2 == 1 and (i + 3) // 2 < NPAIR:
                        split((i + 3) // 2)

            @block.vector
            def _(v):
                def stats(c):
                    v.wait_ge(s_x[c], 16)
                    for n in range(4 * c, 4 * c + 4):
                        v.bn_stats(st[:, n, :], xa[:, n, :]).then_inc(s_st, 1)
                    for n in range(4 * c, 4 * c + 4):
                        v.wait_ge(s_st, n + 1)
                        v.bn_aggr(mv[:, n, :], st[:, n, :]).then_inc(s_mv, 1)

                def xnorm(c):
                    v.wait_ge(s_mv, 4 * c + 4)
                    v.wait_ge(s_rs, c + 1)
                    for n in range(4 * c, 4 * c + 4):
                        v.tensor_scalar(xa[:, n, :], xa[:, n, :], mv[:, n, 0:1], rs[:, n:n + 1],
                                        ALU.subtract, ALU.mult).then_inc(s_xn, 1)

                def qchunk(c):
                    for m in range(2):
                        n = 2 * c + m
                        v.wait_ge(s_q, n + 1)
                        v.wait_ge(s_bd, 4 * n)
                        v.tensor_scalar(qT[:, :], pT[m][:, :], bcol[:, m:m + 1], 0.25, ALU.add, ALU.mult
                                        ).then_inc(s_qe, 1)
                        v.wait_ge(s_qe, n + 1)
                        for h in range(4):
                            v.tensor_scalar(qbd[:, m, 16 * c:16 * c + 16, h, :],
                                            qT[:, :].rearrange("p (t b) -> p t b", b=NQ),
                                            gm[:, h:h + 1], None, ALU.mult).then_inc(s_bd, 1)

                stats(0)
                v.wait_ge(s_w, 16 * 10)
                v.wait_ge(s_c, 48)
                v.tensor_copy(wH[:, :, :], wA[:, :, :]).then_inc(s_wh, 1)
                v.wait_ge(s_wh, 1)
                v.tensor_tensor(wL[:, :, :], wA[:, :, :], wH[:, :, :].bitcast(F32), ALU.subtract).then_inc(s_wl, 1)
                xnorm(0)
                v.wait_ge(s_vx, 1)
                v.tensor_copy(vx[:, :, 0:64], B[6][0:T, 0:C].rearrange("p (g c) -> p g c", g=4)).then_inc(s_vxe, 1)
                v.wait_ge(s_base, 1)
                v.tensor_tensor(base[:, :], B[7][:, 0:C], bcc[:, 0, :], ALU.add).then_inc(s_basee, 1)
                qchunk(0)

                def clip(i, g):
                    v.wait_ge(s_s, 4 * i + g + 1)
                    v.tensor_scalar(Sc[:, i % 2, g, :], B[g % 2][:, 0:NK], -CLAMP, -CLAMP, ALU.max, ALU.max,
                                    accum_out=mx[:, i % 2, g:g + 1]).then_inc(s_cl, 1)

                def negmax(i, p):
                    v.wait_ge(s_cl, 4 * i + 2 * p + 2)
                    v.tensor_scalar(nm[:, i % 2, 2 * p:2 * p + 2], mx[:, i % 2, 2 * p:2 * p + 2], CLAMP, -1.0,
                                    ALU.min, ALU.mult).then_inc(s_nm, 1)

                def ptevac(i, p):
                    v.wait_ge(s_t, 2 * i + p + 1)
                    v.tensor_scalar(PT[:, i % 2, p, :, :].rearrange("p a b -> p (a b)"), pT[p][:, :], 1.0, None,
                                    ALU.min).then_inc(s_pte, 1)

                def recip(i):
                    v.wait_ge(s_o, i + 1)
                    v.reciprocal(rc[:, i % 2, :], pO[i % 2][:, 0:260].rearrange("p (g c) -> p g c", g=4)[:, :, 64]
                                 ).then_inc(s_rc, 1)

                def rmask(i):
                    v.wait_ge(s_rc, i + 1)
                    v.tensor_tensor(rm[:, i % 2, :, :], rc[:, i % 2, :].unsqueeze(2).broadcast_to([128, 4, 4]),
                                    om.unsqueeze(1).broadcast_to([128, 4, 4]), ALU.mult).then_inc(s_rm, 1)

                def norm(i):
                    v.wait_ge(s_rm, i + 1)
                    v.tensor_tensor(Mb[:, i % 2, :].rearrange("p (g h c) -> p g h c", g=4, h=4),
                                    pO[i % 2][:, 0:260].rearrange("p (g c) -> p g c", g=4)[:, :, 0:64]
                                    .rearrange("p g (h c) -> p g h c", h=4),
                                    rm[:, i % 2, :, :].unsqueeze(3).broadcast_to([128, 4, 4, 16]), ALU.mult
                                    ).then_inc(s_m, 1)

                for i in range(T + 2):
                    if i < T:
                        clip(i, 0)
                    if i >= 2:
                        recip(i - 2)
                    if i < T:
                        clip(i, 1)
                    if i >= 2:
                        rmask(i - 2)
                    if i < T:
                        negmax(i, 0)
                    if 1 <= i <= T:
                        ptevac(i - 1, 0)
                    if i >= 2:
                        norm(i - 2)
                    if i < T:
                        clip(i, 2)
                        clip(i, 3)
                    if 1 <= i <= T:
                        ptevac(i - 1, 1)
                    if i < T:
                        negmax(i, 1)
                    if i < 48 and i % 16 == 2:
                        stats(i // 16 + 1)
                    if i < 48 and i % 16 == 4:
                        xnorm(i // 16 + 1)
                    if i < 48 and i % 16 == 6:
                        qchunk(i // 16 + 1)

            @block.scalar
            def _(a):
                def qchunk(c):
                    for k in range(2):
                        a.wait_ge(s_t0, 2 * c + k + 1)
                        if c:
                            a.wait_ge(s_q, 2 * c)
                        a.activation(xnT[:, k, :], pT[k][:, :], ACT.Copy).then_inc(s_t0e, 1)

                qchunk(0)

                def kevac(i, m):
                    a.wait_ge(s_k, 2 * i + m + 1)
                    n = 3 * i + m
                    if m == 1 and i >= 2:
                        a.wait_ge(s_tt, i - 1)
                    ins = a.activation(KT[:, i % 2, m, :], pP[n % 2][:, 0:NKP], ACT.Identity,
                                       bias=bcol[:, 2 + m:3 + m])
                    ins.then_inc(s_ke, 1)

                def vevac(i):
                    a.wait_ge(s_v, i + 1)
                    n = 3 * i + 2
                    if i == 0:
                        a.wait_ge(s_v1, 2)
                    a.activation(Vs[:, i % 3, :, :, 0:64],
                                 pP[n % 2][:, :].rearrange("p (c g e) -> p c g e", c=2, g=4), ACT.Copy
                                 ).then_inc(s_ve, 1)

                def tevac(i):
                    a.wait_ge(s_tt, i + 1)
                    n = 3 * (i + 2) + 1
                    a.activation(PTt[:, i % 2, :], pP[n % 2][0:4, 384:512], ACT.Copy).then_inc(s_tte, 1)

                def exps(i, g):
                    a.wait_ge(s_nm, 2 * i + g // 2 + 1)
                    a.activation(Pm[:, i % 2, g, :], Sc[:, i % 2, g, :], ACT.Exp, bias=nm[:, i % 2, g:g + 1]
                                 ).then_inc(s_ex, 1)

                def otevac(i):
                    a.wait_ge(s_ot, i + 1)
                    a.activation(OT[:, :, :].rearrange("p m (b t) -> p m b t", t=T)[:, :, :, i],
                                 pO[i % 2][:, 320:384].rearrange("p (m q) -> p m q", m=2), ACT.Copy
                                 ).then_inc(s_ote, 1)

                for i in range(-1, T + 2):
                    if i + 1 < T:
                        kevac(i + 1, 0)
                    if 0 <= i < T:
                        exps(i, 0)
                        exps(i, 1)
                    if i + 1 < T:
                        kevac(i + 1, 1)
                    if 1 <= i <= T:
                        tevac(i - 1)
                    if 0 <= i < T:
                        exps(i, 2)
                        exps(i, 3)
                    if i + 1 < T:
                        vevac(i + 1)
                    if i >= 2:
                        otevac(i - 2)
                    if i < 48 and i % 16 == 6:
                        qchunk(i // 16 + 1)

            @block.tensor
            def _(t):
                t.wait_ge(s_c, 48)
                t.wait_ge(s_w, 16 * 10)
                for k in range(2):
                    K = 128 - 64 * k
                    mm = t.matmul(B[6][0:T, 0:C], c256[0:K, k, :], wA[0:K, k, C:2 * C], start=(k == 0), stop=(k == 1))
                mm.then_inc(s_vx, 1)
                for k in range(2):
                    mm = t.matmul(B[7][:, 0:C], bcol[:, 4 + k:5 + k].broadcast_to([128, 128]), Wo[:, k, :],
                                  start=(k == 0), stop=(k == 1))
                mm.then_inc(s_base, 1)
                def qchunk(c):
                    for k in range(2):
                        for j in range(4 * c, 4 * c + 4):
                            t.wait_ge(s_xn, j + 1)
                            mm = t.transpose(pT[k][:, 128 * (j % 4):128 * (j % 4) + 128], xa[:, j, 128 * k:128 * k + 128],
                                             ident)
                        mm.then_inc(s_t0, 1)
                    t.wait_ge(s_t0e, 2 * c + 2)
                    for m in range(2):
                        for k in range(2):
                            mm = t.matmul(pT[m][:, :], Wq[:, k, 128 * m:128 * m + 128], xnT[:, k, :],
                                          start=(k == 0), stop=(k == 1))
                        mm.then_inc(s_q, 1)

                def terms(b, bi):
                    hi0, hi1 = hA[:, b, 0, bi, :], hA[:, b, 1, bi, :]
                    lo0 = lA[:, b, bi, :]
                    return [(hi0, wH[:, 0, :]), (hi0, wL[:, 0, :]), (lo0, wH[:, 0, :]),
                            (hi1, wH[:, 1, :]), (hi1, wL[:, 1, :])]

                def wait_pp(n):
                    if n < 2:
                        return
                    i, r = (n - 2) // 3, (n - 2) % 3
                    if r == 2:
                        t.wait_ge(s_ve, i + 1)
                    else:
                        t.wait_ge(s_ke, 2 * i + r + 1)
                        if r == 1 and i >= 2:
                            t.wait_ge(s_tte, i - 1)

                def kproj(i, m):
                    n = 3 * i + m
                    wait_pp(n)
                    t.wait_ge(s_lo, 2 * (i // 2 + 1))
                    for e, (c, w) in enumerate(terms((i // 2) % 2, i % 2)):
                        mm = t.matmul(pP[n % 2][:, 0:NKP], w[:, 128 * m:128 * m + 128], c, start=(e == 0), stop=(e == 4))
                    mm.then_inc(s_k, 1)

                def vproj(i):
                    n = 3 * i + 2
                    wait_pp(n)
                    for c in range(2):
                        for e, (x, w) in enumerate(terms((i // 2) % 2, i % 2)):
                            mm = t.matmul(pP[n % 2][:, C * c:C * c + C], x[:, 128 * c:128 * c + 128], w[:, C:2 * C],
                                          start=(e == 0), stop=(e == 4))
                    mm.then_inc(s_v, 1)

                def scores(i, p):
                    if p == 0:
                        t.wait_ge(s_ke, 2 * i + 2)
                    for gg in range(2):
                        if 4 * i + 2 * p >= 2:
                            t.wait_ge(s_cl, 4 * i + 2 * p - 1 + gg)
                        r = slice(64 * gg, 64 * gg + 64)
                        t.matmul(B[gg][:, 0:NK], qbd[r, p, i, :, :], KT[r, i % 2, p, 0:NK], start=True, stop=True
                                 ).then_inc(s_s, 1)

                def transp(i, p):
                    t.wait_ge(s_ex, 4 * i + 2 * p + 2)
                    if i >= 1:
                        t.wait_ge(s_pte, 2 * (i - 1) + p + 1)
                    if i % 16 == 6 and i < 48:
                        t.wait_ge(s_qe, 2 * (i // 16 + 1) + 2)
                    if i == 0:
                        t.wait_ge(s_qe, 2)
                    for gg in range(2):
                        for c in range(2):
                            o = 256 * gg + 128 * c
                            mm = t.transpose(pT[p][:, o:o + 128], Pm[:, i % 2, 2 * p + gg, 128 * c:128 * c + 128], ident)
                    mm.then_inc(s_t, 1)

                def tail(i):
                    t.wait_ge(s_pt, i + 1)
                    n = 3 * (i + 2) + 1
                    if i + 2 >= T:
                        t.wait_ge(s_ve, T)
                        t.wait_ge(s_tte, i)
                    t.transpose(pP[n % 2][0:4, 384:512], Pt[:, i % 2, :], ident).then_inc(s_tt, 1)

                def pv(i):
                    if i >= 2:
                        t.wait_ge(s_ote, i - 1)
                    t.wait_ge(s_ve, i + 1)
                    first = True
                    for p in range(2):
                        t.wait_ge(s_pte, 2 * i + p + 1)
                        for gg in range(2):
                            g = 2 * p + gg
                            for c in range(2):
                                t.matmul(pO[i % 2][:, 65 * g:65 * g + 65], PT[:, i % 2, p, 2 * gg + c, :],
                                         Vs[:, i % 3, c, g, :], start=first, stop=False, skip_group_check=True)
                                first = False
                    t.wait_ge(s_tte, i + 1)
                    c = i // CH
                    t.wait_ge(s_vb[c % 2], 64 * (c // 2 + 1))
                    t.matmul(pO[i % 2][:, 0:260], PTt[:, i % 2, :], Vbd[:, c % 2, i % CH, :], start=False, stop=True,
                             skip_group_check=True).then_inc(s_o, 1)

                def gather(i):
                    t.wait_ge(s_m, i + 1)
                    for m in range(2):
                        mm = t.matmul(pO[i % 2][:, 320 + NQ * m:320 + NQ * m + NQ], Mb[:, i % 2, 128 * m:128 * m + 128],
                                      cst[:, C_R:C_R + 32], start=True, stop=True)
                    mm.then_inc(s_ot, 1)

                t.wait_ge(s_wl, 1)
                qchunk(0)
                t.wait_ge(s_vxe, 1)
                t.wait_ge(s_basee, 1)
                for i in range(-1, T + 2):
                    if 0 <= i < T:
                        if i % 16 == 0:
                            t.wait_ge(s_bd, 8 * (i // 16 + 1))
                        scores(i, 0)
                    if i + 1 < T:
                        kproj(i + 1, 0)
                    if 1 <= i <= T:
                        transp(i - 1, 0)
                    if 0 <= i < T:
                        scores(i, 1)
                    if i + 1 < T:
                        kproj(i + 1, 1)
                    if 1 <= i <= T:
                        tail(i - 1)
                        transp(i - 1, 1)
                    if i + 1 < T:
                        vproj(i + 1)
                    if 1 <= i <= T:
                        pv(i - 1)
                    if i >= 2:
                        gather(i - 2)
                    if i < 48 and i % 16 == 6:
                        t.wait_ge(s_pte, 2 * i)
                        qchunk(i // 16 + 1)

        area(139, 155)
        xTh = put("xTh", [128, 2, 512], F32R)
        xTl = put("xTl", [128, 2, 512], F32R)
        hp = put("hp", [128, 2, 512])
        xn = put("xn", [128, 4, C])
        area(155, 207.75)
        stg = put("stg", [128, 2, 1024])
        b1h = put("b1h", [40, 1024], F32R)
        keep3 = top[0][0]
        XY = put("XY", [128, 2, 4, 512])
        L = put("L", [128, 4, 64])
        sm = put("sm", [128, 3, 4])
        Ab = put("Ab", [128, 2, 4, 128])
        AT = put("AT", [128, 4, 128])
        zs = put("zs", [128, 2, 512])
        yn = put("yn", [128, 4, C])
        gh = put("gh", [128, 2, 512], F32R)
        gw = put("gw", [128, 2, 512], F32R)

        u_y = sem("u_y")
        u_x = sem("u_x")
        u_xb = sem("u_xb")
        u_st = sem("u_st")
        u_mv = sem("u_mv")
        u_e = sem("u_e")
        u_rs = sem("u_rs")
        u_xn = sem("u_xn")
        u_t = sem("u_t")
        u_te = sem("u_te")
        u_tl = sem("u_tl")
        u_h = sem("u_h")
        u_he = sem("u_he")
        u_sc = sem("u_sc")
        u_l = sem("u_l")
        u_ch = sem("u_ch")
        u_sub = sem("u_sub")
        u_ex = sem("u_ex")
        u_az = sem("u_az")
        u_a = sem("u_a")
        u_at = sem("u_at")
        u_ate = sem("u_ate")
        u_xy = sem("u_xy")
        u_ye = sem("u_ye")
        u_cb = sem("u_cb")
        u_o = sem("u_o")
        u_z = sem("u_z")
        u_zt = sem("u_zt")
        u_b2 = sem("u_b2")
        u_x3 = sem("u_x3")
        f_st = sem("f_st")
        f_mv = sem("f_mv")
        f_rs = sem("f_rs")
        f_yn = sem("f_yn")
        f_yd = sem("f_yd")
        f_t = sem("f_t")
        f_hi = sem("f_hi")
        f_lo = sem("f_lo")
        f_wg = sem("f_wg")
        f_g = sem("f_g")
        f_gl = sem("f_gl")
        f_gs = sem("f_gs")
        f_ge = sem("f_ge")
        f_gt = sem("f_gt")
        w_d = [sem("w_d0"), sem("w_d1")]
        w_h = sem("w_h")
        w_l = sem("w_l")
        w_b = sem("w_b")
        w_o = sem("w_o")
        m01 = cst[:, C_M01:C_M01 + 1]
        m10 = cst[:, C_M01 + 1:C_M01 + 2]

        uses = []
        for k in range(7):
            if k < 4:
                uses += [(("y", k, h), u_x, 2 * k + h + 1) for h in range(2)]
            if 0 <= k - 1 < 4:
                uses += [(("h", k - 1, m), u_he, 2 * (k - 1) + m + 1) for m in range(2)]
                uses += [(("s", k - 1), u_l, 2 * (k - 1) + 2)]
            if 0 <= k - 2 < 4:
                uses += [(("at", k - 2), u_ate, k - 1)]
            if 0 <= k - 1 < 4:
                uses += [(("xy", k - 1, j), u_ye, 4 * (k - 1) + j + 1) for j in range(4)]
            if 0 <= k - 2 < 4:
                uses += [(("ay", k - 2, h), u_z, 2 * (k - 2) + h + 1) for h in range(2)]
            if 0 <= k - 3 < 4:
                uses += [(("t3", k - 3, h), f_lo, 2 * (k - 3) + h + 1) for h in range(2)]
                uses += [(("g", k - 3), f_gl, k - 2)]
            if k < 4:
                uses += [(("t", k, h), u_tl, 2 * k + h + 1) for h in range(2)]
        place = {u[0]: n for n, u in enumerate(uses)}

        def bank(*key):
            return B[place[key] % 8]

        def w1(q, part):
            o = (q // 2) * 4096 + part * 2048 + (q % 2) * 1024
            return W1[:, o:o + 1024]

        PIECES = [[0, 1, 2], [3, 4, 5], [6, 7], [8, 9], [10, 11], [12, 13], [14, 15]]

        with nc.Block() as block:

            @block.sync
            def _(sp):
                sp.wait_ge(s_ote, T)
                for k in range(7):
                    for q in PIECES[k]:
                        if q >= 2:
                            sp.wait_ge(w_l, q - 1)
                        sp.dma_start(stg[:, q % 2, :], d["W1T"][q // 2, 128 * (q % 2):128 * (q % 2) + 128, :]
                                     ).then_inc(w_d[q % 2], 16)
                    c = k - 2
                    if 0 <= c < 4:
                        sp.wait_ge(f_yn, 4 * c + 4)
                        sp.dma_start(y_d.rearrange("(n p) c -> p n c", p=128)[:, 4 * c:4 * c + 4, :], yn[:, :, :]
                                     ).then_inc(f_yd, 16)
                sp.wait_ge(f_yd, 64)

            @block.tensor
            def _(t):
                t.wait_ge(s_ote, T)
                t.wait_ge(s_w2, 48)
                t.wait_ge(s_wsd, 6)

                def take(*key):
                    n = place[key]
                    if n >= 8:
                        _, s, val = uses[n - 8]
                        t.wait_ge(s, val)
                    return B[n % 8]

                for k in range(7):
                    if k < 4:
                        for h in range(2):
                            b = take("y", k, h)
                            for jj in range(2):
                                j = 4 * k + 2 * h + jj
                                for m in range(2):
                                    mm = t.matmul(b[:, C * jj:C * jj + C], OT[:, m, 128 * j:128 * j + 128], Wo[:, m, :],
                                                  start=(m == 0), stop=(m == 1))
                            mm.then_inc(u_y, 1)
                    c = k - 1
                    if 0 <= c < 4:
                        t.wait_ge(u_tl, 2 * c + 2)
                        for m in range(2):
                            b = take("h", c, m)
                            e = 0
                            for h in range(2):
                                s = slice(128 * m, 128 * m + 128)
                                for w, x in ((0, xTh), (1, xTh), (0, xTl)):
                                    mm = t.matmul(b[:, :], WaR[:, w, h, s], x[:, h, :], start=(e == 0), stop=(e == 5))
                                    e += 1
                            mm.then_inc(u_h, 1)
                        b = take("s", c)
                        t.wait_ge(u_he, 2 * c + 2)
                        for h in range(2):
                            mm = t.matmul(b[:, :], bcol[:, 6 + h:7 + h].broadcast_to([128, 128]), hp[:, h, :],
                                          start=(h == 0), stop=(h == 1))
                        mm.then_inc(u_sc, 1)
                    c = k - 2
                    if 0 <= c < 4:
                        b = take("at", c)
                        t.wait_ge(u_a, 2 * c + 2)
                        for j in range(4):
                            mm = t.transpose(b[:, 128 * j:128 * j + 128], Ab[:, c % 2, j, :], ident)
                        mm.then_inc(u_at, 1)
                    c = k - 1
                    if 0 <= c < 4:
                        for j in range(4):
                            b = take("xy", c, j)
                            e = 0
                            for h in range(2):
                                s = slice(128 * j, 128 * j + 128)
                                for x, w in ((xTh, 0), (xTh, 1), (xTl, 0)):
                                    mm = t.matmul(b[:, :], x[:, h, s], WcR[:, w, h, :], start=(e == 0), stop=(e == 5))
                                    e += 1
                            mm.then_inc(u_xy, 1)
                    c = k - 2
                    if 0 <= c < 4:
                        t.wait_ge(u_ate, c + 1)
                        t.wait_ge(u_ye, 4 * c + 4)
                        for h in range(2):
                            b = take("ay", c, h)
                            for jj in range(2):
                                j = 2 * h + jj
                                mm = t.matmul(b[:, C * jj:C * jj + C], AT[:, j, :], XY[:, c % 2, j, C:2 * C],
                                              start=True, stop=True)
                            mm.then_inc(u_o, 1)
                    c = k - 3
                    if 0 <= c < 4:
                        for h in range(2):
                            b = take("t3", c, h)
                            for j in range(4):
                                t.wait_ge(f_yn, 4 * c + j + 1)
                                mm = t.transpose(b[:, 128 * j:128 * j + 128], yn[:, j, 128 * h:128 * h + 128], ident)
                            mm.then_inc(f_t, 1)
                        b = take("g", c)
                        t.wait_ge(f_lo, 2 * c + 2)
                        t.wait_ge(f_wg, 2)
                        for j in range(4):
                            e = 0
                            for h in range(2):
                                s = slice(128 * j, 128 * j + 128)
                                for x, w in ((gh, 0), (gh, 1), (gw, 0)):
                                    mm = t.matmul(b[:, E * j:E * j + E], x[:, h, s], WgR[:, w, h, :],
                                                  start=(e == 0), stop=(e == 5))
                                    e += 1
                        mm.then_inc(f_g, 1)
                    if k < 4:
                        for h in range(2):
                            b = take("t", k, h)
                            for j in range(4):
                                t.wait_ge(u_xn, 4 * k + j + 1)
                                mm = t.transpose(b[:, 128 * j:128 * j + 128], xn[:, j, 128 * h:128 * h + 128], ident)
                            mm.then_inc(u_t, 1)

            @block.vector
            def _(v):
                cnt = [0]

                def link(ins):
                    cnt[0] += 1
                    ins.then_inc(u_ch, 1)
                    v.wait_ge(u_ch, cnt[0])

                def gate(c):
                    k = slice(4 * c, 4 * c + 4)

                    def bc(ap):
                        return ap.unsqueeze(2).broadcast_to([128, 4, E])

                    v.wait_ge(f_g, c + 1)
                    v.tensor_copy(gl[:, k, :], bank("g", c)[:, 0:4 * E].rearrange("p (n e) -> p n e", e=E)
                                  ).then_inc(f_gl, 1)
                    v.wait_ge(f_gl, c + 1)
                    link(v.tensor_reduce(gs[:, 0, k], gl[:, k, :], AX.X, ALU.max))
                    v.tensor_tensor(gl[:, k, :], gl[:, k, :], bc(gs[:, 0, k]), ALU.subtract).then_inc(f_gs, 1)
                    v.wait_ge(f_ge, c + 1)
                    link(v.tensor_reduce(gs[:, 1, k], gl[:, k, :], AX.X, ALU.add))
                    link(v.reciprocal(gs[:, 2, k], gs[:, 1, k]))
                    link(v.tensor_tensor(gl[:, k, :], gl[:, k, :], bc(gs[:, 2, k]), ALU.mult))
                    for j in range(4 * c, 4 * c + 4):
                        v.max(g8[:, j, :], gl[:, j, :]).then_inc(f_gt, 1)
                    for j in range(4 * c, 4 * c + 4):
                        v.wait_ge(f_gt, 8 * c + j - 4 * c + 1)
                        v.max_index(gi[:, j, :], g8[:, j, :], gl[:, j, :]).then_inc(f_gt, 1)
                    v.wait_ge(f_gt, 8 * c + 8)
                    link(v.tensor_copy(gs[:, 0:2, k], gi[:, k, 0:2].rearrange("p n a -> p a n")))
                    iot = cst[:, C_IOTA:C_IOTA + 8].unsqueeze(1).broadcast_to([128, 4, E])
                    v.tensor_tensor(oh[:, 0, k, :], iot, bc(gs[:, 0, k]), ALU.is_equal)
                    link(v.tensor_tensor(oh[:, 1, k, :], iot, bc(gs[:, 1, k]), ALU.is_equal))
                    link(v.tensor_tensor(Mk[:, k, :], oh[:, 0, k, :], oh[:, 1, k, :], ALU.add))
                    for j in range(4 * c, 4 * c + 4):
                        link(v.tensor_tensor(cum[:, j + 1, :], cum[:, j, :], Mk[:, j, :], ALU.add))
                    link(v.tensor_tensor(gs[:, 2, k], g8[:, k, 0], g8[:, k, 1], ALU.add))
                    link(v.tensor_scalar(gs[:, 2, k], gs[:, 2, k], 1e-9, None, ALU.add))
                    link(v.reciprocal(gs[:, 3, k], gs[:, 2, k]))
                    link(v.tensor_tensor(cmb[:, :, k], g8[:, k, 0:2].rearrange("p n a -> p a n"),
                                         gs[:, 3, k].unsqueeze(1).broadcast_to([128, 2, 4]), ALU.mult))

                v.wait_ge(s_ote, T)
                v.wait_ge(s_w2, 48)
                link(v.memset(cum[:, 0, :], 0.0))
                v.tensor_copy(WgR[:, 0, :, :], WgT[:, :, :]).then_inc(f_wg, 1)
                v.wait_ge(f_wg, 1)
                v.tensor_tensor(WgR[:, 1, :, :], WgT[:, :, :], WgR[:, 0, :, :].bitcast(F32), ALU.subtract
                                ).then_inc(f_wg, 1)
                for k in range(7):
                    if k < 4:
                        for h in range(2):
                            v.wait_ge(u_y, 2 * k + h + 1)
                            j = 4 * k + 2 * h
                            v.wait_ge(s_xbb, NTILE)
                            v.tensor_tensor(xb[:, j:j + 2, :], bank("y", k, h)[:, :].rearrange("p (a c) -> p a c", a=2),
                                            xb[:, j:j + 2, :], ALU.add).then_inc(u_x, 1)
                        for j in range(4):
                            v.wait_ge(u_x, 2 * k + j // 2 + 1)
                            v.bn_stats(st[:, 4 * k + j, :], xb[:, 4 * k + j, :]).then_inc(u_st, 1)
                        for j in range(4 * k, 4 * k + 4):
                            v.wait_ge(u_st, j + 1)
                            v.bn_aggr(mv[:, j, :], st[:, j, :]).then_inc(u_mv, 1)
                    c = k - 1
                    if 0 <= c < 4:
                        v.wait_ge(u_sc, c + 1)
                        if c:
                            v.wait_ge(u_a, 2 * c)
                        for h in range(2):
                            r = slice(64 * h, 64 * h + 64)
                            v.tensor_tensor(L[r, :, :],
                                            bank("s", c)[r, :].rearrange("p (j h s) -> p j h s", h=2, s=64)[:, :, h, :],
                                            cst[r, C_MN:C_MN + 64].unsqueeze(1).broadcast_to([64, 4, 64]), ALU.add
                                            ).then_inc(u_l, 1)
                        v.wait_ge(u_l, 2 * c + 2)
                        link(v.tensor_reduce(sm[:, 0, :], L[:, :, :], AX.X, ALU.max))
                        v.tensor_tensor(L[:, :, :], L[:, :, :], sm[:, 0, :].unsqueeze(2).broadcast_to([128, 4, 64]),
                                        ALU.subtract).then_inc(u_sub, 1)
                    if k < 4:
                        v.wait_ge(u_rs, k + 1)
                        if k:
                            v.wait_ge(u_t, 2 * k)
                            v.wait_ge(u_b2, 4 * k)
                        for j in range(4):
                            n = 4 * k + j
                            v.tensor_scalar(xn[:, j, :], xb[:, n, :], mv[:, n, 0:1], rs[:, n:n + 1],
                                            ALU.subtract, ALU.mult).then_inc(u_xn, 1)
                        for j in range(4):
                            n = 4 * k + j
                            v.wait_ge(u_xn, n + 1)
                            v.scalar_tensor_tensor(out=xb[:, n, :], in0=xn[:, j, :], scalar=m10, in1=xb[:, n, :],
                                                   op0=ALU.mult, op1=ALU.add).then_inc(u_b2, 1)
                    if 0 <= c < 4:
                        v.wait_ge(u_ex, c + 1)
                        link(v.tensor_reduce(sm[:, 1, :], L[:, :, :], AX.X, ALU.add))
                        link(v.reciprocal(sm[:, 2, :], sm[:, 1, :]))
                        v.wait_ge(u_az, 1)
                        for h in range(2):
                            r = slice(64 * h, 64 * h + 64)
                            v.tensor_tensor(Ab[r, c % 2, :, 64 * h:64 * h + 64], L[r, :, :],
                                            sm[r, 2, :].unsqueeze(2).broadcast_to([64, 4, 64]), ALU.mult
                                            ).then_inc(u_a, 1)
                    c = k - 2
                    if 0 <= c < 4:
                        for h in range(2):
                            v.wait_ge(u_o, 2 * c + h + 1)
                            v.wait_ge(u_cb, 4 * c + 2 * h + 2)
                            if c:
                                v.wait_ge(u_x3, 2 * c + h - 1)
                            v.tensor_tensor(zs[:, h, :].rearrange("p (a c) -> p a c", a=2),
                                            bank("ay", c, h)[:, :].rearrange("p (a c) -> p a c", a=2),
                                            XY[:, c % 2, 2 * h:2 * h + 2, 0:C], ALU.add).then_inc(u_z, 1)
                    c = k - 3
                    if 0 <= c < 4:
                        for h in range(2):
                            v.wait_ge(f_hi, 2 * c + h + 1)
                            v.tensor_tensor(gw[:, h, :], bank("t3", c, h)[:, :], gh[:, h, :].bitcast(F32), ALU.subtract
                                            ).then_inc(f_lo, 1)
                    c = k - 2
                    if 0 <= c < 4:
                        for h in range(2):
                            v.wait_ge(u_zt, 2 * c + h + 1)
                            v.wait_ge(u_b2, 4 * c + 4)
                            j = 4 * c + 2 * h
                            v.scalar_tensor_tensor(out=xb[:, j:j + 2, :],
                                                   in0=zs[:, h, :].rearrange("p (a c) -> p a c", a=2), scalar=m01,
                                                   in1=xb[:, j:j + 2, :], op0=ALU.mult, op1=ALU.add).then_inc(u_x3, 1)
                        for j in range(4 * c, 4 * c + 4):
                            v.wait_ge(u_x3, j // 2 + 1)
                            v.bn_stats(st[:, j, :], xb[:, j, :]).then_inc(f_st, 1)
                        for j in range(4 * c, 4 * c + 4):
                            v.wait_ge(f_st, j + 1)
                            v.bn_aggr(mv[:, j, :], st[:, j, :]).then_inc(f_mv, 1)
                    if k < 4:
                        for h in range(2):
                            v.wait_ge(u_te, 2 * k + h + 1)
                            v.tensor_tensor(xTl[:, h, :], bank("t", k, h)[:, :], xTh[:, h, :].bitcast(F32), ALU.subtract
                                            ).then_inc(u_tl, 1)
                    if 0 <= c < 4:
                        v.wait_ge(f_rs, c + 1)
                        if c:
                            v.wait_ge(f_t, 2 * c)
                            v.wait_ge(f_yd, 16 * c)
                        for j in range(4):
                            n = 4 * c + j
                            v.tensor_scalar(yn[:, j, :], xb[:, n, :], mv[:, n, 0:1], rs[:, n:n + 1],
                                            ALU.subtract, ALU.mult).then_inc(f_yn, 1)
                    c = k - 3
                    if 0 <= c < 4:
                        gate(c)

            @block.gpsimd
            def _(g):
                g.wait_ge(s_ote, T)
                g.memset(Ab[:, :, :, :], 0.0).then_inc(u_az, 1)
                cnt = [0]

                def rstd(c, ready, done):
                    k = slice(4 * c, 4 * c + 4)
                    g.wait_ge(ready, 4 * c + 4)
                    g.tensor_tensor(rs[:, k], mv[:, k, 1], epw[:, 0, k], ALU.add).then_inc(u_e, 1)
                    cnt[0] += 1
                    g.wait_ge(u_e, cnt[0])
                    g.tensor_tensor(rs[:, k], rs[:, k], epw[:, 1, k], ALU.pow).then_inc(done, 1)

                def lows(q):
                    g.wait_ge(w_h, q + 1)
                    g.tensor_tensor(w1(q, 1), stg[:, q % 2, :], w1(q, 0).bitcast(F32), ALU.subtract).then_inc(w_l, 1)

                for k in range(7):
                    if k < 4:
                        rstd(k, u_mv, u_rs)
                    if 0 <= k - 1 < 4:
                        c = k - 1
                        for j in range(4):
                            g.wait_ge(u_ye, 4 * c + j + 1)
                            g.tensor_tensor(XY[:, c % 2, j, 0:C], XY[:, c % 2, j, 0:C], bcc[:, 1, :], ALU.add
                                            ).then_inc(u_cb, 1)
                    if 0 <= k - 2 < 4:
                        rstd(k - 2, f_mv, f_rs)
                    for q in PIECES[k]:
                        lows(q)

            @block.scalar
            def _(a):
                a.wait_ge(s_ote, T)

                def highs(q):
                    a.wait_ge(w_d[q % 2], 16 * (q // 2 + 1))
                    if q >= 10:
                        a.wait_ge(u_y, 8)
                    if q >= 12:
                        a.wait_ge(u_xy, 16)
                        a.wait_ge(u_b2, 16)
                    a.activation(w1(q, 0), stg[:, q % 2, :], ACT.Copy).then_inc(w_h, 1)

                for k in range(7):
                    c = k - 1
                    if 0 <= c < 4:
                        for m in range(2):
                            a.wait_ge(u_h, 2 * c + m + 1)
                            if c:
                                a.wait_ge(u_sc, c)
                            a.activation(hp[:, m, :], bank("h", c, m)[:, :], ACT.Tanh).then_inc(u_he, 1)
                    c = k - 2
                    if 0 <= c < 4:
                        a.wait_ge(u_at, c + 1)
                        if c:
                            a.wait_ge(u_o, 2 * c)
                        a.activation(AT[:, :, :].rearrange("p j n -> p (j n)"), bank("at", c)[:, :], ACT.Copy
                                     ).then_inc(u_ate, 1)
                    c = k - 1
                    if 0 <= c < 4:
                        for j in range(4):
                            a.wait_ge(u_xy, 4 * c + j + 1)
                            if c >= 2:
                                a.wait_ge(u_z, 2 * (c - 1))
                            a.activation(XY[:, c % 2, j, :], bank("xy", c, j)[:, :], ACT.Copy).then_inc(u_ye, 1)
                            if j == 0:
                                a.wait_ge(u_sub, c + 1)
                                a.activation(L[:, :, :], L[:, :, :], ACT.Exp).then_inc(u_ex, 1)
                    c = k - 2
                    if 0 <= c < 4:
                        for h in range(2):
                            a.wait_ge(u_z, 2 * c + h + 1)
                            a.activation(zs[:, h, :], zs[:, h, :], ACT.Tanh).then_inc(u_zt, 1)
                    c = k - 3
                    if 0 <= c < 4:
                        for h in range(2):
                            a.wait_ge(f_t, 2 * c + h + 1)
                            if c:
                                a.wait_ge(f_g, c)
                            a.activation(gh[:, h, :], bank("t3", c, h)[:, :], ACT.Copy).then_inc(f_hi, 1)
                    if k < 4:
                        for h in range(2):
                            a.wait_ge(u_t, 2 * k + h + 1)
                            if k:
                                a.wait_ge(u_xy, 4 * k)
                            a.activation(xTh[:, h, :], bank("t", k, h)[:, :], ACT.Copy).then_inc(u_te, 1)
                    for q in PIECES[k]:
                        highs(q)
                    c = k - 3
                    if 0 <= c < 4:
                        a.wait_ge(f_gs, c + 1)
                        a.activation(gl[:, 4 * c:4 * c + 4, :], gl[:, 4 * c:4 * c + 4, :], ACT.Exp).then_inc(f_ge, 1)

        top[0] = [keep3, BASE + int(207.75 * KB)]
        WoT = put("WoT", [128, 4, C])
        b1r = put("b1r", [40, 1024])
        ti = put("ti", [128, E])
        tj = put("tj", [128, 3, E])
        th = put("th", [128, E, 16])
        ps = put("ps", [128, NTILE, E])
        pf = put("pf", [128, 2, NTILE])
        pi = put("pi", [128, 2, NTILE], I32)
        rq = put("rq", [128, 2, 2, NTILE], I32)
        rf = put("rf", [128, 2, 2, NTILE])
        te = put("te", [128, 40, E])
        tf = put("tf", [128, 40])
        ew = put("ew", [1, 40], I32)
        sel = put("sel", [40, 40], F32R)
        i16 = put("i16", [128, 128], F16)
        A16 = put("A16", [128, 4, 128], F16)
        B16 = put("B16", [128, 4, 40], F16)
        inv = put("inv", [128, 40], I32)
        Xg = put("Xg", [128, 3, C])
        xh = put("xh", [128, 2, 2, 128], F32R)
        xl = put("xl", [128, 2, 2, 128], F32R)
        sg = put("sg", [128, 2, 512])
        gg = put("gg", [128, 2, 512])
        area(27, 60)
        cg = put("cg", [128, 2, 2, 512])
        zc = put("zc", [128, 2, 512])
        zT = put("zT", [128, 2, 512])
        fo = put("fo", [128, 4, C])

        r_b = sem("r_b")
        r_z = sem("r_z")
        r_p = sem("r_p")
        r_c = sem("r_c")
        r_A = sem("r_A")
        r_i = sem("r_i")
        r_iv = sem("r_iv")
        r_ew = sem("r_ew")
        r_b3 = sem("r_b3")
        e_x = [sem(f"e_x{i}") for i in range(3)]
        e_t = sem("e_t")
        e_hi = sem("e_hi")
        e_lo = sem("e_lo")
        e_h = sem("e_h")
        e_sg = sem("e_sg")
        e_g = sem("e_g")
        e_gd = [sem("e_gd0"), sem("e_gd1")]
        c_g = [sem("c_g0"), sem("c_g1")]
        c_z = sem("c_z")
        c_m = sem("c_m")
        c_t = sem("c_t")
        c_te = sem("c_te")
        c_o = sem("c_o")
        c_f = sem("c_f")
        c_out = [sem(f"c_out{i}") for i in range(4)]

        def tb(i):
            return B[2 + i % 2]

        def ab(i):
            return [(B[4], B[5]), (B[6], B[7]), (B[0], B[1])][i % 3]

        with nc.Block() as block:

            @block.sync
            def _(sp):
                sp.wait_ge(r_z, 1)
                sp.dma_start(b1r[0:8, :], d["b1"]).then_inc(w_b, 16)
                sp.dma_start(b1r[32:40, :], d["b1"]).then_inc(w_b, 16)
                sp.dma_start(WoT[:, :, :], d["fWoT"].rearrange("(k p) n -> p k n", p=128)).then_inc(w_o, 16)
                for i in range(NS):
                    sp.wait_ge(e_g, i + 1)
                    sp.dma_start(g_d[128 * i:128 * i + 128, :], gg[:, i % 2, :]).then_inc(e_gd[i % 2], 16)
                od = out.rearrange("t (n b) c -> n b t c", b=2)
                for j in range(NTILE):
                    sp.wait_ge(c_f, j + 1)
                    sp.dma_start(od[j], fo[:, j % 4, :]).then_inc(c_out[j % 4], 16)
                for s in c_out:
                    sp.wait_ge(s, 64)

            @block.gpsimd
            def _(g):
                g.memset(b1r[:, :], 0.0).then_inc(r_z, 1)
                g.wait_ge(r_iv, 1)
                g.wait_ge(f_yd, 64)
                for i in range(NS):
                    if i >= 3:
                        g.wait_ge(e_t, i - 2)
                    g.indirect_dma_start(out=Xg[:, i % 3, :], out_offset=None, in_=y_d,
                                         in_offset=bass.IndirectOffsetOnAxis(ap=inv[:, i:i + 1], axis=0)
                                         ).then_inc(e_x[i % 3], 16)
                g.wait_ge(e_gd[0], 16 * 20)
                g.wait_ge(e_gd[1], 16 * 19)
                g.wait_ge(e_h, NS)
                for j in range(NTILE):
                    if j >= 2:
                        g.wait_ge(c_z, j - 1)
                    for k in range(2):
                        g.indirect_dma_start(out=cg[:, j % 2, k, :], out_offset=None, in_=g_d,
                                             in_offset=bass.IndirectOffsetOnAxis(ap=pi[:, k, j:j + 1], axis=0)
                                             ).then_inc(c_g[j % 2], 16)

            def glu(v, i):
                v.wait_ge(e_sg, i + 1)
                if i >= 2:
                    v.wait_ge(e_gd[i % 2], 16 * (i // 2))
                v.tensor_tensor(gg[:, i % 2, :], ab(i)[0][:, :], sg[:, i % 2, :], ALU.mult).then_inc(e_g, 1)

            def final(v, j):
                v.wait_ge(c_o, j + 1)
                if j >= 4:
                    v.wait_ge(c_out[j % 4], 16 * (j // 4))
                v.tensor_tensor(fo[:, j % 4, :], B[4 + j % 4][:, 0:C], xb[:, j, :], ALU.add).then_inc(c_f, 1)

            @block.vector
            def _(v):
                cnt = [0]

                def link(ins):
                    cnt[0] += 1
                    ins.then_inc(r_c, 1)
                    v.wait_ge(r_c, cnt[0])

                v.wait_ge(u_ch, 1)
                v.tensor_copy(i16[:, :], cst[:, C_I128:C_I128 + 128]).then_inc(r_b, 1)
                v.wait_ge(w_b, 32)
                v.tensor_copy(b1h[:, :], b1r[:, :]).then_inc(r_b, 1)
                v.wait_ge(r_b, 2)
                v.tensor_tensor(b1h[32:40, :], b1r[32:40, :], b1h[32:40, :].bitcast(F32), ALU.subtract).then_inc(r_b, 1)
                v.wait_ge(r_p, 1)
                link(v.tensor_copy(ti[:, :], B[0][:, 128:136]))
                link(v.tensor_tensor(th[:, :, :], ti[:, :].unsqueeze(2).broadcast_to([128, E, 16]),
                                     cst[:, C_TH:C_TH + 16].unsqueeze(1).broadcast_to([128, E, 16]), ALU.is_gt))
                link(v.tensor_reduce(ti[:, :], th[:, :, :], AX.X, ALU.add))
                link(v.tensor_copy(tj[:, 0, :], ti[:, :]))
                a, b = 0, 1
                for s in (1, 2, 4):
                    v.tensor_copy(tj[:, b, 0:s], tj[:, a, 0:s]).then_inc(r_c, 1)
                    cnt[0] += 1
                    link(v.tensor_tensor(tj[:, b, s:E], tj[:, a, s:E], tj[:, a, 0:E - s], ALU.add))
                    a, b = b, a
                incl = tj[:, a, :]
                link(v.tensor_tensor(tj[:, 2, :], incl, ti[:, :], ALU.subtract))
                link(v.tensor_scalar(tj[:, 2, :], tj[:, 2, :], 128.0, None, ALU.mult))
                link(v.tensor_tensor(ps[:, :, :], B[0][:, 0:128].rearrange("p (n e) -> p n e", e=E),
                                     tj[:, 2, :].unsqueeze(1).broadcast_to([128, NTILE, E]), ALU.add))
                for k in range(2):
                    link(v.tensor_tensor(oh[:, k, :, :], oh[:, k, :, :], ps[:, :, :], ALU.mult))
                    link(v.tensor_reduce(pf[:, k, :], oh[:, k, :, :], AX.X, ALU.add))
                link(v.tensor_copy(pi[:, :, :], pf[:, :, :]))
                v.tensor_scalar(rq[:, 0, :, :], pi[:, :, :], 127, None, ALU.bitwise_and).then_inc(r_c, 1)
                cnt[0] += 1
                link(v.tensor_scalar(rq[:, 1, :, :], pi[:, :, :], 7, None, ALU.logical_shift_right))
                link(v.tensor_copy(rf[:, :, :, :], rq[:, :, :, :]))
                for n in range(32):
                    k, j = n // NTILE, n % NTILE
                    if n >= 4:
                        v.wait_ge(r_i, n - 3)
                    v.tensor_scalar(A16[:, n % 4, :], i16[:, :], rf[:, 0, k, j:j + 1], None, ALU.is_equal
                                    ).then_inc(r_A, 1)
                    v.tensor_scalar(B16[:, n % 4, :], i16[:, 0:40], rf[:, 1, k, j:j + 1],
                                    cst[:, C_TOK + j:C_TOK + j + 1], ALU.is_equal, ALU.mult).then_inc(r_A, 1)
                v.wait_ge(r_i, 32)
                v.tensor_copy(inv[:, :], B[1][:, 0:40]).then_inc(r_iv, 1)
                link(v.tensor_tensor(te[:, :, :], cst[:, C_I128:C_I128 + 40].unsqueeze(2).broadcast_to([128, 40, E]),
                                     incl.unsqueeze(1).broadcast_to([128, 40, E]), ALU.is_ge))
                link(v.tensor_reduce(tf[:, :], te[:, :, :], AX.X, ALU.add))
                link(v.tensor_scalar(tf[:, :], tf[:, :], float(E - 1), None, ALU.min))
                v.tensor_scalar(ew[:, :], tf[0:1, :], 4096.0, None, ALU.mult).then_inc(r_ew, 1)
                v.tensor_scalar(sel[:, :], tf[0:40, :], cst[0:40, C_PE:C_PE + 1], None, ALU.is_equal).then_inc(r_ew, 1)
                link(v.tensor_tensor(gs[:, 0, :], cmb[:, 0, :], cmb[:, 1, :], ALU.add))

                for i in range(NS):
                    v.wait_ge(e_hi, i + 1)
                    v.tensor_tensor(xl[:, i % 2, :, :].rearrange("p k n -> p (k n)"), tb(i)[:, 0:C],
                                    xh[:, i % 2, :, :].rearrange("p k n -> p (k n)").bitcast(F32), ALU.subtract
                                    ).then_inc(e_lo, 1)
                    if i:
                        glu(v, i - 1)
                    if i >= 2 and i - 2 < NTILE:
                        n = i - 2
                        v.scalar_tensor_tensor(out=xb[:, n, :], in0=bcc[:, 2, :], scalar=gs[:, 0, n:n + 1],
                                               in1=xb[:, n, :], op0=ALU.mult, op1=ALU.add).then_inc(r_b3, 1)
                glu(v, NS - 1)
                v.wait_ge(r_b3, NTILE)
                for j in range(NTILE):
                    v.wait_ge(c_g[j % 2], 32 * (j // 2 + 1))
                    if j >= 2:
                        v.wait_ge(c_t, j - 1)
                    v.tensor_scalar(zc[:, j % 2, :], cg[:, j % 2, 0, :], cmb[:, 0, j:j + 1], None, ALU.mult
                                    ).then_inc(c_m, 1)
                    v.wait_ge(c_m, j + 1)
                    v.scalar_tensor_tensor(out=zc[:, j % 2, :], in0=cg[:, j % 2, 1, :], scalar=cmb[:, 1, j:j + 1],
                                           in1=zc[:, j % 2, :], op0=ALU.mult, op1=ALU.add).then_inc(c_z, 1)
                    if j >= 2:
                        final(v, j - 2)
                final(v, NTILE - 2)
                final(v, NTILE - 1)

            @block.scalar
            def _(a):
                def high(i):
                    a.wait_ge(e_t, i + 1)
                    if i >= 2:
                        a.wait_ge(e_h, i - 1)
                    a.activation(xh[:, i % 2, :, :].rearrange("p k n -> p (k n)"), tb(i)[:, 0:C], ACT.Copy
                                 ).then_inc(e_hi, 1)

                high(0)
                for i in range(NS):
                    if i + 1 < NS:
                        high(i + 1)
                    a.wait_ge(e_h, i + 1)
                    if i >= 2:
                        a.wait_ge(e_g, i - 1)
                    a.activation(sg[:, i % 2, :], ab(i)[1][:, :], ACT.Sigmoid).then_inc(e_sg, 1)
                for j in range(NTILE):
                    a.wait_ge(c_t, j + 1)
                    if j >= 2:
                        a.wait_ge(c_o, j - 1)
                    a.activation(zT[:, j % 2, :], B[j % 2][:, :], ACT.Copy).then_inc(c_te, 1)

            @block.tensor
            def _(t):
                t.wait_ge(u_ch, 73)
                M = Mk[:, :, :].rearrange("p n e -> p (n e)")
                t.matmul(B[0][:, 0:128], cst[:, C_U:C_U + 128], M, start=True, stop=False, skip_group_check=True)
                t.matmul(B[0][:, 0:128], cst[:, C_ONE:C_ONE + 128], cum[:, 0:NTILE, :].rearrange("p n e -> p (n e)"),
                         start=False, stop=True, skip_group_check=True)
                t.matmul(B[0][:, 128:136], cst[:, C_ONE:C_ONE + 128], cum[:, NTILE, :], start=True, stop=True,
                         skip_group_check=True).then_inc(r_p, 1)
                for n in range(32):
                    t.wait_ge(r_A, 2 * n + 2)
                    t.matmul(B[1][:, 0:40], A16[:, n % 4, :], B16[:, n % 4, :], start=(n == 0), stop=(n == 31)
                             ).then_inc(r_i, 1)
                t.wait_ge(r_b, 3)
                t.wait_ge(r_ew, 2)
                t.wait_ge(w_l, 16)
                t.wait_ge(r_iv, 1)

                def turn(i):
                    t.wait_ge(e_x[i % 3], 16 * (i // 3 + 1))
                    if i >= 2:
                        t.wait_ge(e_lo, i - 1)
                    for k in range(2):
                        mm = t.transpose(tb(i)[:, 128 * k:128 * k + 128], Xg[:, i % 3, 128 * k:128 * k + 128], ident)
                    mm.then_inc(e_t, 1)

                turn(0)
                for i in range(NS):
                    if i + 1 < NS:
                        turn(i + 1)
                    w = t.value_load(ew[0:1, i:i + 1], min_val=0, max_val=(E - 1) * 4096)
                    t.wait_ge(e_lo, i + 1)
                    if i >= 3:
                        t.wait_ge(e_g, i - 2)
                    for h in (1, 0):
                        o = ab(i)[h][:, :]
                        t.matmul(o, sel[:, i:i + 1].broadcast_to([40, 128]), b1h[:, 512 * h:512 * h + 512],
                                 start=True, stop=False)
                        for k in range(2):
                            for x, part in ((xh, 0), (xh, 1), (xl, 0)):
                                mm = t.matmul(o, x[:, i % 2, k, :],
                                              W1[:, bass.DynSlice(w + (part * 2048 + k * 1024 + 512 * h), 512)],
                                              start=False, stop=(k == 1 and part == 0 and x is xl))
                    mm.then_inc(e_h, 1)

                def back(j):
                    t.wait_ge(c_z, j + 1)
                    if j >= 2:
                        t.wait_ge(c_te, j - 1)
                    for m in range(4):
                        mm = t.transpose(B[j % 2][:, 128 * m:128 * m + 128], zc[:, j % 2, 128 * m:128 * m + 128], ident)
                    mm.then_inc(c_t, 1)

                t.wait_ge(w_o, 16)
                t.wait_ge(e_g, NS)
                back(0)
                for j in range(NTILE):
                    if j + 1 < NTILE:
                        back(j + 1)
                    t.wait_ge(c_te, j + 1)
                    if j >= 4:
                        t.wait_ge(c_f, j - 3)
                    for m in range(4):
                        mm = t.matmul(B[4 + j % 4][:, 0:C], zT[:, j % 2, 128 * m:128 * m + 128], WoT[:, m, :],
                                      start=(m == 0), stop=(m == 3))
                    mm.then_inc(c_o, 1)


def bcast(ap, n, row=False):
    if row:
        return bass.AP(tensor=ap.tensor, offset=ap.offset, ap=[[0, n]] + list(ap.ap[1:]))
    return bass.AP(tensor=ap.tensor, offset=ap.offset, ap=[[0, n]] + list(ap.ap))


def kernel(**inputs):
    import concourse.bacc as bacc
    from concourse.bass_utils import run_bass_kernel_spmd

    nc = bacc.Bacc("TRN2", target_bir_lowering=False, num_devices=1)
    a = {k: np.asarray(v) for k, v in inputs.items()}
    ctx = a["ctx_768"]
    col = lambda v: v.reshape(-1, 128).T
    arrays = {
        "x": a["x"],
        "cst": constants(),
        "Wq": a["L0_xattn_Wq"],
        "Wk": a["L0_xattn_Wk"],
        "Wv": a["L0_xattn_Wv"],
        "xWo": a["L0_xattn_Wo"],
        "ctxT": np.concatenate([ctx, ctx[:, -1:]], axis=1).transpose(0, 2, 1),
        "c256": ctx[:, NK - 1, :].T,
        "bcol": np.concatenate([col(a["L0_xattn_bq"]), col(a["L0_xattn_bk"]), col(a["L0_xattn_bv"]),
                                col(a["L0_attn_proj"])], axis=1),
        "brow": np.stack([a["L0_xattn_bo"], a["L0_attn_concat_b"], a["L0_ffn_bo"]]),
        "aW": a["L0_attn_W"],
        "cwT": a["L0_attn_concat_w"].T.reshape(2, 256, 256).transpose(1, 0, 2),
        "WgT": a["L0_ffn_Wg"].T,
        "W1T": a["L0_ffn_W1"].transpose(0, 2, 1),
        "b1": a["L0_ffn_b1"],
        "fWoT": a["L0_ffn_Wo"].T,
    }
    arrays = {k: np.ascontiguousarray(v) for k, v in arrays.items()}
    d = {k: nc.dram_tensor("in_" + k, v.shape, F32, kind="ExternalInput").ap() for k, v in arrays.items()}
    out = nc.dram_tensor("out", [T, NQ, C], F32, kind="ExternalOutput").ap()
    vx_d = nc.dram_tensor("vx_d", [4, T, 65], F32, kind="Internal").ap()
    y_d = nc.dram_tensor("y_d", [NT, C], F32, kind="Internal").ap()
    g_d = nc.dram_tensor("g_d", [NS * 128, HF], F32, kind="Internal").ap()
    build(nc, d, out, vx_d, y_d, g_d)
    r = run_bass_kernel_spmd(nc, [{"in_" + k: v for k, v in arrays.items()}], core_ids=[0])
    return r.results[0]["out"]
```

```python
from contextlib import ExitStack

import numpy as np
import concourse.bass as bass
from concourse import mybir

ALU = mybir.AluOpType
ACT = mybir.ActivationFunctionType
AX = mybir.AxisListType
F32 = mybir.dt.float32
F32R = mybir.dt.float32r
F16 = mybir.dt.float16
I32 = mybir.dt.int32

T, NQ, C, CK, NK = 64, 32, 256, 192, 257
NKP = 258
NT = T * NQ
NTILE = NT // 128
CLAMP = 10000.0
EPS = 1e-5
NEG = float(np.finfo(np.float32).min)
E, HF = 8, 512
NPAIR = T // 2
CH = 2
NS = 39
BASE = 16512
KB = 1024

C_ID = 0
C_GM = 128
C_OM = 132
C_R = 136
C_MN = 168
C_M01 = 232
C_IOTA = 234
C_U = 242
C_I128 = 370
C_ONE = 498
C_PE = 626
C_TH = 627
C_TOK = 643
C_END = 659


def constants():
    p = np.arange(128)
    c = np.zeros((128, C_END), np.float32)
    c[:, C_ID:C_ID + 128] = np.eye(128)
    c[:, C_GM:C_GM + 4] = (p[:, None] // 16) % 4 == np.arange(4)
    c[:, C_OM:C_OM + 4] = p[:, None] // 32 == np.arange(4)
    c[:, C_R:C_R + 32] = p[:, None] % 32 == np.arange(32)
    c[:, C_MN:C_MN + 64] = np.where(np.arange(64) < (p % 64)[:, None], 0.0, NEG)
    c[:, C_M01] = (p % 64) >= 2
    c[:, C_M01 + 1] = (p % 64) < 2
    c[:, C_IOTA:C_IOTA + 8] = np.arange(8)
    c[:, C_U:C_U + 128] = p[:, None] < np.arange(128)
    c[:, C_I128:C_I128 + 128] = np.arange(128)
    c[:, C_ONE:C_ONE + 128] = 1.0
    c[:, C_PE] = np.where(p % 32 < 8, p % 32, -1)
    c[:, C_TH:C_TH + 16] = 128.0 * np.arange(16)
    c[:, C_TOK:C_TOK + 16] = 128 * np.arange(16) + p[:, None]
    return c


def build(nc, d, out, vx_d, y_d, g_d):
    ctx = ExitStack()
    with ctx:
        def sem(name):
            return ctx.enter_context(nc.semaphore(name))

        B = [ctx.enter_context(nc.psum_tensor(f"bank{i}", [128, 512], F32)) for i in range(8)]

        top = [0]

        def area(start, end):
            top[0] = [BASE + int(start * KB), BASE + int(end * KB)]

        def put(name, shape, dt=F32):
            size = 2 if dt == F16 else 4
            for n in shape[1:]:
                size *= n
            size = -(-size // 32) * 32
            at, end = top[0]
            assert at + size <= end, (name, at + size - end)
            top[0][0] += size
            return nc.alloc_sbuf_tensor_at(name, shape, dt, offset=at)

        area(0, 27)
        cst = put("cst", [128, C_END])
        xb = put("xb", [128, NTILE, C])
        bcol = put("bcol", [128, 8])
        bcc = put("bcc", [128, 3, C])
        st = put("st", [128, NTILE, 6])
        mv = put("mv", [128, NTILE, 2])
        rs = put("rs", [128, NTILE])
        epw = put("epw", [128, 2, NTILE])
        WgT = put("WgT", [128, 2, E])
        gl = put("gl", [128, NTILE, E])
        g8 = put("g8", [128, NTILE, E])
        gi = put("gi", [128, NTILE, E], mybir.dt.uint32)
        oh = put("oh", [128, 2, NTILE, E])
        Mk = put("Mk", [128, NTILE, E])
        cum = put("cum", [128, NTILE + 1, E])
        gs = put("gs", [128, 4, NTILE])
        cmb = put("cmb", [128, 2, NTILE])
        area(27, 155)
        W1 = put("W1", [128, E * 2 * 2 * 1024], F32R)
        area(107, 123)
        OT = put("OT", [128, 2, NT])
        area(123, 139)
        Wo = put("Wo", [128, 2, C])
        WaR = put("WaR", [128, 2, 2, C], F32R)
        WcR = put("WcR", [128, 2, 2, 2 * C], F32R)

        ident = cst[:, C_ID:C_ID + 128]

        s_c = sem("s_c")
        s_w = sem("s_w")
        s_w3 = sem("s_w3")
        s_w2 = sem("s_w2")
        s_x = [sem(f"s_x{i}") for i in range(4)]
        s_xb = sem("s_xb")
        s_st = sem("s_st")
        s_mv = sem("s_mv")
        s_ep = sem("s_ep")
        s_rs = sem("s_rs")
        s_xn = sem("s_xn")
        s_t0 = sem("s_t0")
        s_t0e = sem("s_t0e")
        s_q = sem("s_q")
        s_qe = sem("s_qe")
        s_bd = sem("s_bd")
        s_wh = sem("s_wh")
        s_wl = sem("s_wl")
        s_cx = [sem("s_cx0"), sem("s_cx1")]
        s_hi = sem("s_hi")
        s_lo = sem("s_lo")
        s_vx = sem("s_vx")
        s_vxe = sem("s_vxe")
        s_vz = sem("s_vz")
        s_vd = sem("s_vd")
        s_vc = sem("s_vc")
        s_vb = [sem("s_vb0"), sem("s_vb1")]
        s_v1 = sem("s_v1")
        s_base = sem("s_base")
        s_basee = sem("s_basee")
        s_xbb = sem("s_xbb")
        s_ws = sem("s_ws")
        s_wsh = sem("s_wsh")
        s_wsd = sem("s_wsd")
        s_k = sem("s_k")
        s_v = sem("s_v")
        s_s = sem("s_s")
        s_t = sem("s_t")
        s_tt = sem("s_tt")
        s_o = sem("s_o")
        s_ot = sem("s_ot")
        s_cl = sem("s_cl")
        s_nm = sem("s_nm")
        s_pte = [sem("s_pte0"), sem("s_pte1")]
        s_kl = sem("s_kl")
        s_ttl = sem("s_ttl")
        s_vz2 = sem("s_vz2")
        s_qb = sem("s_qb")
        s_pz = sem("s_pz")
        s_cm = sem("s_cm")
        s_rc = sem("s_rc")
        s_rm = sem("s_rm")
        s_m = sem("s_m")
        s_ke = sem("s_ke")
        s_ve = sem("s_ve")
        s_tte = sem("s_tte")
        s_ex = sem("s_ex")
        s_pt = sem("s_pt")
        s_ote = sem("s_ote")

        area(27, 107)
        qh = put("qh", [128, 4, T, NQ])
        ql = put("ql", [128, 2, T, NQ])
        QH = put("QH", [128, 2, 4, 128], F32R)
        QL = put("QL", [128, 2, 2, 128], F32R)
        xnT = put("xnT", [128, 2, 512])
        qT = put("qT", [128, 2, 512])
        wA = put("wA", [128, 2, 2 * C])
        wH = put("wH", [128, 2, 2 * C], F32R)
        wL = put("wL", [128, 2, 2 * C], F32R)
        Wq = put("Wq", [128, 2, C])
        base = put("base", [128, C])
        c256 = put("c256", [128, 2, T])
        area(22.375, 27)
        lA = put("lA", [128, 2, 2, NKP], F32R)
        area(137, 139)
        Mb = put("Mb", [128, 2, C])
        area(139, 207.75)
        cx = put("cx", [128, 2, 2, 2, NKP])
        hA = put("hA", [128, 2, 2, 2, NKP], F32R)
        vx = put("vx", [T, 2, 4, 65], F32R)
        Vs = put("Vs", [128, 3, 2, 4, 65])
        Vw = put("Vw", [128, 2, CH, 260])
        Vbd = put("Vbd", [96, 2, CH, 260], F32R)
        KS = put("KS", [128, 2, 4, NKP], F32R)
        Sc = put("Sc", [128, 2, 4, NK])
        Pm = put("Pm", [128, 2, 4, NK])
        PT = put("PT", [128, 2, 2, 4, 128])
        mx = put("mx", [128, 2, 4])
        nm = put("nm", [128, 2, 4])
        Pt = put("Pt", [128, 2, 96])
        PTt = put("PTt", [96, 2, 128], F32R)
        rc = put("rc", [128, 2, 4])
        rm = put("rm", [128, 2, 4, 4])

        xa = xb
        cf = cst
        gm = cf[:, C_GM:C_GM + 4]
        om = cf[:, C_OM:C_OM + 4]

        pP = [B[2], B[3]]
        pT = [B[4], B[5]]
        pO = [B[6], B[7]]

        def whalves(n):
            if n == 0:
                return [WaR[:, w, :, :].rearrange("p k n -> p (k n)") for w in range(2)]
            return [WcR[:, w, n - 1, :] for w in range(2)]

        with nc.Block() as block:

            @block.sync
            def _(sp):
                def load_x(g):
                    sp.dma_start(xa[:, 4 * g:4 * g + 4, :],
                                 d["x"].rearrange("(n a) b c -> (a b) n c", a=4)[:, 4 * g:4 * g + 4, :]
                                 ).then_inc(s_x[g], 16)

                load_x(0)
                sp.dma_start(cst[:, :], d["cst"]).then_inc(s_c, 16)
                sp.dma_start(Wq[:, :, :], d["Wq"].rearrange("(k p) n -> p k n", p=128)).then_inc(s_c, 16)
                sp.dma_start(bcol[:, :], d["bcol"]).then_inc(s_c, 16)
                for i, w in enumerate(("Wk", "Wv")):
                    o = i * C
                    sp.dma_start(wA[:, 0, o:o + C], d[w][0:128, :]).then_inc(s_w, 16)
                    sp.dma_start(wA[0:64, 1, o:o + C], d[w][128:192, :]).then_inc(s_w, 16)
                    sp.dma_start(wA[64:128, 1, o:o + C], d[w][128:192, :]).then_inc(s_w, 16)

                def load_ctx(j):
                    if j >= 2:
                        sp.wait_ge(s_lo, 2 * (j - 1))
                    s = s_cx[j % 2]
                    src = d["ctxT"]
                    sp.dma_start(cx[:, j % 2, 0, :, :], src[2 * j:2 * j + 2, 0:128, :].rearrange("b p n -> p b n")).then_inc(s, 16)
                    for h in range(2):
                        sp.dma_start(cx[64 * h:64 * h + 64, j % 2, 1, :, :],
                                     src[2 * j:2 * j + 2, 128:192, :].rearrange("b p n -> p b n")).then_inc(s, 16)

                load_ctx(0)
                sp.dma_start(c256[:, 0, :], d["c256"][0:128, :]).then_inc(s_w3, 16)
                sp.dma_start(c256[0:64, 1, :], d["c256"][128:192, :]).then_inc(s_w3, 16)
                sp.dma_start(Wo[:, :, :], d["xWo"].rearrange("(k p) n -> p k n", p=128)).then_inc(s_w3, 16)
                sp.dma_start(bcc[:, :, :], bcast(d["brow"], 128)).then_inc(s_w3, 16)
                load_ctx(1)
                for g in range(1, 4):
                    load_x(g)
                sp.wait_ge(s_vz, 1)
                sp.dma_start(vx_d.rearrange("w g t c -> (w g t c)").rearrange("(p n) -> p n", p=128),
                             Vw[:, :, :, :].rearrange("p a b c -> p (a b c)")).then_inc(s_vz2, 16)
                sp.wait_ge(s_vz2, 16)
                sp.wait_ge(s_vxe, 2)
                sp.wait_ge(s_v1, 3)
                for w in range(2):
                    sp.dma_start(bass.AP(tensor=vx_d.tensor, offset=w * 4 * T * 260,
                                         ap=[[260, T], [T * 260 + 65, 4], [1, 65]]), vx[:, w, :, :].bitcast(F32)).then_inc(s_vd, 16)
                sp.wait_ge(s_vd, 32)

                def load_vb(c):
                    if c >= 2:
                        sp.wait_ge(s_vc, c - 1)
                    for n, w in enumerate((0, 1, 0)):
                        sp.dma_start(Vw[32 * n:32 * n + 4, c % 2, :, :], vx_d[w, :, CH * c:CH * c + CH, :]
                                     ).then_inc(s_vb[c % 2], 16)

                load_vb(0)
                load_vb(1)
                xbd = d["x"].rearrange("t (n b) c -> b t n c", b=2)
                for j in range(2, NPAIR):
                    load_ctx(j)
                    load_vb(j)
                    if j == 3:
                        sp.wait_ge(s_wl, 1)
                        sp.dma_start(wA[:, 0, :].rearrange("p (k n) -> p k n", k=2),
                                     d["aW"].rearrange("(k p) n -> p k n", p=128)).then_inc(s_w2, 16)
                        sp.dma_start(wA[:, 1, :], d["cwT"][0:128].rearrange("p k n -> p (k n)")).then_inc(s_w2, 16)
                        sp.dma_start(WgT[:, :, :], d["WgT"].rearrange("(k p) n -> p k n", p=128)).then_inc(s_w2, 16)
                    if j == 10:
                        sp.wait_ge(s_wsd, 4)
                        sp.dma_start(wA[:, 0, :], d["cwT"][128:256].rearrange("p k n -> p (k n)")).then_inc(s_ws, 16)
                    if j == 22:
                        sp.wait_ge(s_t0, 8)
                        sp.dma_start(xb[0:64, :, :], xbd[0]).then_inc(s_xb, 16)
                        sp.dma_start(xb[64:128, :, :], xbd[1]).then_inc(s_xb, 16)

            @block.gpsimd
            def _(g):
                g.memset(epw[:, 0, :], EPS).then_inc(s_ep, 1)
                g.memset(epw[:, 1, :], -0.5).then_inc(s_ep, 1)
                g.memset(Vw[:, :, :, :], 0.0).then_inc(s_vz, 1)
                g.memset(Vs[:, :, :, :, 64:65], 1.0).then_inc(s_v1, 1)
                g.memset(vx[:, 0, :, 64:65].bitcast(F32), 1.0).then_inc(s_v1, 1)
                g.memset(vx[:, 1, :, 64:65].bitcast(F32), 0.0).then_inc(s_v1, 1)
                g.memset(Pt[:, :, :], 0.0).then_inc(s_pz, 1)

                def rstd(c):
                    k = slice(4 * c, 4 * c + 4)
                    g.wait_ge(s_mv, 4 * c + 4)
                    if c == 0:
                        g.wait_ge(s_ep, 2)
                    g.tensor_tensor(rs[:, k], mv[:, k, 1], epw[:, 0, k], ALU.add).then_inc(s_ep, 1)
                    g.wait_ge(s_ep, 3 + c)
                    g.tensor_tensor(rs[:, k], rs[:, k], epw[:, 1, k], ALU.pow).then_inc(s_rs, 1)
                    g.wait_ge(s_rs, c + 1)

                def wlow(n, h):
                    g.wait_ge(s_wsh, n + 1)
                    hi, lo = whalves(n)
                    c = slice(256 * h, 256 * h + 256)
                    g.tensor_tensor(lo[:, c], wA[:, n % 2, c], hi[:, c].bitcast(F32), ALU.subtract).then_inc(s_wsd, 1)
                    g.wait_ge(s_wsd, 2 * n + h + 1)

                rstd(0)
                def split(j, n):
                    b = j % 2
                    if n == 0:
                        g.wait_ge(s_cx[b], 48 * (j // 2 + 1))
                        g.wait_ge(s_v, 2 * (j - 1))
                    if n == 2 and j < 2:
                        g.wait_ge(s_cx[b], 48)
                    if n < 2:
                        g.tensor_scalar(hA[:, b, n, :, :], cx[:, b, n, :, :], 1.0, None, ALU.mult).then_inc(s_hi, 1)
                    elif n == 2:
                        g.wait_ge(s_hi, 2 * j + 2)
                        g.tensor_tensor(lA[:, b, :, :], cx[:, b, 0, :, :], hA[:, b, 0, :, :].bitcast(F32), ALU.subtract
                                        ).then_inc(s_lo, 1)
                    else:
                        g.wait_ge(s_lo, 2 * j + 1)
                        g.tensor_tensor(hA[64:128, b, 1, :, :], cx[64:128, b, 1, :, :],
                                        hA[64:128, b, 1, :, :].bitcast(F32), ALU.subtract).then_inc(s_lo, 1)
                        g.wait_ge(s_lo, 2 * j + 2)

                def spread(i):
                    if i % 16 == 0:
                        g.wait_ge(s_bd, 12 * (i // 16 + 1))
                    if i >= 2:
                        g.wait_ge(s_s, 4 * (i - 1))
                    g.tensor_tensor(QH[:, i % 2, :, :].rearrange("p g (h q) -> p g h q", h=4),
                                    qh[:, :, i, :].unsqueeze(2).broadcast_to([128, 4, 4, NQ]),
                                    gm.unsqueeze(1).unsqueeze(3).broadcast_to([128, 4, 4, NQ]), ALU.mult
                                    ).then_inc(s_qb, 1)
                    g.tensor_tensor(QL[:, i % 2, :, :].rearrange("p g (h q) -> p g h q", h=4),
                                    ql[:, :, i, :].unsqueeze(2).broadcast_to([128, 2, 4, NQ]),
                                    gm.unsqueeze(1).unsqueeze(3).broadcast_to([128, 2, 4, NQ]), ALU.mult
                                    ).then_inc(s_qb, 1)

                for n in (2, 3):
                    split(0, n)
                for i in range(T):
                    if i == 0:
                        spread(0)
                        g.wait_ge(s_pz, 1)
                    if i + 1 < T:
                        spread(i + 1)
                    if i == 0:
                        for n in (2, 3):
                            split(1, n)
                    j, n = (i + 3) // 2 if i % 2 else (i + 2) // 2, 0 if i % 2 else 2
                    go = 2 <= j < NPAIR
                    if go:
                        split(j, n)
                        split(j, n + 1)
                    g.wait_ge(s_ex, 4 * i + 4)
                    if i >= 2:
                        g.wait_ge(s_tt, i - 1)
                    g.tensor_copy(Pt[:, i % 2, :].rearrange("p (w g) -> p w g", w=3)[:, :, 0:4],
                                  Pm[:, i % 2, :, NK - 1].unsqueeze(1).broadcast_to([128, 3, 4])).then_inc(s_pt, 1)
                    if i % 16 == 2 and i < 48:
                        rstd(i // 16 + 1)
                    if i in (10, 12, 14, 16, 30, 32):
                        m = (10, 12, 14, 16, 30, 32).index(i)
                        wlow(m // 2, m % 2)
                    if i == 47:
                        g.wait_ge(s_xb, 32)
                        g.wait_ge(s_basee, 1)
                    if 47 <= i < 47 + NTILE:
                        m = i - 47
                        g.tensor_tensor(xb[:, m, :], xb[:, m, :], base[:, :], ALU.add).then_inc(s_xbb, 1)
                        g.wait_ge(s_xbb, m + 1)

            @block.vector
            def _(v):
                def stats(c):
                    v.wait_ge(s_x[c], 16)
                    for n in range(4 * c, 4 * c + 4):
                        v.bn_stats(st[:, n, :], xa[:, n, :]).then_inc(s_st, 1)
                    for n in range(4 * c, 4 * c + 4):
                        v.wait_ge(s_st, n + 1)
                        v.bn_aggr(mv[:, n, :], st[:, n, :]).then_inc(s_mv, 1)

                def xnorm(c):
                    v.wait_ge(s_mv, 4 * c + 4)
                    v.wait_ge(s_rs, c + 1)
                    for n in range(4 * c, 4 * c + 4):
                        v.tensor_scalar(xa[:, n, :], xa[:, n, :], mv[:, n, 0:1], rs[:, n:n + 1],
                                        ALU.subtract, ALU.mult).then_inc(s_xn, 1)

                def qevac(c):
                    for m in range(2):
                        v.wait_ge(s_q, 2 * c + m + 1)
                        if c:
                            v.wait_ge(s_bd, 12 * c)
                        v.tensor_scalar(qT[:, m, :], pT[m][:, :], bcol[:, m:m + 1], 0.25, ALU.add, ALU.mult
                                        ).then_inc(s_qe, 1)

                def qsplit(c, n):
                    m, n = n // 6, n % 6
                    k = slice(16 * c, 16 * c + 16)
                    gg = n % 2
                    r = slice(64 * gg, 64 * gg + 64)
                    o = slice(64 * (1 - gg), 128 - 64 * gg)
                    src = qT[r, m, :].rearrange("p (t b) -> p t b", b=NQ)
                    v.wait_ge(s_qe, 2 * c + m + 1)
                    if n < 2:
                        v.tensor_copy(qh[r, 2 * m + gg, k, :].bitcast(F32R), src).then_inc(s_bd, 1)
                    elif n < 4:
                        v.tensor_copy(qh[o, 2 * m + gg, k, :].bitcast(F32R), src).then_inc(s_bd, 1)
                    else:
                        v.wait_ge(s_bd, 12 * c + 6 * m + gg + 1)
                        v.tensor_tensor(ql[r, m, k, :], src, qh[r, 2 * m + gg, k, :], ALU.subtract).then_inc(s_bd, 1)

                stats(0)
                xnorm(0)
                v.wait_ge(s_w, 16 * 6)
                v.wait_ge(s_c, 48)
                v.tensor_copy(wH[:, :, :], wA[:, :, :]).then_inc(s_wh, 1)
                v.wait_ge(s_wh, 1)
                v.tensor_tensor(wL[:, :, :], wA[:, :, :], wH[:, :, :].bitcast(F32), ALU.subtract).then_inc(s_wl, 1)
                qevac(0)
                v.wait_ge(s_vx, 1)
                vs = B[6][0:T, 0:C].rearrange("p (g c) -> p g c", g=4)
                v.tensor_copy(vx[:, 0, :, 0:64], vs).then_inc(s_vxe, 1)
                v.wait_ge(s_vxe, 1)
                v.tensor_tensor(vx[:, 1, :, 0:64], vs, vx[:, 0, :, 0:64].bitcast(F32), ALU.subtract).then_inc(s_vxe, 1)
                v.wait_ge(s_base, 1)
                v.tensor_tensor(base[:, :], B[7][:, 0:C], bcc[:, 0, :], ALU.add).then_inc(s_basee, 1)
                for n in range(12):
                    qsplit(0, n)

                def clip(i, g):
                    v.wait_ge(s_s, 4 * i + g + 1)
                    v.tensor_scalar(Sc[:, i % 2, g, :], B[g % 2][:, 0:NK], -CLAMP, -CLAMP, ALU.max, ALU.max,
                                    accum_out=mx[:, i % 2, g:g + 1]).then_inc(s_cl, 1)

                def negmax(i, p):
                    v.wait_ge(s_cl, 4 * i + 2 * p + 2)
                    sc = Sc[:, i % 2, 2 * p:2 * p + 2, :].rearrange("p a b -> p (a b)")
                    v.tensor_scalar(sc, sc, CLAMP, None, ALU.min).then_inc(s_cm, 1)
                    v.tensor_scalar(nm[:, i % 2, 2 * p:2 * p + 2], mx[:, i % 2, 2 * p:2 * p + 2], CLAMP, -1.0,
                                    ALU.min, ALU.mult).then_inc(s_nm, 1)

                def klow(i, m):
                    v.wait_ge(s_ke, 4 * i + 2 * m + 2)
                    for gg in range(2):
                        r = slice(64 * gg, 64 * gg + 64)
                        o = slice(64 * (1 - gg), 128 - 64 * gg)
                        v.scalar_tensor_tensor(out=KS[o, i % 2, 2 * m + gg, :], in0=pP[(3 * i + m) % 2][r, 0:NKP],
                                               scalar=bcol[r, 2 + m:3 + m], in1=KS[r, i % 2, 2 * m + gg, :].bitcast(F32),
                                               op0=ALU.add, op1=ALU.subtract).then_inc(s_kl, 1)

                def taillow(i):
                    v.wait_ge(s_tte, i + 1)
                    n = 3 * (i + 2) + 1
                    v.tensor_tensor(PTt[64:96, i % 2, :], pP[n % 2][64:96, 384:512], PTt[64:96, i % 2, :].bitcast(F32),
                                    ALU.subtract).then_inc(s_ttl, 1)

                def vcopy(c):
                    v.wait_ge(s_vb[c % 2], 48 * (c // 2 + 1))
                    if c >= 2:
                        v.wait_ge(s_o, CH * (c - 1))
                    v.tensor_copy(Vbd[:, c % 2, :, :], Vw[0:96, c % 2, :, :]).then_inc(s_vc, 1)

                def otsum(i):
                    v.wait_ge(s_ot, i + 1)
                    v.tensor_reduce(OT[:, :, :].rearrange("p m (b t) -> p m b t", t=T)[:, :, :, i],
                                    pO[i % 2][:, 0:C].rearrange("p (m h q) -> p m q h", m=2, h=4), AX.X, ALU.add
                                    ).then_inc(s_ote, 1)

                def recip(i):
                    v.wait_ge(s_o, i + 1)
                    v.reciprocal(rc[:, i % 2, :], pO[i % 2][:, 0:260].rearrange("p (g c) -> p g c", g=4)[:, :, 64]
                                 ).then_inc(s_rc, 1)

                def rmask(i):
                    v.wait_ge(s_rc, i + 1)
                    v.tensor_tensor(rm[:, i % 2, :, :], rc[:, i % 2, :].unsqueeze(2).broadcast_to([128, 4, 4]),
                                    om.unsqueeze(1).broadcast_to([128, 4, 4]), ALU.mult).then_inc(s_rm, 1)

                def norm(i):
                    v.wait_ge(s_rm, i + 1)
                    v.tensor_tensor(Mb[:, i % 2, :].rearrange("p (g h c) -> p g h c", g=4, h=4),
                                    pO[i % 2][:, 0:260].rearrange("p (g c) -> p g c", g=4)[:, :, 0:64]
                                    .rearrange("p g (h c) -> p g h c", h=4),
                                    rm[:, i % 2, :, :].unsqueeze(3).broadcast_to([128, 4, 4, 16]), ALU.mult
                                    ).then_inc(s_m, 1)

                klow(0, 0)
                klow(0, 1)
                for i in range(T + 3):
                    if i < T:
                        clip(i, 0)
                    if i >= 3:
                        otsum(i - 3)
                    if 2 <= i < T + 2:
                        recip(i - 2)
                    if i < T:
                        clip(i, 1)
                    if 2 <= i < T + 2:
                        rmask(i - 2)
                    if i < T:
                        negmax(i, 0)
                    if i + 1 < T:
                        klow(i + 1, 0)
                    if 2 <= i < T + 2:
                        norm(i - 2)
                    if i < T:
                        clip(i, 2)
                        clip(i, 3)
                        negmax(i, 1)
                    if i + 1 < T:
                        klow(i + 1, 1)
                    if 1 <= i <= T:
                        taillow(i - 1)
                    if i % 2 == 0 and i < T:
                        vcopy(i // 2)
                    if i < 48:
                        c = i // 16 + 1
                        if i % 16 == 2:
                            stats(c)
                        if i % 16 == 4:
                            xnorm(c)
                        if i % 16 == 7:
                            qevac(c)
                        if 8 <= i % 16 < 14:
                            for n in range(2):
                                qsplit(c, 2 * (i % 16 - 8) + n)

            @block.scalar
            def _(a):
                def qchunk(c):
                    for k in range(2):
                        a.wait_ge(s_t0, 2 * c + k + 1)
                        if c:
                            a.wait_ge(s_q, 2 * c)
                        a.activation(xnT[:, k, :], pT[k][:, :], ACT.Copy).then_inc(s_t0e, 1)

                qchunk(0)
                for j in range(2):
                    a.wait_ge(s_cx[j], 48)
                    for n in range(2):
                        a.activation(hA[:, j, n, :, :], cx[:, j, n, :, :], ACT.Copy).then_inc(s_hi, 1)

                def kevac(i, m):
                    a.wait_ge(s_k, 2 * i + m + 1)
                    n = 3 * i + m
                    if m == 1 and i >= 2:
                        a.wait_ge(s_tt, i - 1)
                    for gg in range(2):
                        r = slice(64 * gg, 64 * gg + 64)
                        a.activation(KS[r, i % 2, 2 * m + gg, :], pP[n % 2][r, 0:NKP], ACT.Identity,
                                     bias=bcol[r, 2 + m:3 + m]).then_inc(s_ke, 1)

                def vevac(i):
                    a.wait_ge(s_v, i + 1)
                    n = 3 * i + 2
                    if i == 0:
                        a.wait_ge(s_v1, 3)
                    a.activation(Vs[:, i % 3, :, :, 0:64],
                                 pP[n % 2][:, :].rearrange("p (c g e) -> p c g e", c=2, g=4), ACT.Copy
                                 ).then_inc(s_ve, 1)

                def tevac(i):
                    a.wait_ge(s_tt, i + 1)
                    n = 3 * (i + 2) + 1
                    if i + 2 < T:
                        a.wait_ge(s_kl, 4 * (i + 2) + 4)
                    a.activation(PTt[:, i % 2, :], pP[n % 2][0:96, 384:512], ACT.Copy).then_inc(s_tte, 1)

                def ptevac(i, p):
                    a.wait_ge(s_t, 2 * i + p + 1)
                    a.activation(PT[:, i % 2, p, :, :].rearrange("p a b -> p (a b)"), pT[p][:, :], ACT.Copy
                                 ).then_inc(s_pte[p], 1)

                def exps(i, g):
                    a.wait_ge(s_cm, 2 * i + g // 2 + 1)
                    a.wait_ge(s_nm, 2 * i + g // 2 + 1)
                    a.activation(Pm[:, i % 2, g, :], Sc[:, i % 2, g, :], ACT.Exp, bias=nm[:, i % 2, g:g + 1]
                                 ).then_inc(s_ex, 1)

                for i in range(-1, T + 2):
                    if i + 1 < T:
                        kevac(i + 1, 0)
                    if 1 <= i <= T:
                        ptevac(i - 1, 0)
                    if 0 <= i < T:
                        exps(i, 0)
                        exps(i, 1)
                    if i + 1 < T:
                        kevac(i + 1, 1)
                    if 1 <= i <= T:
                        ptevac(i - 1, 1)
                    if 0 <= i < T:
                        exps(i, 2)
                        exps(i, 3)
                    if 1 <= i <= T:
                        tevac(i - 1)
                    if i + 1 < T:
                        vevac(i + 1)
                    if i < 48 and i % 16 == 6:
                        qchunk(i // 16 + 1)
                    if i in (8, 10, 28):
                        n = (8, 10, 28).index(i)
                        a.wait_ge([s_w2, s_w2, s_ws][n], [48, 48, 16][n])
                        a.activation(whalves(n)[0], wA[:, n % 2, :], ACT.Copy).then_inc(s_wsh, 1)

            @block.tensor
            def _(t):
                t.wait_ge(s_c, 48)
                def qturn(c):
                    for k in range(2):
                        if c:
                            t.wait_ge(s_pte[k], 16 * c - 10)
                        for j in range(4 * c, 4 * c + 4):
                            t.wait_ge(s_xn, j + 1)
                            mm = t.transpose(pT[k][:, 128 * (j % 4):128 * (j % 4) + 128], xa[:, j, 128 * k:128 * k + 128],
                                             ident)
                        mm.then_inc(s_t0, 1)

                def qproj(c):
                    t.wait_ge(s_t0e, 2 * c + 2)
                    for m in range(2):
                        if c:
                            t.wait_ge(s_pte[m], 16 * c - 9)
                        for k in range(2):
                            mm = t.matmul(pT[m][:, :], Wq[:, k, 128 * m:128 * m + 128], xnT[:, k, :],
                                          start=(k == 0), stop=(k == 1))
                        mm.then_inc(s_q, 1)

                def terms(b, bi):
                    hi0, hi1 = hA[:, b, 0, bi, :], hA[:, b, 1, bi, :]
                    lo0 = lA[:, b, bi, :]
                    return [(hi0, wH[:, 0, :]), (hi0, wL[:, 0, :]), (lo0, wH[:, 0, :]),
                            (hi1, wH[:, 1, :]), (hi1, wL[:, 1, :])]

                def wait_pp(n):
                    if n < 2:
                        return
                    i, r = (n - 2) // 3, (n - 2) % 3
                    if r == 2:
                        t.wait_ge(s_ve, i + 1)
                    else:
                        t.wait_ge(s_kl, 4 * i + 2 * r + 2)
                        if r == 1 and i >= 2:
                            t.wait_ge(s_ttl, i - 1)

                def kproj(i, m):
                    n = 3 * i + m
                    wait_pp(n)
                    t.wait_ge(s_lo, 2 * (i // 2 + 1))
                    for e, (c, w) in enumerate(terms((i // 2) % 2, i % 2)):
                        mm = t.matmul(pP[n % 2][:, 0:NKP], w[:, 128 * m:128 * m + 128], c, start=(e == 0), stop=(e == 4))
                    mm.then_inc(s_k, 1)

                def vproj(i):
                    n = 3 * i + 2
                    wait_pp(n)
                    for c in range(2):
                        for e, (x, w) in enumerate(terms((i // 2) % 2, i % 2)):
                            mm = t.matmul(pP[n % 2][:, C * c:C * c + C], x[:, 128 * c:128 * c + 128], w[:, C:2 * C],
                                          start=(e == 0), stop=(e == 4))
                    mm.then_inc(s_v, 1)

                def scores(i, p):
                    t.wait_ge(s_kl, 4 * i + 2 * p + 2)
                    t.wait_ge(s_qb, 2 * i + 2)
                    for gg in range(2):
                        if 4 * i + 2 * p >= 2:
                            t.wait_ge(s_cl, 4 * i + 2 * p - 1 + gg)
                        g = 2 * p + gg
                        r = slice(64 * gg, 64 * gg + 64)
                        t.matmul(B[gg][:, 0:NKP], QH[:, i % 2, g, :], KS[:, i % 2, g, :], start=True, stop=False)
                        t.matmul(B[gg][:, 0:NKP], QL[r, i % 2, p, :], KS[r, i % 2, g, :], start=False, stop=True
                                 ).then_inc(s_s, 1)

                def transp(i, p):
                    t.wait_ge(s_ex, 4 * i + 2 * p + 2)
                    if i >= 1:
                        t.wait_ge(s_pte[p], i)
                    if i % 16 == 6 and i < 48:
                        t.wait_ge(s_t0e, 2 * (i // 16 + 1) + p + 1)
                    if i % 16 == 7 and i < 48:
                        t.wait_ge(s_qe, 2 * (i // 16 + 1) + p + 1)
                    if i == 0:
                        t.wait_ge(s_qe, 2)
                    for gg in range(2):
                        for c in range(2):
                            o = 256 * gg + 128 * c
                            mm = t.transpose(pT[p][:, o:o + 128], Pm[:, i % 2, 2 * p + gg, 128 * c:128 * c + 128], ident)
                    mm.then_inc(s_t, 1)

                def tail(i):
                    t.wait_ge(s_pt, i + 1)
                    n = 3 * (i + 2) + 1
                    if i + 2 >= T:
                        t.wait_ge(s_ve, T)
                        t.wait_ge(s_ttl, i)
                    t.transpose(pP[n % 2][0:96, 384:512], Pt[:, i % 2, :], ident).then_inc(s_tt, 1)

                def pv(i):
                    if i >= 2:
                        t.wait_ge(s_ote, i - 1)
                    t.wait_ge(s_ve, i + 1)
                    first = True
                    for p in range(2):
                        t.wait_ge(s_pte[p], i + 1)
                        for gg in range(2):
                            g = 2 * p + gg
                            for c in range(2):
                                t.matmul(pO[i % 2][:, 65 * g:65 * g + 65], PT[:, i % 2, p, 2 * gg + c, :],
                                         Vs[:, i % 3, c, g, :], start=first, stop=False, skip_group_check=True)
                                first = False

                def pvtail(i):
                    t.wait_ge(s_ttl, i + 1)
                    c = i // CH
                    t.wait_ge(s_vc, c + 1)
                    t.matmul(pO[i % 2][:, 0:260], PTt[:, i % 2, :], Vbd[0:96, c % 2, i % CH, :], start=False, stop=True,
                             skip_group_check=True).then_inc(s_o, 1)

                def gather(i):
                    t.wait_ge(s_m, i + 1)
                    for m in range(2):
                        mm = t.transpose(pO[i % 2][:, 128 * m:128 * m + 128], Mb[:, i % 2, 128 * m:128 * m + 128], ident)
                    mm.then_inc(s_ot, 1)

                qturn(0)
                qproj(0)
                t.wait_ge(s_w, 16 * 6)
                t.wait_ge(s_w3, 16 * 4)
                for k in range(2):
                    K = 128 - 64 * k
                    mm = t.matmul(B[6][0:T, 0:C], c256[0:K, k, :], wA[0:K, k, C:2 * C], start=(k == 0), stop=(k == 1))
                mm.then_inc(s_vx, 1)
                for k in range(2):
                    mm = t.matmul(B[7][:, 0:C], bcol[:, 4 + k:5 + k].broadcast_to([128, 128]), Wo[:, k, :],
                                  start=(k == 0), stop=(k == 1))
                mm.then_inc(s_base, 1)
                t.wait_ge(s_wl, 1)
                t.wait_ge(s_vxe, 1)
                t.wait_ge(s_basee, 1)
                for i in range(-1, T + 2):
                    if 0 <= i < T:
                        scores(i, 0)
                    if i >= 2:
                        pvtail(i - 2)
                    if i + 1 < T:
                        kproj(i + 1, 0)
                    if 1 <= i <= T:
                        transp(i - 1, 0)
                    if 0 <= i < T:
                        scores(i, 1)
                    if i + 1 < T:
                        kproj(i + 1, 1)
                    if 1 <= i <= T:
                        tail(i - 1)
                        transp(i - 1, 1)
                    if i + 1 < T:
                        vproj(i + 1)
                    if 1 <= i <= T:
                        pv(i - 1)
                    if i >= 2:
                        gather(i - 2)
                    if i < 48 and i % 16 == 6:
                        qturn(i // 16 + 1)
                    if i < 48 and i % 16 == 7:
                        qproj(i // 16 + 1)

        area(139, 155)
        xTh = put("xTh", [128, 2, 512], F32R)
        xTl = put("xTl", [128, 2, 512], F32R)
        hp = put("hp", [128, 2, 512])
        xn = put("xn", [128, 4, C])
        area(155, 207.75)
        stg = put("stg", [128, 3, 1024])
        keep3 = top[0][0]
        XY = put("XY", [128, 2, 4, 512])
        L = put("L", [128, 4, 64])
        sm = put("sm", [128, 3, 4])
        Ab = put("Ab", [128, 2, 4, 128])
        AT = put("AT", [128, 4, 128])
        zs = put("zs", [128, 2, 512])
        yn = put("yn", [128, 4, C])
        gh = put("gh", [128, 2, 512])

        u_y = sem("u_y")
        u_x = sem("u_x")
        u_st = sem("u_st")
        u_mv = sem("u_mv")
        u_e = sem("u_e")
        u_rs = sem("u_rs")
        u_xn = sem("u_xn")
        u_t = sem("u_t")
        u_te = sem("u_te")
        u_tl = sem("u_tl")
        u_h = sem("u_h")
        u_he = sem("u_he")
        u_sc = sem("u_sc")
        u_l = sem("u_l")
        u_ch = sem("u_ch")
        u_sub = sem("u_sub")
        u_ex = sem("u_ex")
        u_az = sem("u_az")
        u_a = sem("u_a")
        u_at = sem("u_at")
        u_ate = sem("u_ate")
        u_xy = sem("u_xy")
        u_ye = sem("u_ye")
        u_cb = sem("u_cb")
        u_o = sem("u_o")
        u_z = sem("u_z")
        u_zt = sem("u_zt")
        u_b2 = sem("u_b2")
        u_x3 = sem("u_x3")
        f_st = sem("f_st")
        f_mv = sem("f_mv")
        f_rs = sem("f_rs")
        f_yn = sem("f_yn")
        f_yd = sem("f_yd")
        f_t = sem("f_t")
        f_hi = sem("f_hi")
        f_g = sem("f_g")
        f_gl = sem("f_gl")
        f_gs = sem("f_gs")
        f_ge = sem("f_ge")
        f_gt = sem("f_gt")
        w_d = [sem(f"w_d{i}") for i in range(3)]
        w_h = sem("w_h")
        w_l = sem("w_l")
        w_b = [sem(f"w_b{e}") for e in range(4)]
        w_o = sem("w_o")
        m01 = cst[:, C_M01:C_M01 + 1]
        m10 = cst[:, C_M01 + 1:C_M01 + 2]

        uses = [(("y", 0, h), u_x, h + 1) for h in range(2)]
        for k in range(7):
            if 0 <= k - 1 < 4:
                uses += [(("h", k - 1, m), u_he, 2 * (k - 1) + m + 1) for m in range(2)]
            if 0 <= k - 2 < 4:
                uses += [(("at", k - 2), u_ate, k - 1)]
            if 0 <= k - 1 < 4:
                uses += [(("s", k - 1), u_l, 2 * (k - 1) + 2)]
                uses += [(("xy", k - 1, j), u_ye, 4 * (k - 1) + j + 1) for j in range(4)]
            turned = [(("t3", k - 3, h), f_hi, 2 * (k - 3) + h + 1) for h in range(2) if 0 <= k - 3 < 4]
            summed = [(("ay", k - 2, h), u_z, 2 * (k - 2) + h + 1) for h in range(2) if 0 <= k - 2 < 4]
            uses += summed + turned if k == 5 else turned + summed
            if 0 <= k - 3 < 4:
                uses += [(("g", k - 3), f_gl, k - 2)]
            if k == 0:
                uses += [(("y", 1, h), u_x, h + 3) for h in range(2)]
            if k < 4:
                uses += [(("t", k, h), u_tl, 2 * k + h + 1) for h in range(2)]
            if 1 <= k < 3:
                uses += [(("y", k + 1, h), u_x, 2 * k + h + 3) for h in range(2)]
        place = {u[0]: n for n, u in enumerate(uses)}

        def bank(*key):
            return B[place[key] % 8]

        def w1(q, part):
            o = (q // 2) * 4096 + part * 2048 + (q % 2) * 1024
            return W1[:, o:o + 1024]

        def load_piece(sp, q):
            if q >= NW:
                sp.wait_ge(w_l, q - NW + 1)
            sp.dma_start(stg[:, q % NW, :], d["W1T"][q // 2, 128 * (q % 2):128 * (q % 2) + 128, :]
                         ).then_inc(w_d[q % NW], 16)

        def highs(a, q):
            a.wait_ge(w_d[q % NW], 16 * (q // NW + 1))
            if q >= 10:
                a.wait_ge(u_y, 8)
            if q >= 12:
                a.wait_ge(u_xy, 16)
                a.wait_ge(u_b2, 16)
            a.activation(w1(q, 0), stg[:, q % NW, :], ACT.Copy).then_inc(w_h, 1)

        def lows(g, q):
            g.wait_ge(w_h, q + 1)
            g.tensor_tensor(w1(q, 1), stg[:, q % NW, :], w1(q, 0).bitcast(F32), ALU.subtract).then_inc(w_l, 1)

        PIECES = [[0, 1, 2], [3, 4], [5, 6], [7, 8], [9], [10], [11, 12]]
        LATE = [13, 14, 15]
        NW = 3

        with nc.Block() as block:

            @block.sync
            def _(sp):
                sp.wait_ge(s_ote, T)
                for k in range(7):
                    for q in PIECES[k] if k < 4 else range(9, 13) if k == 4 else []:
                        load_piece(sp, q)
                    c = k - 2
                    if 0 <= c < 4:
                        sp.wait_ge(f_yn, 4 * c + 4)
                        sp.dma_start(y_d.rearrange("(n p) c -> p n c", p=128)[:, 4 * c:4 * c + 4, :], yn[:, :, :]
                                     ).then_inc(f_yd, 16)
                for q in LATE:
                    load_piece(sp, q)
                sp.wait_ge(f_yd, 64)

            @block.tensor
            def _(t):
                t.wait_ge(s_ote, T)
                t.wait_ge(s_w2, 48)
                t.wait_ge(s_wsd, 6)

                def take(*key):
                    n = place[key]
                    if n >= 8:
                        _, s, val = uses[n - 8]
                        t.wait_ge(s, val)
                    return B[n % 8]

                def attended(c):
                    for h in range(2):
                        b = take("y", c, h)
                        for jj in range(2):
                            j = 4 * c + 2 * h + jj
                            for m in range(2):
                                mm = t.matmul(b[:, C * jj:C * jj + C], OT[:, m, 128 * j:128 * j + 128], Wo[:, m, :],
                                              start=(m == 0), stop=(m == 1))
                        mm.then_inc(u_y, 1)

                def turned(k):
                    c = k - 3
                    if 0 <= c < 4:
                        for h in range(2):
                            b = take("t3", c, h)
                            for j in range(4):
                                t.wait_ge(f_yn, 4 * c + j + 1)
                                mm = t.transpose(b[:, 128 * j:128 * j + 128], yn[:, j, 128 * h:128 * h + 128], ident)
                            mm.then_inc(f_t, 1)

                def summed(k):
                    c = k - 2
                    if 0 <= c < 4:
                        t.wait_ge(u_ate, c + 1)
                        t.wait_ge(u_ye, 4 * c + 4)
                        for h in range(2):
                            b = take("ay", c, h)
                            for jj in range(2):
                                j = 2 * h + jj
                                mm = t.matmul(b[:, C * jj:C * jj + C], AT[:, j, :], XY[:, c % 2, j, C:2 * C],
                                              start=True, stop=True)
                            mm.then_inc(u_o, 1)

                attended(0)
                attended(1)
                for k in range(7):
                    c = k - 1
                    if 0 <= c < 4:
                        t.wait_ge(u_tl, 2 * c + 2)
                        for m in range(2):
                            b = take("h", c, m)
                            e = 0
                            for h in range(2):
                                s = slice(128 * m, 128 * m + 128)
                                for w, x in ((0, xTh), (1, xTh), (0, xTl)):
                                    mm = t.matmul(b[:, :], WaR[:, w, h, s], x[:, h, :], start=(e == 0), stop=(e == 5))
                                    e += 1
                            mm.then_inc(u_h, 1)
                    c = k - 2
                    if 0 <= c < 4:
                        b = take("at", c)
                        t.wait_ge(u_a, 2 * c + 2)
                        for j in range(4):
                            mm = t.transpose(b[:, 128 * j:128 * j + 128], Ab[:, c % 2, j, :], ident)
                        mm.then_inc(u_at, 1)
                    c = k - 1
                    if 0 <= c < 4:
                        b = take("s", c)
                        t.wait_ge(u_he, 2 * c + 2)
                        for h in range(2):
                            mm = t.matmul(b[:, :], bcol[:, 6 + h:7 + h].broadcast_to([128, 128]), hp[:, h, :],
                                          start=(h == 0), stop=(h == 1))
                        mm.then_inc(u_sc, 1)
                    c = k - 1
                    if 0 <= c < 4:
                        for j in range(4):
                            b = take("xy", c, j)
                            e = 0
                            for h in range(2):
                                s = slice(128 * j, 128 * j + 128)
                                for x, w in ((xTh, 0), (xTh, 1), (xTl, 0)):
                                    mm = t.matmul(b[:, :], x[:, h, s], WcR[:, w, h, :], start=(e == 0), stop=(e == 5))
                                    e += 1
                            mm.then_inc(u_xy, 1)
                    for step in ((summed, turned) if k == 5 else (turned, summed)):
                        step(k)
                    c = k - 3
                    if 0 <= c < 4:
                        b = take("g", c)
                        t.wait_ge(f_hi, 2 * c + 2)
                        for j in range(4):
                            for h in range(2):
                                mm = t.matmul(b[:, E * j:E * j + E], gh[:, h, 128 * j:128 * j + 128], WgT[:, h, :],
                                              start=(h == 0), stop=(h == 1))
                        mm.then_inc(f_g, 1)
                    if k < 4:
                        for h in range(2):
                            b = take("t", k, h)
                            for j in range(4):
                                t.wait_ge(u_xn, 4 * k + j + 1)
                                mm = t.transpose(b[:, 128 * j:128 * j + 128], xn[:, j, 128 * h:128 * h + 128], ident)
                            mm.then_inc(u_t, 1)
                    if 1 <= k < 3:
                        attended(k + 1)

            @block.vector
            def _(v):
                cnt = [0]

                def link(ins):
                    cnt[0] += 1
                    ins.then_inc(u_ch, 1)
                    v.wait_ge(u_ch, cnt[0])

                def bc(ap):
                    return ap.unsqueeze(2).broadcast_to([128, 4, E])

                def gate(c):
                    k = slice(4 * c, 4 * c + 4)

                    v.wait_ge(f_g, c + 1)
                    v.tensor_copy(gl[:, k, :], bank("g", c)[:, 0:4 * E].rearrange("p (n e) -> p n e", e=E)
                                  ).then_inc(f_gl, 1)
                    v.wait_ge(f_gl, c + 1)
                    link(v.tensor_reduce(gs[:, 0, k], gl[:, k, :], AX.X, ALU.max))
                    v.tensor_tensor(gl[:, k, :], gl[:, k, :], bc(gs[:, 0, k]), ALU.subtract).then_inc(f_gs, 1)

                def choose(c):
                    k = slice(4 * c, 4 * c + 4)
                    v.wait_ge(f_ge, c + 1)
                    link(v.tensor_reduce(gs[:, 1, k], gl[:, k, :], AX.X, ALU.add))
                    link(v.reciprocal(gs[:, 2, k], gs[:, 1, k]))
                    link(v.tensor_tensor(gl[:, k, :], gl[:, k, :], bc(gs[:, 2, k]), ALU.mult))
                    for j in range(4 * c, 4 * c + 4):
                        v.max(g8[:, j, :], gl[:, j, :]).then_inc(f_gt, 1)
                    for j in range(4 * c, 4 * c + 4):
                        v.wait_ge(f_gt, 8 * c + j - 4 * c + 1)
                        v.max_index(gi[:, j, :], g8[:, j, :], gl[:, j, :]).then_inc(f_gt, 1)
                    v.wait_ge(f_gt, 8 * c + 8)
                    link(v.tensor_copy(gs[:, 0:2, k], gi[:, k, 0:2].rearrange("p n a -> p a n")))
                    iot = cst[:, C_IOTA:C_IOTA + 8].unsqueeze(1).broadcast_to([128, 4, E])
                    v.tensor_tensor(oh[:, 0, k, :], iot, bc(gs[:, 0, k]), ALU.is_equal)
                    link(v.tensor_tensor(oh[:, 1, k, :], iot, bc(gs[:, 1, k]), ALU.is_equal))
                    link(v.tensor_tensor(Mk[:, k, :], oh[:, 0, k, :], oh[:, 1, k, :], ALU.add))
                    for j in range(4 * c, 4 * c + 4):
                        link(v.tensor_tensor(cum[:, j + 1, :], cum[:, j, :], Mk[:, j, :], ALU.add))
                    link(v.tensor_tensor(gs[:, 2, k], g8[:, k, 0], g8[:, k, 1], ALU.add))
                    link(v.tensor_scalar(gs[:, 2, k], gs[:, 2, k], 1e-9, None, ALU.add))
                    link(v.reciprocal(gs[:, 3, k], gs[:, 2, k]))
                    link(v.tensor_tensor(cmb[:, :, k], g8[:, k, 0:2].rearrange("p n a -> p a n"),
                                         gs[:, 3, k].unsqueeze(1).broadcast_to([128, 2, 4]), ALU.mult))

                v.wait_ge(s_ote, T)
                v.wait_ge(s_w2, 48)
                link(v.memset(cum[:, 0, :], 0.0))
                def first(k):
                    for h in range(2):
                        v.wait_ge(u_y, 2 * k + h + 1)
                        j = 4 * k + 2 * h
                        v.wait_ge(s_xbb, NTILE)
                        v.tensor_tensor(xb[:, j:j + 2, :], bank("y", k, h)[:, :].rearrange("p (a c) -> p a c", a=2),
                                        xb[:, j:j + 2, :], ALU.add).then_inc(u_x, 1)
                    for j in range(4):
                        v.wait_ge(u_x, 2 * k + j // 2 + 1)
                        v.bn_stats(st[:, 4 * k + j, :], xb[:, 4 * k + j, :]).then_inc(u_st, 1)
                    for j in range(4 * k, 4 * k + 4):
                        v.wait_ge(u_st, j + 1)
                        v.bn_aggr(mv[:, j, :], st[:, j, :]).then_inc(u_mv, 1)

                first(0)
                for k in range(7):
                    if k < 4:
                        v.wait_ge(u_rs, k + 1)
                        if k:
                            v.wait_ge(u_t, 2 * k)
                            v.wait_ge(u_b2, 4 * k)
                        for j in range(4):
                            n = 4 * k + j
                            v.tensor_scalar(xn[:, j, :], xb[:, n, :], mv[:, n, 0:1], rs[:, n:n + 1],
                                            ALU.subtract, ALU.mult).then_inc(u_xn, 1)
                    c = k - 1
                    if 0 <= c < 4:
                        v.wait_ge(u_sc, c + 1)
                        if c:
                            v.wait_ge(u_a, 2 * c)
                        for h in range(2):
                            r = slice(64 * h, 64 * h + 64)
                            v.tensor_tensor(L[r, :, :],
                                            bank("s", c)[r, :].rearrange("p (j h s) -> p j h s", h=2, s=64)[:, :, h, :],
                                            cst[r, C_MN:C_MN + 64].unsqueeze(1).broadcast_to([64, 4, 64]), ALU.add
                                            ).then_inc(u_l, 1)
                        v.wait_ge(u_l, 2 * c + 2)
                        link(v.tensor_reduce(sm[:, 0, :], L[:, :, :], AX.X, ALU.max))
                        v.tensor_tensor(L[:, :, :], L[:, :, :], sm[:, 0, :].unsqueeze(2).broadcast_to([128, 4, 64]),
                                        ALU.subtract).then_inc(u_sub, 1)
                    if 0 <= c < 4:
                        v.wait_ge(u_ex, c + 1)
                        link(v.tensor_reduce(sm[:, 1, :], L[:, :, :], AX.X, ALU.add))
                        link(v.reciprocal(sm[:, 2, :], sm[:, 1, :]))
                        v.wait_ge(u_az, 1)
                        for h in range(2):
                            r = slice(64 * h, 64 * h + 64)
                            v.tensor_tensor(Ab[r, c % 2, :, 64 * h:64 * h + 64], L[r, :, :],
                                            sm[r, 2, :].unsqueeze(2).broadcast_to([64, 4, 64]), ALU.mult
                                            ).then_inc(u_a, 1)
                    c = k - 2
                    if 0 <= c < 4:
                        for h in range(2):
                            v.wait_ge(u_o, 2 * c + h + 1)
                            v.wait_ge(u_cb, 4 * c + 2 * h + 2)
                            if c:
                                v.wait_ge(u_x3, 2 * c + h - 1)
                            v.tensor_tensor(zs[:, h, :].rearrange("p (a c) -> p a c", a=2),
                                            bank("ay", c, h)[:, :].rearrange("p (a c) -> p a c", a=2),
                                            XY[:, c % 2, 2 * h:2 * h + 2, 0:C], ALU.add).then_inc(u_z, 1)
                    c = k - 2
                    if 0 <= c < 4:
                        for h in range(2):
                            v.wait_ge(u_zt, 2 * c + h + 1)
                            v.wait_ge(u_b2, 4 * c + 4)
                            j = 4 * c + 2 * h
                            v.scalar_tensor_tensor(out=xb[:, j:j + 2, :],
                                                   in0=zs[:, h, :].rearrange("p (a c) -> p a c", a=2), scalar=m01,
                                                   in1=xb[:, j:j + 2, :], op0=ALU.mult, op1=ALU.add).then_inc(u_x3, 1)
                        for j in range(4 * c, 4 * c + 4):
                            v.wait_ge(u_x3, j // 2 + 1)
                            v.bn_stats(st[:, j, :], xb[:, j, :]).then_inc(f_st, 1)
                        for j in range(4 * c, 4 * c + 4):
                            v.wait_ge(f_st, j + 1)
                            v.bn_aggr(mv[:, j, :], st[:, j, :]).then_inc(f_mv, 1)
                    if k in (3, 4, 6):
                        gate(k - 3)
                    if k < 4:
                        for h in range(2):
                            v.wait_ge(u_te, 2 * k + h + 1)
                            v.tensor_tensor(xTl[:, h, :], bank("t", k, h)[:, :], xTh[:, h, :].bitcast(F32), ALU.subtract
                                            ).then_inc(u_tl, 1)
                    if k < 4:
                        for j in range(4):
                            n = 4 * k + j
                            v.wait_ge(u_xn, n + 1)
                            v.scalar_tensor_tensor(out=xb[:, n, :], in0=xn[:, j, :], scalar=m10, in1=xb[:, n, :],
                                                   op0=ALU.mult, op1=ALU.add).then_inc(u_b2, 1)
                    if k + 1 < 4:
                        first(k + 1)
                    if 0 <= c < 4:
                        v.wait_ge(f_rs, c + 1)
                        if c:
                            v.wait_ge(f_t, 2 * c)
                            v.wait_ge(f_yd, 16 * c)
                        for j in range(4):
                            n = 4 * c + j
                            v.tensor_scalar(yn[:, j, :], xb[:, n, :], mv[:, n, 0:1], rs[:, n:n + 1],
                                            ALU.subtract, ALU.mult).then_inc(f_yn, 1)
                    if k == 5:
                        gate(2)
                        choose(1)
                    if k in (3, 5, 6):
                        choose(k - 3)

            @block.gpsimd
            def _(g):
                g.wait_ge(s_ote, T)
                g.memset(Ab[:, :, :, :], 0.0).then_inc(u_az, 1)
                cnt = [0]

                def rstd(c, ready, done):
                    k = slice(4 * c, 4 * c + 4)
                    g.wait_ge(ready, 4 * c + 4)
                    g.tensor_tensor(rs[:, k], mv[:, k, 1], epw[:, 0, k], ALU.add).then_inc(u_e, 1)
                    cnt[0] += 1
                    g.wait_ge(u_e, cnt[0])
                    g.tensor_tensor(rs[:, k], rs[:, k], epw[:, 1, k], ALU.pow).then_inc(done, 1)

                rstd(0, u_mv, u_rs)
                for k in range(7):
                    if 0 <= k - 1 < 4:
                        c = k - 1
                        for j in range(4):
                            g.wait_ge(u_ye, 4 * c + j + 1)
                            g.tensor_tensor(XY[:, c % 2, j, 0:C], XY[:, c % 2, j, 0:C], bcc[:, 1, :], ALU.add
                                            ).then_inc(u_cb, 1)
                    if k < 5:
                        lows(g, PIECES[k][0])
                    if 0 <= k - 2 < 4:
                        rstd(k - 2, f_mv, f_rs)
                    if k + 1 < 4:
                        rstd(k + 1, u_mv, u_rs)
                    for q in PIECES[k][1:] if k < 5 else PIECES[k]:
                        lows(g, q)

            @block.scalar
            def _(a):
                a.wait_ge(s_ote, T)

                def turned(k):
                    c = k - 3
                    if 0 <= c < 4:
                        for h in range(2):
                            a.wait_ge(f_t, 2 * c + h + 1)
                            if c:
                                a.wait_ge(f_g, c)
                            a.activation(gh[:, h, :], bank("t3", c, h)[:, :], ACT.Copy).then_inc(f_hi, 1)

                def squashed(k):
                    c = k - 2
                    if 0 <= c < 4:
                        for h in range(2):
                            a.wait_ge(u_z, 2 * c + h + 1)
                            a.activation(zs[:, h, :], zs[:, h, :], ACT.Tanh).then_inc(u_zt, 1)

                for k in range(7):
                    c = k - 1
                    if 0 <= c < 4:
                        for m in range(2):
                            a.wait_ge(u_h, 2 * c + m + 1)
                            if c:
                                a.wait_ge(u_sc, c)
                            a.activation(hp[:, m, :], bank("h", c, m)[:, :], ACT.Tanh).then_inc(u_he, 1)
                    c = k - 2
                    if 0 <= c < 4:
                        a.wait_ge(u_at, c + 1)
                        if c:
                            a.wait_ge(u_o, 2 * c)
                        a.activation(AT[:, :, :].rearrange("p j n -> p (j n)"), bank("at", c)[:, :], ACT.Copy
                                     ).then_inc(u_ate, 1)
                    c = k - 1
                    if 0 <= c < 4:
                        for j in range(4):
                            a.wait_ge(u_xy, 4 * c + j + 1)
                            if c >= 2:
                                a.wait_ge(u_z, 2 * (c - 1))
                            a.activation(XY[:, c % 2, j, :], bank("xy", c, j)[:, :], ACT.Copy).then_inc(u_ye, 1)
                            if j == 0:
                                a.wait_ge(u_sub, c + 1)
                                a.activation(L[:, :, :], L[:, :, :], ACT.Exp).then_inc(u_ex, 1)
                    if k != 5:
                        turned(k)
                        if k < 5:
                            highs(a, PIECES[k][0])
                    squashed(k)
                    if k == 5:
                        highs(a, 10)
                        turned(k)
                    if k == 6:
                        highs(a, 11)
                        highs(a, 12)
                    if k < 4:
                        for h in range(2):
                            a.wait_ge(u_t, 2 * k + h + 1)
                            if k:
                                a.wait_ge(u_xy, 4 * k)
                            a.activation(xTh[:, h, :], bank("t", k, h)[:, :], ACT.Copy).then_inc(u_te, 1)
                    for c in {3: [0], 5: [1, 2], 6: [3]}.get(k, []):
                        a.wait_ge(f_gs, c + 1)
                        a.activation(gl[:, 4 * c:4 * c + 4, :], gl[:, 4 * c:4 * c + 4, :], ACT.Exp).then_inc(f_ge, 1)
                    for q in PIECES[k][1:] if k < 5 else []:
                        highs(a, q)

        area(155, 167)
        Xg = put("Xg", [128, 3, C])
        xh = put("xh", [128, 2, 2, 128], F32R)
        xl = put("xl", [128, 2, 2, 128], F32R)
        WoT = put("WoT", [128, 4, C])
        area(167, 207.75)
        bb = put("bb", [128, E, 1024])
        keep4 = top[0][0]
        th = put("th", [128, E, 16])
        ps = put("ps", [128, NTILE, E])
        te = put("te", [128, 40, E])
        A16 = put("A16", [128, 4, 128], F16)
        B16 = put("B16", [128, 32, 40], F16)
        top[0][0] = keep4
        sg = put("sg", [128, 2, 512])
        gg = put("gg", [128, 2, 512])
        area(22.375, 23.875)
        rq = put("rq", [128, 2, 2, NTILE], I32)
        rf = put("rf", [128, 2, 2, NTILE])
        ew = put("ew", [1, 2, 40], I32)
        i16 = put("i16", [128, 128], F16)
        area(26.3125, 27)
        ti = put("ti", [128, E])
        tj = put("tj", [128, 3, E])
        pf = put("pf", [128, 2, NTILE])
        pi = put("pi", [128, 2, NTILE], I32)
        tf = put("tf", [128, 40])
        inv = put("inv", [128, 40], I32)
        area(27, 60)
        cg = put("cg", [128, 4, 2, 512])
        zc = put("zc", [128, 2, 512])
        zT = put("zT", [128, 2, 512])
        fo = put("fo", [128, 4, C])

        r_b = sem("r_b")
        r_p = sem("r_p")
        r_c = sem("r_c")
        r_f = sem("r_f")
        r_A = sem("r_A")
        r_B0 = sem("r_B0")
        r_B1 = sem("r_B1")
        r_i = sem("r_i")
        r_iv = sem("r_iv")
        r_ew = sem("r_ew")
        r_b3 = sem("r_b3")
        e_x = [sem(f"e_x{i}") for i in range(3)]
        e_t = sem("e_t")
        e_hi = sem("e_hi")
        e_lo = sem("e_lo")
        e_h = sem("e_h")
        e_ad = sem("e_ad")
        e_sg = sem("e_sg")
        e_g = sem("e_g")
        e_gd = [sem("e_gd0"), sem("e_gd1")]
        c_g = [sem(f"c_g{i}") for i in range(4)]
        c_z = sem("c_z")
        c_m = sem("c_m")
        c_t = sem("c_t")
        c_te = sem("c_te")
        c_o = sem("c_o")
        c_f = sem("c_f")
        c_out = [sem(f"c_out{i}") for i in range(4)]

        def choice_rows(k):
            return B16[:, NTILE * k:NTILE * k + NTILE, :]

        def tb(i):
            return B[2 + i % 2]

        def ab(i):
            return [(B[4], B[5]), (B[6], B[7]), (B[0], B[1])][i % 3]

        with nc.Block() as block:

            @block.sync
            def _(sp):
                for e in range(E):
                    sp.dma_start(bb[:, e, :], bcast(d["b1"][e], 128)).then_inc(w_b[e // 2], 16)
                sp.wait_ge(w_l, 16)
                sp.dma_start(WoT[:, :, :], d["fWoT"].rearrange("(k p) n -> p k n", p=128)).then_inc(w_o, 16)
                for i in range(NS):
                    sp.wait_ge(e_g, i + 1)
                    sp.dma_start(g_d[128 * i:128 * i + 128, :], gg[:, i % 2, :]).then_inc(e_gd[i % 2], 16)
                od = out.rearrange("t (n b) c -> n b t c", b=2)
                for j in range(NTILE):
                    sp.wait_ge(c_f, j + 1)
                    sp.dma_start(od[j], fo[:, j % 4, :]).then_inc(c_out[j % 4], 16)
                for s in c_out:
                    sp.wait_ge(s, 64)

            @block.gpsimd
            def _(g):
                for q in LATE[:2]:
                    lows(g, q)
                g.wait_ge(r_f, 1)
                for k in range(2):
                    g.wait_ge(r_B0, k + 1)
                    g.tensor_tensor(choice_rows(k), choice_rows(k),
                                    cst[:, C_TOK:C_TOK + NTILE].unsqueeze(2).broadcast_to([128, NTILE, 40]), ALU.mult
                                    ).then_inc(r_B1, 1)
                lows(g, LATE[2])
                g.wait_ge(w_l, 16)
                g.wait_ge(r_iv, 1)
                g.wait_ge(f_yd, 64)
                for i in range(NS):
                    if i >= 3:
                        g.wait_ge(e_t, i - 2)
                    g.indirect_dma_start(out=Xg[:, i % 3, :], out_offset=None, in_=y_d,
                                         in_offset=bass.IndirectOffsetOnAxis(ap=inv[:, i:i + 1], axis=0)
                                         ).then_inc(e_x[i % 3], 16)
                g.wait_ge(e_gd[0], 16 * 20)
                g.wait_ge(e_gd[1], 16 * 19)
                g.wait_ge(e_h, 2 * NS)
                for j in range(NTILE):
                    if j >= 4:
                        g.wait_ge(c_z, j - 3)
                    for k in range(2):
                        g.indirect_dma_start(out=cg[:, j % 4, k, :], out_offset=None, in_=g_d,
                                             in_offset=bass.IndirectOffsetOnAxis(ap=pi[:, k, j:j + 1], axis=0)
                                             ).then_inc(c_g[j % 4], 16)

            def glu(v, i):
                w = v.value_load(ew[0:1, 1, i:i + 1], min_val=0, max_val=(E - 1) * 1024)
                bf = bb[:, :, :].rearrange("p e n -> p (e n)")
                if i < E and i % 2 == 0:
                    v.wait_ge(w_b[i // 2], 32)
                v.wait_ge(e_h, 2 * i + 1)
                if i >= 2:
                    v.wait_ge(e_g, i - 1)
                v.tensor_tensor(sg[:, i % 2, :], ab(i)[1][:, :], bf[:, bass.DynSlice(w + 512, 512)], ALU.add
                                ).then_inc(e_ad, 1)
                v.wait_ge(e_h, 2 * i + 2)
                if i >= 2:
                    v.wait_ge(e_gd[i % 2], 16 * (i // 2))
                v.tensor_tensor(gg[:, i % 2, :], ab(i)[0][:, :], bf[:, bass.DynSlice(w, 512)], ALU.add
                                ).then_inc(e_ad, 1)
                v.wait_ge(e_ad, 2 * i + 2)
                v.wait_ge(e_sg, i + 1)
                v.tensor_tensor(gg[:, i % 2, :], gg[:, i % 2, :], sg[:, i % 2, :], ALU.mult).then_inc(e_g, 1)

            def final(v, j):
                v.wait_ge(c_o, j + 1)
                if j >= 4:
                    v.wait_ge(c_out[j % 4], 16 * (j // 4))
                v.tensor_tensor(fo[:, j % 4, :], B[4 + j % 4][:, 0:C], xb[:, j, :], ALU.add).then_inc(c_f, 1)

            @block.vector
            def _(v):
                cnt = [0]

                def link(ins):
                    cnt[0] += 1
                    ins.then_inc(r_c, 1)
                    v.wait_ge(r_c, cnt[0])

                v.wait_ge(u_ch, 1)
                v.tensor_copy(i16[:, :], cst[:, C_I128:C_I128 + 128]).then_inc(r_b, 1)
                v.wait_ge(r_p, 1)
                link(v.tensor_copy(ti[:, :], B[0][:, 128:136]))
                link(v.tensor_tensor(th[:, :, :], ti[:, :].unsqueeze(2).broadcast_to([128, E, 16]),
                                     cst[:, C_TH:C_TH + 16].unsqueeze(1).broadcast_to([128, E, 16]), ALU.is_gt))
                link(v.tensor_reduce(ti[:, :], th[:, :, :], AX.X, ALU.add))
                link(v.tensor_copy(tj[:, 0, :], ti[:, :]))
                a, b = 0, 1
                for s in (1, 2, 4):
                    v.tensor_copy(tj[:, b, 0:s], tj[:, a, 0:s]).then_inc(r_c, 1)
                    cnt[0] += 1
                    link(v.tensor_tensor(tj[:, b, s:E], tj[:, a, s:E], tj[:, a, 0:E - s], ALU.add))
                    a, b = b, a
                incl = tj[:, a, :]
                link(v.tensor_tensor(tj[:, 2, :], incl, ti[:, :], ALU.subtract))
                link(v.tensor_scalar(tj[:, 2, :], tj[:, 2, :], 128.0, None, ALU.mult))
                link(v.tensor_tensor(ps[:, :, :], B[0][:, 0:128].rearrange("p (n e) -> p n e", e=E),
                                     tj[:, 2, :].unsqueeze(1).broadcast_to([128, NTILE, E]), ALU.add))
                for k in range(2):
                    link(v.tensor_tensor(oh[:, k, :, :], oh[:, k, :, :], ps[:, :, :], ALU.mult))
                    link(v.tensor_reduce(pf[:, k, :], oh[:, k, :, :], AX.X, ALU.add))
                link(v.tensor_copy(pi[:, :, :], pf[:, :, :]))
                v.tensor_scalar(rq[:, 0, :, :], pi[:, :, :], 127, None, ALU.bitwise_and).then_inc(r_c, 1)
                cnt[0] += 1
                link(v.tensor_scalar(rq[:, 1, :, :], pi[:, :, :], 7, None, ALU.logical_shift_right))
                v.tensor_copy(rf[:, :, :, :], rq[:, :, :, :]).then_inc(r_f, 1)
                v.wait_ge(r_f, 1)
                for k in range(2):
                    v.tensor_tensor(choice_rows(k), i16[:, 0:40].unsqueeze(1).broadcast_to([128, NTILE, 40]),
                                    rf[:, 1, k, :].unsqueeze(2).broadcast_to([128, NTILE, 40]), ALU.is_equal
                                    ).then_inc(r_B0, 1)
                for n in range(32):
                    k, j = n // NTILE, n % NTILE
                    if n >= 4:
                        v.wait_ge(r_i, n - 3)
                    v.tensor_scalar(A16[:, n % 4, :], i16[:, :], rf[:, 0, k, j:j + 1], None, ALU.is_equal
                                    ).then_inc(r_A, 1)
                link(v.tensor_tensor(te[:, :, :], cst[:, C_I128:C_I128 + 40].unsqueeze(2).broadcast_to([128, 40, E]),
                                     incl.unsqueeze(1).broadcast_to([128, 40, E]), ALU.is_ge))
                link(v.tensor_reduce(tf[:, :], te[:, :, :], AX.X, ALU.add))
                link(v.tensor_scalar(tf[:, :], tf[:, :], float(E - 1), None, ALU.min))
                v.tensor_scalar(ew[:, 0, :], tf[0:1, :], 4096.0, None, ALU.mult).then_inc(r_ew, 1)
                v.tensor_scalar(ew[:, 1, :], tf[0:1, :], 1024.0, None, ALU.mult).then_inc(r_ew, 1)
                v.wait_ge(r_i, 32)
                v.tensor_copy(inv[:, :], B[1][:, 0:40]).then_inc(r_iv, 1)
                link(v.tensor_tensor(gs[:, 0, :], cmb[:, 0, :], cmb[:, 1, :], ALU.add))

                for i in range(NS):
                    v.wait_ge(e_hi, i + 1)
                    v.tensor_tensor(xl[:, i % 2, :, :].rearrange("p k n -> p (k n)"), tb(i)[:, 0:C],
                                    xh[:, i % 2, :, :].rearrange("p k n -> p (k n)").bitcast(F32), ALU.subtract
                                    ).then_inc(e_lo, 1)
                    if i:
                        glu(v, i - 1)
                    if i >= 2 and i - 2 < NTILE:
                        n = i - 2
                        v.scalar_tensor_tensor(out=xb[:, n, :], in0=bcc[:, 2, :], scalar=gs[:, 0, n:n + 1],
                                               in1=xb[:, n, :], op0=ALU.mult, op1=ALU.add).then_inc(r_b3, 1)
                glu(v, NS - 1)
                v.wait_ge(r_b3, NTILE)
                for j in range(NTILE):
                    v.wait_ge(c_g[j % 4], 32 * (j // 4 + 1))
                    if j >= 2:
                        v.wait_ge(c_t, j - 1)
                    v.tensor_scalar(zc[:, j % 2, :], cg[:, j % 4, 0, :], cmb[:, 0, j:j + 1], None, ALU.mult
                                    ).then_inc(c_m, 1)
                    v.wait_ge(c_m, j + 1)
                    v.scalar_tensor_tensor(out=zc[:, j % 2, :], in0=cg[:, j % 4, 1, :], scalar=cmb[:, 1, j:j + 1],
                                           in1=zc[:, j % 2, :], op0=ALU.mult, op1=ALU.add).then_inc(c_z, 1)
                    if j >= 2:
                        final(v, j - 2)
                final(v, NTILE - 2)
                final(v, NTILE - 1)

            @block.scalar
            def _(a):
                def high(i):
                    a.wait_ge(e_t, i + 1)
                    if i >= 2:
                        a.wait_ge(e_h, 2 * (i - 1))
                    a.activation(xh[:, i % 2, :, :].rearrange("p k n -> p (k n)"), tb(i)[:, 0:C], ACT.Copy
                                 ).then_inc(e_hi, 1)

                for q in LATE:
                    highs(a, q)
                high(0)
                for i in range(NS):
                    if i + 1 < NS:
                        high(i + 1)
                    a.wait_ge(e_ad, 2 * i + 1)
                    a.activation(sg[:, i % 2, :], sg[:, i % 2, :], ACT.Sigmoid).then_inc(e_sg, 1)
                for j in range(NTILE):
                    a.wait_ge(c_t, j + 1)
                    if j >= 2:
                        a.wait_ge(c_o, j - 1)
                    a.activation(zT[:, j % 2, :], B[j % 2][:, :], ACT.Copy).then_inc(c_te, 1)

            @block.tensor
            def _(t):
                t.wait_ge(u_ch, 73)
                M = Mk[:, :, :].rearrange("p n e -> p (n e)")
                t.matmul(B[0][:, 0:128], cst[:, C_U:C_U + 128], M, start=True, stop=False, skip_group_check=True)
                t.matmul(B[0][:, 0:128], cst[:, C_ONE:C_ONE + 128], cum[:, 0:NTILE, :].rearrange("p n e -> p (n e)"),
                         start=False, stop=True, skip_group_check=True)
                t.matmul(B[0][:, 128:136], cst[:, C_ONE:C_ONE + 128], cum[:, NTILE, :], start=True, stop=True,
                         skip_group_check=True).then_inc(r_p, 1)
                for n in range(32):
                    t.wait_ge(r_A, n + 1)
                    t.wait_ge(r_B1, n // NTILE + 1)
                    t.matmul(B[1][:, 0:40], A16[:, n % 4, :], B16[:, n, :], start=(n == 0), stop=(n == 31)
                             ).then_inc(r_i, 1)
                t.wait_ge(r_ew, 2)
                t.wait_ge(w_l, 16)
                t.wait_ge(r_iv, 1)

                def turn(i):
                    t.wait_ge(e_x[i % 3], 16 * (i // 3 + 1))
                    if i >= 2:
                        t.wait_ge(e_lo, i - 1)
                    for k in range(2):
                        mm = t.transpose(tb(i)[:, 128 * k:128 * k + 128], Xg[:, i % 3, 128 * k:128 * k + 128], ident)
                    mm.then_inc(e_t, 1)

                turn(0)
                for i in range(NS):
                    if i + 1 < NS:
                        turn(i + 1)
                    w = t.value_load(ew[0:1, 0, i:i + 1], min_val=0, max_val=(E - 1) * 4096)
                    t.wait_ge(e_lo, i + 1)
                    if i >= 3:
                        t.wait_ge(e_ad, 2 * (i - 2))
                    for h in (1, 0):
                        o = ab(i)[h][:, :]
                        for k in range(2):
                            for x, part in ((xh, 0), (xh, 1), (xl, 0)):
                                mm = t.matmul(o, x[:, i % 2, k, :],
                                              W1[:, bass.DynSlice(w + (part * 2048 + k * 1024 + 512 * h), 512)],
                                              start=(k == 0 and part == 0 and x is xh),
                                              stop=(k == 1 and part == 0 and x is xl))
                        mm.then_inc(e_h, 1)

                def back(j):
                    t.wait_ge(c_z, j + 1)
                    if j >= 2:
                        t.wait_ge(c_te, j - 1)
                    for m in range(4):
                        mm = t.transpose(B[j % 2][:, 128 * m:128 * m + 128], zc[:, j % 2, 128 * m:128 * m + 128], ident)
                    mm.then_inc(c_t, 1)

                t.wait_ge(w_o, 16)
                t.wait_ge(e_g, NS)
                back(0)
                for j in range(NTILE):
                    if j + 1 < NTILE:
                        back(j + 1)
                    t.wait_ge(c_te, j + 1)
                    if j >= 4:
                        t.wait_ge(c_f, j - 3)
                    for m in range(4):
                        mm = t.matmul(B[4 + j % 4][:, 0:C], zT[:, j % 2, 128 * m:128 * m + 128], WoT[:, m, :],
                                      start=(m == 0), stop=(m == 3))
                    mm.then_inc(c_o, 1)




def bcast(ap, n):
    return bass.AP(tensor=ap.tensor, offset=ap.offset, ap=[[0, n]] + list(ap.ap))


def kernel(**inputs):
    import concourse.bacc as bacc
    from concourse.bass_utils import run_bass_kernel_spmd

    nc = bacc.Bacc("TRN2", target_bir_lowering=False, num_devices=1)
    a = {k: np.asarray(v) for k, v in inputs.items()}
    ctx = a["ctx_768"]
    col = lambda v: v.reshape(-1, 128).T
    arrays = {
        "x": a["x"],
        "cst": constants(),
        "Wq": a["L0_xattn_Wq"],
        "Wk": a["L0_xattn_Wk"],
        "Wv": a["L0_xattn_Wv"],
        "xWo": a["L0_xattn_Wo"],
        "ctxT": np.concatenate([ctx, ctx[:, -1:]], axis=1).transpose(0, 2, 1),
        "c256": ctx[:, NK - 1, :].T,
        "bcol": np.concatenate([col(a["L0_xattn_bq"]), col(a["L0_xattn_bk"]), col(a["L0_xattn_bv"]),
                                col(a["L0_attn_proj"])], axis=1),
        "brow": np.stack([a["L0_xattn_bo"], a["L0_attn_concat_b"], a["L0_ffn_bo"]]),
        "aW": a["L0_attn_W"],
        "cwT": a["L0_attn_concat_w"].T.reshape(2, 256, 256).transpose(1, 0, 2),
        "WgT": a["L0_ffn_Wg"].T,
        "W1T": a["L0_ffn_W1"].transpose(0, 2, 1),
        "b1": a["L0_ffn_b1"],
        "fWoT": a["L0_ffn_Wo"].T,
    }
    arrays = {k: np.ascontiguousarray(v) for k, v in arrays.items()}
    d = {k: nc.dram_tensor("in_" + k, v.shape, F32, kind="ExternalInput").ap() for k, v in arrays.items()}
    out = nc.dram_tensor("out", [T, NQ, C], F32, kind="ExternalOutput").ap()
    vx_d = nc.dram_tensor("vx_d", [2, 4, T, 260], F32, kind="Internal").ap()
    y_d = nc.dram_tensor("y_d", [NT, C], F32, kind="Internal").ap()
    g_d = nc.dram_tensor("g_d", [NS * 128, HF], F32, kind="Internal").ap()
    build(nc, d, out, vx_d, y_d, g_d)
    r = run_bass_kernel_spmd(nc, [{"in_" + k: v for k, v in arrays.items()}], core_ids=[0])
    return r.results[0]["out"]
```
